# Optimizing a Trainium2 kernel written in Bass

```python
import numpy as np
import jax
import jax.numpy as jnp

def _softmax(x, axis=-1):
    return jax.nn.softmax(x, axis=axis)

def _gelu(x):
    return jax.nn.gelu(x, approximate=True)

def _silu(x):
    return jax.nn.silu(x)

def _sigmoid(x):
    return jax.nn.sigmoid(x)

def _layernorm(x, axis=-1, eps=1e-05):
    m = jnp.mean(x, axis=axis, keepdims=True)
    v = jnp.var(x, axis=axis, keepdims=True)
    return (x - m) / jnp.sqrt(v + eps)

def _scatter_add(tgt, idx, src, axis=0):
    return tgt.at[idx].add(src)

def _segment_sum(src, seg, n):
    return jax.ops.segment_sum(src, seg, n)
kernel_name = 'mk_cond_resid_d4_seqx_r4_46eccc'

def setup_inputs(seed: int=0):
    np.random.seed(seed)
    _w = jnp.asarray

    def _rec_inputs():
        import jax
        import jax.numpy as jnp
        _rk = jax.random.key(seed)
        x = -0.000125 + 0.9999 * jax.random.normal(jax.random.fold_in(_rk, 1), (128, 64, 1024), jnp.float32)
        _lenS = 64 - jax.random.randint(jax.random.fold_in(_rk, 7), (128,), 0, max(1, 64 // 4) + 1, jnp.int32)
        _lenS2 = 64 - jax.random.randint(jax.random.fold_in(_rk, 8), (128,), 0, max(1, 64 // 4) + 1, jnp.int32)
        itok_B_0_7 = jax.random.randint(jax.random.fold_in(_rk, 11), (128,), 0, 8, jnp.int32)
        itok_B_0_23 = jax.random.randint(jax.random.fold_in(_rk, 12), (128,), 0, 24, jnp.int32)
        itok_B_3_7 = jax.random.randint(jax.random.fold_in(_rk, 13), (128,), 3, 8, jnp.int32)
        itok_B_78_3631 = jax.random.randint(jax.random.fold_in(_rk, 14), (128,), 78, 908, jnp.int32)
        return (x, itok_B_0_7, itok_B_0_23, itok_B_3_7, itok_B_78_3631)
    x, itok_B_0_7, itok_B_0_23, itok_B_3_7, itok_B_78_3631 = _rec_inputs()

    def _L0_cond_setup():
        import jax, jax.numpy as jnp
        import numpy as np
        TOP_K = 2
        LANG_BIAS = 5.0
        SCALING = 32.0 / 16.0
        LANGUAGE_PAD_ID = -1
        key = jax.random.key(seed)
        ks = jax.random.split(key, 6)
        B, T, D, O, E, R = (4, 512, 1024, 1024, 8, 16)
        x = jax.random.normal(ks[0], (B, T, D), dtype=jnp.float32)
        language_ids = jax.random.randint(ks[1], (B,), 0, E).astype(jnp.int64)
        W = jax.random.normal(ks[2], (O, D), dtype=jnp.float32) * (1.0 / np.sqrt(D))
        Wr = jax.random.normal(ks[3], (E, D), dtype=jnp.float32) * (1.0 / np.sqrt(D))
        A = jax.random.normal(ks[4], (E, R, D), dtype=jnp.float32) * (1.0 / np.sqrt(D))
        Bm = jax.random.normal(ks[5], (O, R), dtype=jnp.float32) * 0.0
        Bm = jnp.broadcast_to(Bm, (E, O, R)) + jax.random.normal(ks[5], (E, O, R), dtype=jnp.float32) * 0.02
        return {'x': x, 'language_ids': language_ids, 'W': W, 'Wr': Wr, 'A': A, 'B': Bm}
    _L0_cond_all = _L0_cond_setup()
    _L0_cond_in = {k: v for k, v in _L0_cond_all.items() if k in ('W', 'Wr', 'A', 'B')}
    del _L0_cond_all

    def _L1_cond_setup():
        import jax, jax.numpy as jnp
        import numpy as np
        R = 16
        ALPHA = 32
        SCALING = ALPHA / R
        SLOTS = 32
        IN_F = 1024
        OUT_F = 1024
        B, T = (8, 256)
        key = jax.random.key(seed)
        k1, k2, k3, k4, k5, k6 = jax.random.split(key, 6)
        x = jax.random.normal(k1, (B, T, IN_F), dtype=jnp.float32)
        adapter_mapping = jax.random.randint(k2, (B,), 0, SLOTS, dtype=jnp.int32)
        W = jax.random.normal(k3, (OUT_F, IN_F), dtype=jnp.float32) * 0.02
        b = jax.random.normal(k4, (OUT_F,), dtype=jnp.float32) * 0.02
        lora_As = jax.random.normal(k5, (SLOTS, IN_F, R), dtype=jnp.float32) * 0.02
        lora_Bs = jax.random.normal(k6, (SLOTS, R, OUT_F), dtype=jnp.float32) * 0.02
        return {'x': x, 'adapter_mapping': adapter_mapping, 'W': W, 'b': b, 'lora_As': lora_As, 'lora_Bs': lora_Bs}
    _L1_cond_all = _L1_cond_setup()
    _L1_cond_in = {k: v for k, v in _L1_cond_all.items() if k in ('W', 'b', 'lora_As', 'lora_Bs')}
    del _L1_cond_all

    def _L2_cond_setup():
        import jax, jax.numpy as jnp
        import numpy as np
        MAX_LORAS, OUT, IN = (8, 1024, 1024)
        B, S = (4, 512)
        key = jax.random.key(seed)
        k1, k2, k3 = jax.random.split(key, 3)
        x = jax.random.normal(k1, (B, S, IN), dtype=jnp.float32)
        weight = jax.random.normal(k2, (MAX_LORAS, OUT, IN), dtype=jnp.float32) * 0.02
        adapter_ids = jax.random.randint(k3, (B,), 0, MAX_LORAS, dtype=jnp.int32)
        return {'x': x, 'weight': weight, 'adapter_ids': adapter_ids}
    _L2_cond_all = _L2_cond_setup()
    _L2_cond_in = {k: v for k, v in _L2_cond_all.items() if k in ('weight',)}
    del _L2_cond_all

    def _L3_cond_setup():
        import math
        import jax, jax.numpy as jnp
        import numpy as np
        B, H, N, L = (16, 64, 64, 1024)
        DT_MIN, DT_MAX = (0.001, 0.1)

        def _get_kernel(log_dt, C, log_A_real, A_imag, length):
            dt = jnp.exp(log_dt)
            Cc = C[..., 0] + 1j * C[..., 1]
            A = -jnp.exp(log_A_real) + 1j * A_imag
            dtA = A * dt[:, None]
            Ct = Cc * (jnp.exp(dtA) - 1.0) / A
            P = dtA[:, :, None] * jnp.arange(length, dtype=jnp.float32)
            K = 2.0 * jnp.einsum('hn,hnl->hl', Ct, jnp.exp(P)).real
            return K
        key = jax.random.key(seed)
        ks = jax.random.split(key, 5)
        u = jax.random.normal(ks[0], (B, H, L), dtype=jnp.float32)
        log_dt = jax.random.uniform(ks[1], (H,), dtype=jnp.float32) * (math.log(DT_MAX) - math.log(DT_MIN)) + math.log(DT_MIN)
        C = jax.random.normal(ks[2], (H, N, 2), dtype=jnp.float32)
        log_A_real = jnp.log(0.5 * jnp.ones((H, N), dtype=jnp.float32))
        A_imag = math.pi * jnp.broadcast_to(jnp.arange(N, dtype=jnp.float32), (H, N))
        D = jax.random.normal(ks[3], (H,), dtype=jnp.float32)
        length = jax.random.randint(ks[4], (B,), 1, L + 1, dtype=jnp.int32)
        return {'u': u, 'log_dt': log_dt, 'C': C, 'log_A_real': log_A_real, 'A_imag': A_imag, 'D': D, 'length': length}
    _L3_cond_all = _L3_cond_setup()
    _L3_cond_in = {k: v for k, v in _L3_cond_all.items() if k in ('log_dt', 'C', 'log_A_real', 'A_imag', 'D')}
    del _L3_cond_all
    return {'x': x, 'itok_B_0_7': itok_B_0_7, 'itok_B_0_23': itok_B_0_23, 'itok_B_3_7': itok_B_3_7, 'itok_B_78_3631': itok_B_78_3631, 'L0_cond_W': _L0_cond_in['W'], 'L0_cond_Wr': _L0_cond_in['Wr'], 'L0_cond_A': _L0_cond_in['A'], 'L0_cond_B': _L0_cond_in['B'], 'L1_cond_W': _L1_cond_in['W'], 'L1_cond_b': _L1_cond_in['b'], 'L1_cond_lora_As': _L1_cond_in['lora_As'], 'L1_cond_lora_Bs': _L1_cond_in['lora_Bs'], 'L2_cond_weight': _L2_cond_in['weight'], 'L3_cond_log_dt': _L3_cond_in['log_dt'], 'L3_cond_C': _L3_cond_in['C'], 'L3_cond_log_A_real': _L3_cond_in['log_A_real'], 'L3_cond_A_imag': _L3_cond_in['A_imag'], 'L3_cond_D': _L3_cond_in['D']}

def reference(x, itok_B_0_7, itok_B_0_23, itok_B_3_7, itok_B_78_3631, L0_cond_W, L0_cond_Wr, L0_cond_A, L0_cond_B, L1_cond_W, L1_cond_b, L1_cond_lora_As, L1_cond_lora_Bs, L2_cond_weight, L3_cond_log_dt, L3_cond_C, L3_cond_log_A_real, L3_cond_A_imag, L3_cond_D):
    import jax
    import jax.numpy as jnp

    def _L0_cond_ref(x, language_ids, W, Wr, A, B):
        import jax, jax.numpy as jnp
        import numpy as np
        TOP_K = 2
        LANG_BIAS = 5.0
        SCALING = 32.0 / 16.0
        LANGUAGE_PAD_ID = -1
        base = jnp.einsum('btd,od->bto', x, W)
        E = Wr.shape[0]
        logits = jnp.einsum('btd,ed->bte', x.astype(jnp.float32), Wr.astype(jnp.float32))
        expert_targets = language_ids
        valid = expert_targets >= 0
        tgt = jnp.where(valid, expert_targets, 0)
        bias = jax.nn.one_hot(tgt, E, dtype=logits.dtype) * LANG_BIAS
        bias = jnp.where(valid[:, None], bias, 0.0)
        logits = logits + bias[:, None, :]
        topw, topi = jax.lax.top_k(logits, TOP_K)
        weights = jax.nn.softmax(topw, axis=-1)
        gates = jnp.sum(jax.nn.one_hot(topi, E, dtype=weights.dtype) * weights[..., None], axis=-2)
        gates = gates.astype(x.dtype)
        h = jnp.einsum('btd,erd->bter', x, A)
        lora_out = jnp.einsum('bter,bte,eor->bto', h, gates, B)
        return base + SCALING * lora_out

    def _L1_cond_ref(x, adapter_mapping, W, b, lora_As, lora_Bs):
        import jax, jax.numpy as jnp
        import numpy as np
        R = 16
        ALPHA = 32
        SCALING = ALPHA / R
        SLOTS = 32
        IN_F = 1024
        OUT_F = 1024
        B, T = (8, 256)
        base_out = jnp.einsum('bti,oi->bto', x, W) + b
        A = lora_As[adapter_mapping]
        Bm = lora_Bs[adapter_mapping]
        lora_h = jnp.einsum('bti,bir->btr', x, A)
        lora_out = jnp.einsum('btr,bro->bto', lora_h, Bm)
        return base_out + lora_out * SCALING

    def _L2_cond_ref(x, weight, adapter_ids):
        import jax, jax.numpy as jnp
        import numpy as np
        MAX_LORAS, OUT, IN = (8, 1024, 1024)
        B, S = (4, 512)
        w = weight[adapter_ids]
        return jnp.einsum('bsi,boi->bso', x, w)

    def _L3_cond_ref(u, log_dt, C, log_A_real, A_imag, D, length):
        import math
        import jax, jax.numpy as jnp
        import numpy as np
        B, H, N, L = (16, 64, 64, 1024)
        DT_MIN, DT_MAX = (0.001, 0.1)

        def _get_kernel(log_dt, C, log_A_real, A_imag, length):
            dt = jnp.exp(log_dt)
            Cc = C[..., 0] + 1j * C[..., 1]
            A = -jnp.exp(log_A_real) + 1j * A_imag
            dtA = A * dt[:, None]
            Ct = Cc * (jnp.exp(dtA) - 1.0) / A
            P = dtA[:, :, None] * jnp.arange(length, dtype=jnp.float32)
            K = 2.0 * jnp.einsum('hn,hnl->hl', Ct, jnp.exp(P)).real
            return K
        Bq, Hq, Lq = u.shape
        K = _get_kernel(log_dt, C, log_A_real, A_imag, Lq)
        n = 2 * Lq
        kf = jnp.fft.rfft(K, n=n)
        uf = jnp.fft.rfft(u, n=n)
        y = jnp.fft.irfft(uf * kf[None], n=n)[..., :Lq]
        y = y + u * D[:, None]
        mask = (jnp.arange(Lq)[None, :] < length[:, None]).astype(u.dtype)
        return y * mask[:, None, :]
    x = x + _L0_cond_ref(x, itok_B_0_7, L0_cond_W, L0_cond_Wr, L0_cond_A, L0_cond_B)
    x = x + _L1_cond_ref(x, itok_B_0_23, L1_cond_W, L1_cond_b, L1_cond_lora_As, L1_cond_lora_Bs)
    x = x + _L2_cond_ref(x, L2_cond_weight, itok_B_3_7)
    x = x + _L3_cond_ref(x, L3_cond_log_dt, L3_cond_C, L3_cond_log_A_real, L3_cond_A_imag, L3_cond_D, itok_B_78_3631)
    return x

_drawn_inputs = setup_inputs


def setup_inputs(seed=0):
    import zlib

    import numpy as np

    out = dict(_drawn_inputs(seed))
    spreads = {'L3_cond_log_A_real': (-0.6931471824645996, 0.2)}
    factors = {'L0_cond_Wr': 6.321, 'L1_cond_b': 6.156}
    for name, (base, spread) in spreads.items():
        noise = np.random.default_rng([zlib.crc32(name.encode()), seed]).standard_normal(out[name].shape)
        drawn = base * np.exp(spread * noise) if base else spread * noise
        out[name] = jnp.asarray(drawn.astype(out[name].dtype))
    for name, factor in factors.items():
        out[name] = (out[name] * factor).astype(out[name].dtype)
    return out
```

```python
from contextlib import ExitStack

import concourse.bass as bass
from concourse import mybir

ALU = mybir.AluOpType
ACT = mybir.ActivationFunctionType
AX = mybir.AxisListType
F32 = mybir.dt.float32
F32R = mybir.dt.float32r
I32 = mybir.dt.int32
U32 = mybir.dt.uint32
BF16 = mybir.dt.bfloat16

P = 128
BATCHES, STEPS, D = 128, 64, 1024
KB = D // P
EXPERTS0, RANK = 8, 16
ADAPTERS = 32
ER = EXPERTS0 * RANK
EXPERTS2 = 8
TOK = 512
TILES = BATCHES * STEPS // TOK
TB = TOK // STEPS
SUB = TOK // P
AW = (KB + 1) * RANK
HALF = 512

SLOTS = (BATCHES + EXPERTS2) // 2
PLACES = 2 * SLOTS
T_READ, T_WRITE, T_PAR, T_RANK, T_FREE = 0, 144, 288, 360, 432
T_EXPERT, T_COUNT = 440, 448
T_WIDTH = 449

NS = 64
QN, RN = 32, 32
KROW = 1152
ROUND = 12582912.0
TWO_PI = 6.283185307179586
TWO_PI_HI = 6.28125
TWO_PI_LO = TWO_PI - TWO_PI_HI


def both(nc, name, shape, ctx):
    return (ctx.enter_context(nc.sbuf_tensor(name + "_hi", shape, F32R)),
            ctx.enter_context(nc.sbuf_tensor(name + "_lo", shape, F32R)))


def scope(nc):
    ctx = ExitStack()

    def sb(name, shape, dt=F32):
        return ctx.enter_context(nc.sbuf_tensor(name, shape, dt))

    def ps(name, shape):
        return ctx.enter_context(nc.psum_tensor(name, shape, F32))

    def sem(name):
        return ctx.enter_context(nc.semaphore(name))

    return ctx, sb, ps, sem


def tables_phase(nc, keep, io):
    ctx, sb, ps, sem = scope(nc)
    with ctx:
        ones = sb("ones", [P, P])
        before = sb("before", [P, P])
        zrow = sb("zrow", [STEPS, P])
        iota_f = sb("iota_f", [P, 144])
        iota_p = sb("iota_p", [P, 1])
        tri = sb("tri", [P, 8, 8])
        eid_i = sb("eid_i", [P, 1], I32)
        eid = sb("eid", [P, 1])
        lang_i = sb("lang_i", [P, BATCHES], I32)
        lang = sb("lang", [P, BATCHES])
        langs = sb("langs", [P, STEPS])
        len_i = sb("len_i", [P, 1], I32)
        oh = sb("oh", [P, 8])
        cum = sb("cum", [P, 2, 8])
        nslot = sb("nslot", [P, 8])
        cum3 = sb("cum3", [P, 8, 8])
        end = sb("end", [P, 8])
        t8 = sb("t8", [P, 8])
        pos = sb("pos", [P, 1])
        ohp = sb("ohp", [P, PLACES])
        ltp = sb("ltp", [P, PLACES])
        row = sb("row", [1, 6, 144])
        cmp3 = sb("cmp3", [1, SLOTS, 8])
        es = sb("es", [1, 4, SLOTS])
        tf = sb("tf", [1, T_WIDTH])
        used = sb("used", [1, 5, 8])
        rank3 = sb("rank3", [1, 8, 8])
        cmp8 = sb("cmp8", [1, 8, 8])
        adp_i = sb("adp_i", [1, BATCHES], I32)
        ldt = sb("ldt", [P, STEPS])
        lar = sb("lar", [P, STEPS])
        aim = sb("aim", [P, STEPS])
        cre = sb("cre", [P, STEPS])
        cim = sb("cim", [P, STEPS])
        sk = sb("sk", [P, 16, STEPS])
        lq = sb("lq", [P, 2, 32])
        off = sb("off", [P, 4])
        tt = sb("tt", [P, STEPS, 32])
        tr = sb("tr", [P, STEPS, 32])
        sn = sb("sn", [P, STEPS, 32])
        mg = sb("mg", [P, STEPS, 32])
        tabs = [sb(f"tab{i}", [P, STEPS, 32]) for i in range(3)]
        acoef = sb("acoef", [P, STEPS, 32])
        kout = sb("kout", [QN, STEPS, RN])
        dskip = sb("dskip", [1, STEPS])

        p_cum = ps("p_cum", [P, HALF])
        p_row = ps("p_row", [P, HALF])
        p_k = ps("p_k", [P, 4 * HALF])

        loaded = sem("tables_loaded")
        pool_step = sem("pool_step")
        consts_ready = sem("consts_ready")
        dve_step = sem("dve_step")
        onehot_ready = sem("onehot_ready")
        places_ready = sem("places_ready")
        angles_ready = sem("angles_ready")
        phase_ready = sem("phase_ready")
        decay_ready = sem("decay_ready")
        coefs_ready = sem("coefs_ready")
        kernel_ready = sem("kernel_ready")
        act_step = sem("act_step")
        pe_step = sem("pe_step")
        stored = sem("k_stored")

        with nc.Block() as block:

            @block.sync
            def _(sp):
                halves = [(0, NS), (NS, 2 * NS)]
                for lo, hi in halves:
                    sp.dma_start(lar[lo:hi, :], io["log_a"]).then_inc(loaded, 16)
                    sp.dma_start(aim[lo:hi, :], io["a_imag"]).then_inc(loaded, 16)
                    sp.dma_start(cre[lo:hi, :], io["c"][0]).then_inc(loaded, 16)
                    sp.dma_start(cim[lo:hi, :], io["c"][1]).then_inc(loaded, 16)
                sp.dma_start(ldt[:], io["log_dt"].to_broadcast([P, STEPS])).then_inc(loaded, 16)
                sp.dma_start(lang_i[:], io["lang"].to_broadcast([P, BATCHES])).then_inc(loaded, 16)
                sp.dma_start(eid_i[:], io["expert"]).then_inc(loaded, 16)
                sp.dma_start(len_i[:], io["length"]).then_inc(loaded, 16)
                sp.dma_start(adp_i[:], io["adapter"]).then_inc(loaded, 16)
                sp.dma_start(dskip[:], io["d"]).then_inc(loaded, 16)
                sp.dma_start(keep["b1"][:], io["b1"]).then_inc(loaded, 16)
                sp.wait_ge(consts_ready, 1)
                sp.dma_start(io["kpad"][:, 0:P - 1], zrow[:, 0:P - 1]).then_inc(stored, 16)
                sp.wait_ge(kernel_ready, 1)
                sp.dma_start(
                    io["kpad"][:, P - 1:P - 1 + D].rearrange("h (q r) -> q h r", q=QN), kout[:]
                ).then_inc(stored, 16)
                sp.wait_ge(stored, 32)

            @block.gpsimd
            def _(pool):
                n = [0]

                def step(ins):
                    n[0] += 1
                    ins.then_inc(pool_step, 1)
                    pool.wait_ge(pool_step, n[0])

                step(pool.memset(ones[:], 1.0))
                step(pool.memset(zrow[:], 0.0))
                step(pool.memset(keep["zero"][:], 0.0))
                step(pool.memset(off[0:NS, 0:1], 0.25))
                step(pool.memset(off[NS:P, 0:1], 0.5))
                step(pool.memset(off[0:NS, 1:2], 0.25))
                step(pool.memset(off[NS:P, 1:2], 0.0))
                step(pool.memset(off[0:NS, 2:3], 0.5))
                step(pool.memset(off[NS:P, 2:3], 0.25))
                step(pool.iota(iota_f[:], [[1, 144]], base=0, channel_multiplier=0,
                          allow_small_or_imprecise_dtypes=True))
                step(pool.iota(iota_p[:], [[0, 1]], base=0, channel_multiplier=1,
                          allow_small_or_imprecise_dtypes=True))
                step(pool.iota(keep["iota8"][:], [[1, 8]], base=0, channel_multiplier=0,
                          allow_small_or_imprecise_dtypes=True))
                step(pool.iota(lq[:, 0, :], [[1, 32]], base=0, channel_multiplier=0,
                          allow_small_or_imprecise_dtypes=True))
                step(pool.iota(lq[:, 1, :], [[RN, 32]], base=0, channel_multiplier=0,
                          allow_small_or_imprecise_dtypes=True))
                step(pool.affine_select(out=keep["ident"][:], in_=ones[:], pattern=[[-1, P]], base=0,
                                   channel_multiplier=1, compare_op=ALU.is_equal, fill=0.0))
                step(pool.affine_select(out=keep["anti"][:], in_=ones[:], pattern=[[1, P]], base=1 - P,
                                   channel_multiplier=1, compare_op=ALU.is_equal, fill=0.0))
                step(pool.affine_select(out=before[:], in_=ones[:], pattern=[[1, P]], base=0,
                                   channel_multiplier=-1, compare_op=ALU.is_gt, fill=0.0))
                step(pool.affine_select(out=tri[:], in_=ones[:, 0:64].rearrange("p (a b) -> p a b", a=8),
                                   pattern=[[1, 8], [-1, 8]], base=0, channel_multiplier=0,
                                   compare_op=ALU.is_ge, fill=0.0))
                own = keep["own2"]
                step(pool.memset(own[:], 2.0))
                step(pool.affine_select(out=own[:], in_=own[:], pattern=[[-RANK, TB], [0, STEPS]], base=0,
                                   channel_multiplier=1, compare_op=ALU.is_ge, fill=0.0))
                pool.affine_select(out=own[:], in_=own[:], pattern=[[RANK, TB], [0, STEPS]], base=RANK,
                                   channel_multiplier=-1, compare_op=ALU.is_gt, fill=0.0).then_inc(consts_ready, 1)

            @block.vector
            def _(dve):
                counts = {}

                def step(ins, signal=dve_step):
                    counts[signal] = counts.get(signal, 0) + 1
                    ins.then_inc(signal, 1)
                    dve.wait_ge(signal, counts[signal])

                dve.wait_ge(loaded, 16 * 15)
                dve.wait_ge(consts_ready, 1)
                tbl = keep["tbl"]
                step(dve.tensor_copy(eid[:], eid_i[:]))
                step(dve.tensor_scalar(eid[:], eid[:], 0.0, float(EXPERTS2 - 1), ALU.max, ALU.min))
                step(dve.tensor_scalar(oh[:], keep["iota8"][:], eid[:, 0:1], None, ALU.is_equal), onehot_ready)
                dve.wait_ge(pe_step, 1)
                step(dve.tensor_copy(cum[:, :, :], p_cum[:, 0:16].rearrange("p (a b) -> p a b", a=2)))
                step(dve.tensor_scalar(nslot[:], cum[:, 1, :], 0.5, 0.25, ALU.mult, ALU.add))
                step(dve.tensor_scalar(nslot[:], nslot[:], ROUND, ROUND, ALU.add, ALU.subtract))
                step(dve.tensor_tensor(cum3[:], tri[:], nslot[:, None, :].to_broadcast([P, 8, 8]), ALU.mult))
                step(dve.tensor_reduce(end[:], cum3[:], AX.X, ALU.add))
                step(dve.tensor_tensor(t8[:], end[:], nslot[:], ALU.subtract))
                step(dve.scalar_tensor_tensor(t8[:], t8[:], 2.0, cum[:, 0, :], ALU.mult, ALU.add))
                step(dve.tensor_tensor(t8[:], t8[:], oh[:], ALU.mult))
                step(dve.tensor_reduce(pos[:], t8[:], AX.X, ALU.add))
                step(dve.tensor_scalar(ohp[:], iota_f[:, 0:PLACES], pos[:, 0:1], None, ALU.is_equal))
                step(dve.tensor_scalar(ltp[:], iota_f[:, 0:PLACES], pos[:, 0:1], None, ALU.is_gt), places_ready)
                dve.wait_ge(pe_step, 2)
                step(dve.tensor_copy(row[:, 0:3, 0:PLACES],
                                     p_row[0:1, 0:3 * PLACES].rearrange("p (a b) -> p a b", a=3)))
                step(dve.tensor_tensor(row[:, 3, 0:PLACES], iota_f[0:1, 0:PLACES], row[:, 2, 0:PLACES], ALU.subtract))
                step(dve.tensor_scalar(row[:, 3, 0:PLACES], row[:, 3, 0:PLACES], float(BATCHES), None, ALU.add))
                step(dve.tensor_scalar(row[:, 4, 0:PLACES], row[:, 1, 0:PLACES], -1.0, 1.0, ALU.mult, ALU.add))
                step(dve.tensor_tensor(row[:, 3, 0:PLACES], row[:, 3, 0:PLACES], row[:, 4, 0:PLACES], ALU.mult))
                step(dve.tensor_tensor(row[:, 3, 0:PLACES], row[:, 3, 0:PLACES], row[:, 0, 0:PLACES], ALU.add))
                step(dve.memset(tf[:], 1.0))
                step(dve.tensor_copy(tf[:, T_READ:T_READ + PLACES], row[:, 0, 0:PLACES]))
                step(dve.tensor_copy(tf[:, T_WRITE:T_WRITE + PLACES], row[:, 3, 0:PLACES]))
                step(dve.tensor_scalar(used[:, 0, :], nslot[0:1, :], 0.5, None, ALU.is_ge))
                step(dve.tensor_tensor(rank3[:], tri[0:1], used[:, 0, None, :].to_broadcast([1, 8, 8]), ALU.mult))
                step(dve.tensor_reduce(used[:, 1, :], rank3[:], AX.X, ALU.add))
                step(dve.tensor_tensor(rank3[:], used[:, 1, None, :].to_broadcast([1, 8, 8]),
                                       iota_f[0:1, 1:9, None].to_broadcast([1, 8, 8]), ALU.is_equal))
                step(dve.tensor_tensor(rank3[:], rank3[:], used[:, 0, None, :].to_broadcast([1, 8, 8]), ALU.mult))
                step(dve.tensor_tensor(cmp8[:], rank3[:], iota_f[0:1, None, 0:8].to_broadcast([1, 8, 8]), ALU.mult))
                step(dve.tensor_reduce(used[:, 2, :], cmp8[:], AX.X, ALU.add))
                step(dve.tensor_tensor(cmp8[:], rank3[:], end[0:1, None, :].to_broadcast([1, 8, 8]), ALU.mult))
                step(dve.tensor_reduce(used[:, 3, :], cmp8[:], AX.X, ALU.add))
                step(dve.tensor_tensor(cmp3[:], iota_f[0:1, 0:SLOTS, None].to_broadcast([1, SLOTS, 8]),
                                       end[0:1, None, :].to_broadcast([1, SLOTS, 8]), ALU.is_ge))
                step(dve.tensor_tensor(cmp3[:], cmp3[:], used[:, 0, None, :].to_broadcast([1, SLOTS, 8]), ALU.mult))
                step(dve.tensor_reduce(es[:, 0, :], cmp3[:], AX.X, ALU.add))
                step(dve.tensor_scalar(used[:, 4, 0:1], used[:, 1, 7:8], -1.0, None, ALU.add))
                step(dve.tensor_scalar(es[:, 0, :], es[:, 0, :], used[:, 4, 0:1], None, ALU.min))
                step(dve.tensor_scalar(es[:, 1, :], es[:, 0, :], 0.5, 0.25, ALU.mult, ALU.subtract))
                step(dve.tensor_scalar(es[:, 1, :], es[:, 1, :], ROUND, ROUND, ALU.add, ALU.subtract))
                step(dve.scalar_tensor_tensor(tf[:, T_PAR:T_PAR + SLOTS], es[:, 1, :], -2.0, es[:, 0, :],
                                              ALU.mult, ALU.add))
                step(dve.tensor_copy(tf[:, T_RANK:T_RANK + SLOTS], es[:, 0, :]))
                step(dve.tensor_scalar(tf[:, T_FREE + 2:T_FREE + 8], used[:, 3, 0:6], 1.0, None, ALU.add))
                step(dve.tensor_copy(tf[:, T_EXPERT:T_EXPERT + 8], used[:, 2, :]))
                step(dve.tensor_copy(tf[:, T_COUNT:T_COUNT + 1], used[:, 1, 7:8]))
                step(dve.tensor_copy(tbl[:], tf[:]))
                step(dve.tensor_scalar(keep["adapter"][:], adp_i[:], 0, ADAPTERS - 1, ALU.max, ALU.min))
                step(dve.tensor_copy(keep["length"][:], len_i[:]))
                step(dve.tensor_copy(lang[:], lang_i[:]))
                lv = lang[:].rearrange("p (s two) -> p s two", two=2)
                step(dve.tensor_copy(langs[0:STEPS, :], lv[0:STEPS, :, 0]))
                step(dve.tensor_copy(langs[STEPS:P, :], lv[STEPS:P, :, 1]))
                gb = keep["gate_bias"]
                step(dve.tensor_tensor(gb[:], keep["iota8"][:, None, :].to_broadcast([P, STEPS, 8]),
                                       langs[:, :, None].to_broadcast([P, STEPS, 8]), ALU.is_equal))
                step(dve.tensor_scalar(gb[:], gb[:], 5.0, None, ALU.mult))
                DT, AR, DRE, DIM, UF, T0, T1, MAG, SI, CO, NR, NI, IV, CR, CI, T2 = range(16)
                dve.wait_ge(act_step, 2)
                step(dve.tensor_scalar(sk[:, AR, :], sk[:, AR, :], -1.0, None, ALU.mult))
                step(dve.tensor_tensor(sk[:, DRE, :], sk[:, AR, :], sk[:, DT, :], ALU.mult))
                step(dve.tensor_tensor(sk[:, DIM, :], aim[:], sk[:, DT, :], ALU.mult))
                step(dve.tensor_scalar(sk[:, T0, :], sk[:, DIM, :], 1.0 / TWO_PI, None, ALU.mult))
                step(dve.tensor_scalar(sk[:, T1, :], sk[:, T0, :], ROUND, ROUND, ALU.add, ALU.subtract))
                step(dve.scalar_tensor_tensor(sk[:, T0, :], sk[:, T1, :], -TWO_PI_HI, sk[:, DIM, :], ALU.mult, ALU.add))
                step(dve.scalar_tensor_tensor(sk[:, T0, :], sk[:, T1, :], -TWO_PI_LO, sk[:, T0, :], ALU.mult, ALU.add))
                step(dve.tensor_scalar(sk[:, UF, :], sk[:, T0, :], 1.0 / TWO_PI, None, ALU.mult))
                step(dve.tensor_scalar(sk[:, T0, :], sk[:, UF, :], 0.25, None, ALU.add))
                step(dve.tensor_scalar(sk[:, T1, :], sk[:, T0, :], ROUND, ROUND, ALU.add, ALU.subtract))
                step(dve.tensor_tensor(sk[:, T0, :], sk[:, T0, :], sk[:, T1, :], ALU.subtract), angles_ready)
                dve.wait_ge(act_step, 5)
                step(dve.tensor_tensor(sk[:, NR, :], sk[:, MAG, :], sk[:, CO, :], ALU.mult))
                step(dve.tensor_scalar(sk[:, NR, :], sk[:, NR, :], -1.0, None, ALU.add))
                step(dve.tensor_tensor(sk[:, NI, :], sk[:, MAG, :], sk[:, SI, :], ALU.mult))
                step(dve.tensor_tensor(sk[:, T0, :], sk[:, AR, :], sk[:, AR, :], ALU.mult))
                step(dve.tensor_tensor(sk[:, T1, :], aim[:], aim[:], ALU.mult))
                step(dve.tensor_tensor(sk[:, T0, :], sk[:, T0, :], sk[:, T1, :], ALU.add))
                step(dve.tensor_scalar(sk[:, T0, :], sk[:, T0, :], 0.5, None, ALU.mult))
                step(dve.reciprocal(sk[:, IV, :], sk[:, T0, :]))
                step(dve.tensor_tensor(sk[:, T0, :], cre[:], sk[:, NR, :], ALU.mult))
                step(dve.tensor_tensor(sk[:, T1, :], cim[:], sk[:, NI, :], ALU.mult))
                step(dve.tensor_tensor(sk[:, T0, :], sk[:, T0, :], sk[:, T1, :], ALU.subtract))
                step(dve.tensor_tensor(sk[:, T1, :], cre[:], sk[:, NI, :], ALU.mult))
                step(dve.tensor_tensor(sk[:, T2, :], cim[:], sk[:, NR, :], ALU.mult))
                step(dve.tensor_tensor(sk[:, T1, :], sk[:, T1, :], sk[:, T2, :], ALU.add))
                step(dve.tensor_tensor(sk[:, CR, :], sk[:, T0, :], sk[:, AR, :], ALU.mult))
                step(dve.tensor_tensor(sk[:, T2, :], sk[:, T1, :], aim[:], ALU.mult))
                step(dve.tensor_tensor(sk[:, CR, :], sk[:, CR, :], sk[:, T2, :], ALU.add))
                step(dve.tensor_tensor(sk[:, CR, :], sk[:, CR, :], sk[:, IV, :], ALU.mult))
                step(dve.tensor_tensor(sk[:, CI, :], sk[:, T1, :], sk[:, AR, :], ALU.mult))
                step(dve.tensor_tensor(sk[:, T2, :], sk[:, T0, :], aim[:], ALU.mult))
                step(dve.tensor_tensor(sk[:, CI, :], sk[:, CI, :], sk[:, T2, :], ALU.subtract))
                step(dve.tensor_tensor(sk[:, CI, :], sk[:, CI, :], sk[:, IV, :], ALU.mult))
                wide = [P, STEPS, 32]
                for i, which in enumerate((0, 1, 1)):
                    lb = lq[:, which, None, :].to_broadcast(wide)
                    if i:
                        dve.wait_ge(act_step, 5 + 2 * i)
                    step(dve.tensor_tensor(tt[:], sk[:, UF, :, None].to_broadcast(wide), lb, ALU.mult))
                    step(dve.tensor_scalar(tt[:], tt[:], off[:, i:i + 1], None, ALU.add))
                    step(dve.tensor_scalar(tr[:], tt[:], ROUND, ROUND, ALU.add, ALU.subtract))
                    step(dve.tensor_tensor(tt[:], tt[:], tr[:], ALU.subtract), phase_ready)
                    step(dve.tensor_tensor(tr[:], sk[:, DRE, :, None].to_broadcast(wide), lb, ALU.mult), decay_ready)
                    dve.wait_ge(act_step, 7 + 2 * i)
                    step(dve.tensor_tensor(tabs[i][:], sn[:], mg[:], ALU.mult))
                step(dve.tensor_tensor(acoef[:], tabs[1][:], sk[:, CR, :, None].to_broadcast(wide), ALU.mult))
                step(dve.tensor_tensor(tabs[2][:], tabs[2][:], sk[:, CI, :, None].to_broadcast(wide), ALU.mult))
                step(dve.tensor_tensor(acoef[:], acoef[:], tabs[2][:], ALU.add), coefs_ready)
                dve.wait_ge(pe_step, 3)
                step(dve.tensor_copy(kout[:], p_k[0:QN, :].rearrange("q (h r) -> q h r", r=RN)))
                step(dve.tensor_tensor(kout[0:1, :, 0], kout[0:1, :, 0], dskip[:], ALU.add), kernel_ready)

            @block.scalar
            def _(act):
                DT, AR, DRE, DIM, UF, T0, T1, MAG, SI, CO = range(10)
                act.wait_ge(loaded, 16 * 15)
                act.wait_ge(consts_ready, 1)
                act.activation(sk[:, DT, :], ldt[:], ACT.Exp, bias=keep["zero"][:]).then_inc(act_step, 1)
                act.activation(sk[:, AR, :], lar[:], ACT.Exp, bias=keep["zero"][:]).then_inc(act_step, 1)
                act.wait_ge(angles_ready, 1)
                act.activation(sk[:, MAG, :], sk[:, DRE, :], ACT.Exp, bias=keep["zero"][:]).then_inc(act_step, 1)
                act.activation(sk[:, SI, :], sk[:, UF, :], ACT.Sin, bias=keep["zero"][:], scale=TWO_PI).then_inc(act_step, 1)
                act.activation(sk[:, CO, :], sk[:, T0, :], ACT.Sin, bias=keep["zero"][:], scale=TWO_PI).then_inc(act_step, 1)
                for i in range(3):
                    act.wait_ge(phase_ready, i + 1)
                    act.activation(sn[:], tt[:], ACT.Sin, bias=keep["zero"][:], scale=TWO_PI).then_inc(act_step, 1)
                    act.wait_ge(decay_ready, i + 1)
                    act.activation(mg[:], tr[:], ACT.Exp, bias=keep["zero"][:]).then_inc(act_step, 1)

            @block.tensor
            def _(pe):
                pe.wait_ge(onehot_ready, 1)
                pe.wait_ge(consts_ready, 1)
                pe.matmul(p_cum[:, 0:8], before[:], oh[:], start=True, stop=True)
                pe.matmul(p_cum[:, 8:16], ones[:], oh[:], start=True, stop=True).then_inc(pe_step, 1)
                pe.wait_ge(places_ready, 1)
                pe.matmul(p_row[0:1, 0:PLACES], iota_p[:], ohp[:], start=True, stop=True)
                pe.matmul(p_row[0:1, PLACES:2 * PLACES], ones[:, 0:1], ohp[:], start=True, stop=True)
                pe.matmul(p_row[0:1, 2 * PLACES:3 * PLACES], ones[:, 0:1], ltp[:], start=True,
                          stop=True).then_inc(pe_step, 1)
                pe.wait_ge(coefs_ready, 1)
                for h in range(STEPS):
                    last = pe.matmul(p_k[0:QN, h * RN:(h + 1) * RN], acoef[:, h, :], tabs[0][:, h, :],
                                     start=True, stop=True)
                last.then_inc(pe_step, 1)




def products_phase(nc, keep, io):
    ctx, sb, ps, sem = scope(nc)
    QW = D + ADAPTERS * RANK
    NCH = QW // HALF
    with ctx:
        q_hi, q_lo = both(nc, "q", [P, KB, QW], ctx)
        q_raw = sb("q_raw", [P, 2, QW])
        s_raw = [sb(f"s_raw{i}", [P, KB, P]) for i in range(2)]
        s_parts = [both(nc, f"s{i}", [P, KB, P], ctx) for i in range(2)]
        prod = sb("prod", [P, 2, D])
        pa = sb("pa", [P, ADAPTERS, KB + 1, RANK])
        p_g = [ps(f"p_g{i}", [P, NCH * HALF]) for i in range(2)]

        q_loaded = [sem(f"q_loaded{i}") for i in range(2)]
        s_loaded = [sem(f"s_loaded{i}") for i in range(2)]
        q_diag = sem("q_diag")
        s_diag = sem("s_diag")
        q_hi_ready = sem("q_hi_ready")
        q_ready = sem("q_ready")
        s_hi_ready = sem("s_hi_ready")
        s_ready = sem("s_ready")
        block_done = sem("block_done")
        m_copied = sem("m_copied")
        a_copied = sem("a_copied")
        m_stored = [sem(f"m_stored{i}") for i in range(2)]
        a_stored = sem("a_stored")

        with nc.Block() as block:

            @block.sync
            def _(sp):
                def load_s(m, par):
                    sp.wait_ge(s_ready, m + 1)
                    sp.dma_start(s_raw[par][:], io["s0"][bass.ds(m, 1)].rearrange("a p j c -> p (a j) c")
                                 ).then_inc(s_loaded[par], 16)

                load_s(0, 0)
                for j in range(KB):
                    if j >= 2:
                        sp.wait_ge(q_ready, j - 1)
                    sp.dma_start(q_raw[:, j % 2, 0:D], io["w1t"][j]).then_inc(q_loaded[j % 2], 16)
                    sp.dma_start(q_raw[:, j % 2, D:QW], io["a1"][j]).then_inc(q_loaded[j % 2], 16)
                    if j == 1:
                        load_s(1, 1)
                with sp.Fori(1, 4) as i:
                    load_s(2 * i, 0)
                    load_s(2 * i + 1, 1)
                load_s(8, 0)
                sp.wait_ge(a_copied, 2 + KB + 1)
                sp.dma_start(io["pa"].rearrange("s p c -> p s c"), pa[:].rearrange("p s k r -> p s (k r)")
                             ).then_inc(a_stored, 16)
                sp.wait_ge(a_stored, 16)

            @block.gpsimd
            def _(pool):
                ident = keep["ident"]

                def diag_s(m, par, n):
                    pool.wait_ge(s_loaded[par], 16 * n)
                    blk = s_raw[par][:, bass.ds(m, 1), :].rearrange("p a c -> p (a c)")
                    pool.tensor_tensor(blk, blk, ident[:], ALU.add).then_inc(s_diag, 1)

                diag_s(0, 0, 1)
                for j in range(KB):
                    pool.wait_ge(q_loaded[j % 2], 32 * (j // 2 + 1))
                    blk = q_raw[:, j % 2, j * P:(j + 1) * P]
                    pool.tensor_tensor(blk, blk, ident[:], ALU.add).then_inc(q_diag, 1)
                diag_s(1, 1, 1)
                with pool.Fori(1, 4) as i:
                    diag_s(2 * i, 0, i + 1)
                    diag_s(2 * i + 1, 1, i + 1)

            @block.scalar
            def _(act):
                def split_s(m, par, last=False):
                    if last:
                        act.wait_ge(s_loaded[par], 16 * 5)
                    else:
                        act.wait_ge(s_diag, m + 1)
                    act.wait_ge(block_done, m)
                    act.copy(s_parts[par][0][:], s_raw[par][:]).then_inc(s_hi_ready, 1)

                def take_m(m, par, n):
                    act.wait_ge(block_done, m + 2)
                    act.wait_ge(m_stored[par], 16 * n)
                    act.copy(prod[:, par, :], p_g[par][:, 0:D]).then_inc(m_copied, 1)
                    act.wait_ge(m_copied, m + 3)
                    act.dma_start(io["m01"][bass.ds(m, 1)].rearrange("a p c -> p (a c)"), prod[:, par, :]
                                  ).then_inc(m_stored[par], 16)

                act.sem_inc(m_copied, 2)
                act.sem_inc(m_stored[0], 16)
                act.sem_inc(m_stored[1], 16)
                act.wait_ge(s_diag, 1)
                act.copy(s_parts[0][0][:], s_raw[0][:]).then_inc(s_hi_ready, 1)
                for j in range(KB):
                    act.wait_ge(q_diag, j + 1)
                    act.copy(q_hi[:, j, :], q_raw[:, j % 2, :]).then_inc(q_hi_ready, 1)
                with act.Fori(0, 3) as i:
                    split_s(2 * i + 1, 1)
                    take_m(2 * i, 0, i + 1)
                    split_s(2 * i + 2, 0)
                    take_m(2 * i + 1, 1, i + 1)
                split_s(7, 1)
                take_m(6, 0, 4)
                split_s(8, 0, last=True)
                take_m(7, 1, 4)
                take_m(8, 0, 5)
                act.wait_ge(m_stored[0], 16 * 6)
                act.wait_ge(m_stored[1], 16 * 5)

            @block.vector
            def _(dve):
                def rest_s(m, par):
                    dve.wait_ge(s_hi_ready, m + 1)
                    dve.tensor_tensor(s_parts[par][1][:], s_raw[par][:], s_parts[par][0][:], ALU.subtract
                                      ).then_inc(s_ready, 1)

                def take_a(m, par):
                    dve.wait_ge(block_done, m + 2)
                    dst = pa[:, :, bass.ds(m, 1), :].rearrange("p s a r -> p s (a r)")
                    dve.tensor_copy(dst, p_g[par][:, D:QW].rearrange("p (s r) -> p s r", r=RANK)
                                    ).then_inc(a_copied, 1)

                dve.sem_inc(a_copied, 2)
                dve.sem_inc(s_ready, 2)
                rest_s(0, 0)
                for j in range(KB):
                    dve.wait_ge(q_hi_ready, j + 1)
                    dve.tensor_tensor(q_lo[:, j, :], q_raw[:, j % 2, :], q_hi[:, j, :], ALU.subtract
                                      ).then_inc(q_ready, 1)
                with dve.Fori(0, 4) as i:
                    rest_s(2 * i + 1, 1)
                    take_a(2 * i, 0)
                    rest_s(2 * i + 2, 0)
                    take_a(2 * i + 1, 1)
                take_a(8, 0)

            @block.tensor
            def _(pe):
                def product(m, par, first=False):
                    pe.wait_ge(s_ready, m + 3)
                    pe.wait_ge(m_copied, m + 1)
                    pe.wait_ge(a_copied, m + 1)
                    hi, lo = s_parts[par]
                    for j in range(KB):
                        if first:
                            pe.wait_ge(q_ready, j + 1)
                        for w, q, start, stop in ((hi, q_hi, j == 0, False), (hi, q_lo, False, False),
                                                  (lo, q_hi, False, j == KB - 1)):
                            for n in range(NCH):
                                last = pe.matmul(p_g[par][:, n * HALF:(n + 1) * HALF], w[:, j, :],
                                                 q[:, j, n * HALF:(n + 1) * HALF], start=start, stop=stop)
                    last.then_inc(block_done, 1)

                pe.sem_inc(block_done, 1)
                product(0, 0, first=True)
                product(1, 1)
                with pe.Fori(1, 4) as i:
                    product(2 * i, 0)
                    product(2 * i + 1, 1)
                product(8, 0)


def layers01_phase(nc, keep, io):
    ctx, sb, ps, sem = scope(nc)
    with ctx:
        m_hi, m_lo = both(nc, "m01", [P, KB + 1, D], ctx)
        x_parts = [both(nc, f"x{i}", [P, KB, TOK], ctx) for i in range(2)]
        x_raw = sb("x_raw", [P, 2, TOK])
        a0_hi, a0_lo = both(nc, "a0", [P, KB, P], ctx)
        wr_raw = sb("wr_raw", [P, KB, 8])
        wr = sb("wr_hi_lo", [P, (KB - 1) * 16 + P], F32R)
        wr_k = wr[:, 0:KB * 16].rearrange("p (k c) -> p k c", c=16)
        logits_t = sb("logits_t", [16, TOK])
        pa_raw = sb("pa_raw", [P, TB, AW])
        pa_hi, pa_lo = both(nc, "pa_tile", [P, KB + 1, TB * RANK], ctx)
        w_raw = sb("w_raw", [P, D])
        b_hi, b_lo = both(nc, "b1_tile", [P, D], ctx)
        g_parts = [both(nc, f"g{i}", [P, TOK], ctx) for i in range(2)]
        h1_hi, h1_lo = both(nc, "h1", [P, TOK], ctx)
        scratch = sb("scratch", [P, TOK])
        h0 = sb("h0", [P, TOK])
        gexp = sb("gexp", [P, SUB, P])
        x2_out = sb("x2_out", [P, 2, TOK])
        lg = sb("lg", [P, 3, SUB, 8])
        top = sb("top", [P, SUB, 8])
        topi = sb("topi", [P, SUB, 8], U32)
        topf = sb("topf", [P, SUB, 2])
        wt = sb("wt", [P, 5, SUB])

        staged = [w_raw[:], x2_out[:].rearrange("p a n -> p (a n)")]

        p_out = [ps(f"p_out{i}", [P, TOK]) for i in range(4)]
        p_lg = ps("p_lg", [P, TOK])
        p_h0 = ps("p_h0", [P, TOK])
        p_h1 = ps("p_h1", [P, TOK])
        p_gt = ps("p_gt", [P, TOK])

        wr_loaded = sem("wr_loaded")
        w_loaded = [sem(f"w_loaded{i}") for i in range(2)]
        x_loaded = [sem(f"x_loaded{i}") for i in range(2)]
        pa_loaded = sem("pa_loaded")
        b_loaded = sem("b_loaded")
        wr_hi_ready = sem("wr_hi_ready")
        wr_ready = sem("wr_ready")
        w_hi_ready = sem("w_hi_ready")
        w_ready = sem("w_ready")
        x_hi_ready = sem("x_hi_ready")
        x_ready = sem("x_ready")
        pa_hi_ready = sem("pa_hi_ready")
        pa_ready = sem("pa_ready")
        b_hi_ready = sem("b_hi_ready")
        b_ready = sem("b_ready")
        ranks_done = sem("ranks_done")
        out_done = sem("out_done")
        out_copied = sem("out_copied")
        out_stored = [sem(f"out_stored{i}") for i in range(2)]
        logits_done = sem("logits_done")
        logits_copied = sem("logits_copied")
        logits_turned = sem("logits_turned")
        h0_done = sem("h0_done")
        h0_copied = sem("h0_copied")
        gap_ready = sem("gap_ready")
        exp_ready = sem("exp_ready")
        gexp_ready = sem("gexp_ready")
        gates_turned = sem("gates_turned")
        g_product = sem("g_product")
        g_hi_ready = sem("g_hi_ready")
        h1_product = sem("h1_product")
        h1_hi_ready = sem("h1_hi_ready")
        g_ready = sem("g_ready")
        h1_ready = sem("h1_ready")
        dve_step = sem("dve_step01")
        dve_passed = sem("dve_passed")
        pe_passed = sem("pe_passed")
        pool_passed = sem("pool_passed01")
        adapter = keep["adapter"]

        with nc.Block() as block:

            @block.sync
            def _(sp):
                def adapters_of(t):
                    return [sp.value_load(adapter[0:1, bass.ds(t * TB + b, 1)], min_val=0,
                                          max_val=ADAPTERS - 1) for b in range(TB)]

                def load_pa(t, slots):
                    sp.wait_ge(pa_ready, t + 1)
                    for b in range(TB):
                        sp.dma_start(pa_raw[:, b, :], io["pa"][bass.ds(slots[b], 1)].rearrange("a p c -> p (a c)")
                                     ).then_inc(pa_loaded, 16)

                def load_b(t, slots):
                    sp.wait_ge(b_ready, t + 1)
                    for b in range(TB):
                        sp.dma_start(w_raw[b * RANK:(b + 1) * RANK, :],
                                     io["b1r"][bass.ds(slots[b], 1)].rearrange("a r c -> (a r) c")
                                     ).then_inc(b_loaded, 16)

                def load_x(t):
                    for k in range(KB):
                        sp.wait_ge(x_ready, t * KB + k + 1)
                        sp.dma_start(x_raw[:, k % 2, :],
                                     io["xt"][bass.ds(t, 1), :, k, :].rearrange("a p n -> p (a n)")
                                     ).then_inc(x_loaded[k % 2], 16)

                sp.dma_start(wr_raw[:], io["wr"]).then_inc(wr_loaded, 16)
                sp.dma_start(staged[0], io["a0"]).then_inc(w_loaded[0], 16)
                slots = adapters_of(0)
                load_pa(0, slots)
                load_x(0)
                for n in range(1, KB + 2):
                    if n >= 2:
                        sp.wait_ge(w_ready, n - 1)
                    sp.dma_start(staged[n % 2], io["m01"][n - 1]).then_inc(w_loaded[n % 2], 16)
                sp.wait_ge(w_ready, KB + 1)
                load_b(0, slots)
                with sp.Fori(1, TILES) as t:
                    slots = adapters_of(t)
                    load_pa(t, slots)
                    load_x(t)
                    load_b(t, slots)

            @block.gpsimd
            def _(pool):
                pool.sem_inc(pa_ready, 1)
                pool.sem_inc(b_ready, 1)

                def split_pa(t):
                    pool.wait_ge(pa_loaded, 16 * TB * (t + 1))
                    pool.wait_ge(ranks_done, t + 1)
                    raw = pa_raw[:].rearrange("p b (k r) -> p b k r", r=RANK)
                    hi, lo = [part[:].rearrange("p k (b r) -> p b k r", r=RANK) for part in (pa_hi, pa_lo)]
                    pool.sem_inc(pool_passed, 1)
                    pool.tensor_scalar(hi, raw, 1.0, 0.0, ALU.mult, ALU.add).then_inc(pa_hi_ready, 1)
                    pool.wait_ge(pa_hi_ready, t + 1)
                    pool.tensor_tensor(lo, raw, hi, ALU.subtract).then_inc(pa_ready, 1)

                def split_b(t):
                    pool.wait_ge(b_loaded, 16 * TB * (t + 1))
                    pool.wait_ge(out_done, t * KB + KB)
                    pool.sem_inc(pool_passed, 1)
                    pool.tensor_scalar(b_hi[:], w_raw[:], 1.0, 0.0, ALU.mult, ALU.add).then_inc(b_hi_ready, 1)
                    pool.wait_ge(b_hi_ready, t + 1)
                    pool.tensor_tensor(b_lo[:], w_raw[:], b_hi[:], ALU.subtract).then_inc(b_ready, 1)

                split_pa(0)
                with pool.Fori(0, TILES - 1) as t:
                    split_b(t)
                    split_pa(t + 1)
                split_b(TILES - 1)

            @block.scalar
            def _(act):
                def x_hi(t, par):
                    for k in range(KB):
                        if k == 0:
                            act.wait_ge(out_done, t * KB)
                        act.wait_ge(x_loaded[k % 2], t * (KB // 2) * 16 + (k // 2 + 1) * 16)
                        act.copy(x_parts[par][0][:, k, :], x_raw[:, k % 2, :]).then_inc(x_hi_ready, 1)

                def gates(t):
                    act.wait_ge(logits_done, t + 1)
                    act.copy(logits_t[:], p_lg[0:16, :]).then_inc(logits_copied, 1)
                    act.wait_ge(h0_done, t + 1)
                    act.copy(h0[:], p_h0[:]).then_inc(h0_copied, 1)
                    act.wait_ge(gap_ready, t + 1)
                    act.activation(wt[:, 1, :], wt[:, 0, :], ACT.Exp, bias=keep["zero"][:]).then_inc(exp_ready, 1)

                def take(t, o):
                    act.wait_ge(out_done, t * KB + o + KB + 1)
                    act.wait_ge(out_stored[o % 2], t * (KB // 2) * 16 + (o // 2 + 1) * 16)
                    act.activation(x2_out[:, o % 2, :], p_out[o % 4][:], ACT.Identity,
                                   bias=keep["b1"][:, o:o + 1]).then_inc(out_copied, 1)
                    act.wait_ge(out_copied, t * KB + o + 5)
                    act.dma_start(io["x2"][bass.ds(t * TB, TB), :, o, :].rearrange("b p n -> p b n"),
                                  x2_out[:, o % 2, :].rearrange("p (b n) -> p b n", b=TB)
                                  ).then_inc(out_stored[o % 2], 16)

                def tile(t, par, ahead=True):
                    if ahead:
                        x_hi(t + 1, 1 - par)
                    for o in range(KB):
                        if ahead and o == 3:
                            gates(t + 1)
                        take(t, o)

                act.sem_inc(out_copied, 4)
                act.sem_inc(out_stored[0], 16)
                act.sem_inc(out_stored[1], 16)
                act.wait_ge(wr_loaded, 16)
                act.copy(wr_k[:, :, 0:8], wr_raw[:]).then_inc(wr_hi_ready, 1)
                act.wait_ge(w_loaded[0], 16)
                act.copy(a0_hi[:].rearrange("p k c -> p (k c)"), staged[0]).then_inc(w_hi_ready, 1)
                for k in range(KB):
                    act.wait_ge(x_loaded[k % 2], (k // 2 + 1) * 16)
                    act.copy(x_parts[0][0][:, k, :], x_raw[:, k % 2, :]).then_inc(x_hi_ready, 1)
                for n in range(1, KB + 2):
                    act.wait_ge(w_loaded[n % 2], 16 * (n // 2 + 1))
                    act.copy(m_hi[:, n - 1, :], staged[n % 2]).then_inc(w_hi_ready, 1)
                gates(0)
                with act.Fori(0, TILES // 2 - 1) as i:
                    tile(2 * i, 0)
                    tile(2 * i + 1, 1)
                tile(TILES - 2, 0)
                tile(TILES - 1, 1, ahead=False)
                for n in range(2):
                    act.wait_ge(out_stored[n], 16 * (TILES * KB // 2 + 1))

            @block.vector
            def _(dve):
                def x_lo(t, par):
                    for k in range(KB):
                        dve.wait_ge(x_hi_ready, t * KB + k + 1)
                        dve.tensor_tensor(x_parts[par][1][:, k, :], x_raw[:, k % 2, :],
                                          x_parts[par][0][:, k, :], ALU.subtract).then_inc(x_ready, 1)

                GATE_STEPS = 11 + 2 * SUB

                def gates(t):
                    n = [0]

                    def step(ins, signal=None):
                        if signal is not None:
                            ins.then_inc(signal, 1)
                            dve.wait_ge(signal, t + 1)
                        else:
                            n[0] += 1
                            ins.then_inc(dve_step, 1)
                            dve.wait_ge(dve_step, t * GATE_STEPS + n[0])

                    bias = keep["gate_bias"][:, bass.ds(t * SUB, SUB), :]
                    wide = [P, SUB, 8]
                    iota8 = keep["iota8"][:, None, :].to_broadcast(wide)
                    turned = p_gt[:, 0:SUB * 16].rearrange("p (s c) -> p s c", c=16)
                    dve.wait_ge(logits_turned, t + 1)
                    step(dve.tensor_tensor(lg[:, 0], turned[:, :, 8:16], bias, ALU.add))
                    step(dve.tensor_tensor(lg[:, 1], turned[:, :, 0:8], lg[:, 0], ALU.add))
                    for s in range(SUB):
                        dve.sem_inc(dve_passed, 1)
                        step(dve.max(top[:, s, :], lg[:, 1, s, :]))
                        dve.sem_inc(dve_passed, 1)
                        step(dve.max_index(topi[:, s, :], top[:, s, :], lg[:, 1, s, :]))
                    step(dve.tensor_tensor(wt[:, 0, :], top[:, :, 1], top[:, :, 0], ALU.subtract), gap_ready)
                    step(dve.tensor_copy(topf[:], topi[:, :, 0:2]))
                    step(dve.tensor_tensor(lg[:, 0], iota8, topf[:, :, 0:1].to_broadcast(wide), ALU.is_equal))
                    step(dve.tensor_tensor(lg[:, 1], iota8, topf[:, :, 1:2].to_broadcast(wide), ALU.is_equal))
                    dve.wait_ge(exp_ready, t + 1)
                    step(dve.tensor_scalar(wt[:, 2, :], wt[:, 1, :], 1.0, None, ALU.add))
                    step(dve.reciprocal(wt[:, 3, :], wt[:, 2, :]))
                    step(dve.tensor_tensor(wt[:, 4, :], wt[:, 1, :], wt[:, 3, :], ALU.mult))
                    step(dve.tensor_tensor(lg[:, 0], lg[:, 0], wt[:, 3, :, None].to_broadcast(wide), ALU.mult))
                    step(dve.tensor_tensor(lg[:, 1], lg[:, 1], wt[:, 4, :, None].to_broadcast(wide), ALU.mult))
                    step(dve.tensor_tensor(lg[:, 2], lg[:, 0], lg[:, 1], ALU.add))
                    step(dve.tensor_scalar(gexp[:].rearrange("p s (e r) -> p s e r", r=RANK),
                                           lg[:, 2, :, :, None].to_broadcast([P, SUB, 8, RANK]), 2.0, None,
                                           ALU.mult), gexp_ready)
                    assert n[0] == GATE_STEPS, n[0]

                def parts(product, hi, lo, product_ready, hi_ready, ready, t):
                    product.then_inc(product_ready, 1)
                    dve.wait_ge(product_ready, t + 1)
                    dve.tensor_copy(hi, scratch[:]).then_inc(hi_ready, 1)
                    dve.wait_ge(hi_ready, t + 1)
                    dve.tensor_tensor(lo, scratch[:], hi, ALU.subtract).then_inc(ready, 1)
                    dve.wait_ge(ready, t + 1)

                def gated(t, par):
                    dve.wait_ge(gates_turned, t + 1)
                    dve.wait_ge(h0_copied, t + 1)
                    parts(dve.tensor_tensor(scratch[:], p_gt[:], h0[:], ALU.mult), g_parts[par][0][:],
                          g_parts[par][1][:], g_product, g_hi_ready, g_ready, t)

                def ranks1(t):
                    dve.wait_ge(ranks_done, t + 2)
                    dve.wait_ge(out_done, t * KB + KB)
                    parts(dve.tensor_tensor(scratch[:], p_h1[:], keep["own2"][:].rearrange("p b n -> p (b n)"),
                                            ALU.mult), h1_hi[:], h1_lo[:], h1_product, h1_hi_ready, h1_ready, t)

                def tile(t, par, ahead=True):
                    ranks1(t)
                    if ahead:
                        x_lo(t + 1, 1 - par)
                        gates(t + 1)
                        gated(t + 1, 1 - par)

                dve.sem_inc(x_ready, 2)
                dve.wait_ge(wr_hi_ready, 1)
                dve.memset(wr[:, KB * 16:].bitcast(F32), 0.0).then_inc(wr_ready, 1)
                dve.tensor_tensor(wr_k[:, :, 8:16], wr_raw[:], wr_k[:, :, 0:8], ALU.subtract).then_inc(wr_ready, 1)
                dve.wait_ge(w_hi_ready, 1)
                dve.tensor_tensor(a0_lo[:].rearrange("p k c -> p (k c)"), staged[0],
                                  a0_hi[:].rearrange("p k c -> p (k c)"), ALU.subtract).then_inc(w_ready, 1)
                x_lo(0, 0)
                for n in range(1, KB + 2):
                    dve.wait_ge(w_hi_ready, n + 1)
                    dve.tensor_tensor(m_lo[:, n - 1, :], staged[n % 2], m_hi[:, n - 1, :], ALU.subtract
                                      ).then_inc(w_ready, 1)
                gates(0)
                gated(0, 0)
                with dve.Fori(0, TILES // 2 - 1) as i:
                    tile(2 * i, 0)
                    tile(2 * i + 1, 1)
                tile(TILES - 2, 0)
                tile(TILES - 1, 1, ahead=False)

            @block.tensor
            def _(pe):
                def three(out, w_hi, w_lo, v_hi, v_lo, start=False, stop=False):
                    pe.matmul(out, w_hi, v_hi, start=start, stop=False)
                    pe.matmul(out, w_hi, v_lo, start=False, stop=False)
                    return pe.matmul(out, w_lo, v_hi, start=False, stop=stop)

                def first_products(t, par):
                    x_hi, x_lo = x_parts[par]
                    pe.wait_ge(x_ready, t * KB + KB + 2)
                    for part in (x_hi, x_lo):
                        for k in range(KB):
                            last = pe.matmul(p_lg[:], wr[:, k * 16:k * 16 + P], part[:, k, :],
                                             start=(k == 0 and part is x_hi), stop=(k == KB - 1 and part is x_lo))
                    last.then_inc(logits_done, 1)
                    for k in range(KB):
                        last = three(p_h0[:], a0_hi[:, k, :], a0_lo[:, k, :], x_hi[:, k, :], x_lo[:, k, :],
                                     start=(k == 0), stop=(k == KB - 1))
                    last.then_inc(h0_done, 1)
                    pe.wait_ge(logits_copied, t + 1)
                    pe.sem_inc(pe_passed, 1)
                    for s in range(SUB):
                        last = pe.transpose(p_gt[:, s * 16:s * 16 + 16], logits_t[:, s * P:(s + 1) * P],
                                            keep["ident"][0:16, 0:16])
                    last.then_inc(logits_turned, 1)
                    pe.wait_ge(pa_ready, t + 2)
                    for k in range(KB):
                        three(p_h1[:], pa_hi[:, k, :], pa_lo[:, k, :], x_hi[:, k, :], x_lo[:, k, :],
                              start=(k == 0))

                def turn_gates(t):
                    pe.wait_ge(gexp_ready, t + 1)
                    for s in range(SUB):
                        last = pe.transpose(p_gt[:, s * P:(s + 1) * P], gexp[:, s, :], keep["ident"][:])
                    last.then_inc(gates_turned, 1)

                def last_ranks(t, par):
                    pe.wait_ge(g_ready, t + 1)
                    three(p_h1[:], pa_hi[:, KB, :], pa_lo[:, KB, :], g_parts[par][0][:], g_parts[par][1][:],
                          stop=True).then_inc(ranks_done, 1)

                def tile(t, par, ahead=True):
                    x_hi, x_lo = x_parts[par]
                    for o in range(KB):
                        if ahead and o == 3:
                            first_products(t + 1, 1 - par)
                        if ahead and o == 5:
                            turn_gates(t + 1)
                        if ahead and o == 7:
                            last_ranks(t + 1, 1 - par)
                        cols = slice(o * P, (o + 1) * P)
                        out = p_out[o % 4][:]
                        pe.wait_ge(out_copied, t * KB + o + 1)
                        for k in range(KB):
                            three(out, m_hi[:, k, cols], m_lo[:, k, cols], x_hi[:, k, :], x_lo[:, k, :],
                                  start=(k == 0))
                        three(out, m_hi[:, KB, cols], m_lo[:, KB, cols], g_parts[par][0][:], g_parts[par][1][:])
                        if o == 0:
                            pe.wait_ge(h1_ready, t + 1)
                            pe.wait_ge(b_ready, t + 2)
                        three(out, b_hi[:, cols], b_lo[:, cols], h1_hi[:], h1_lo[:], stop=True
                              ).then_inc(out_done, 1)

                pe.sem_inc(out_done, KB)
                pe.sem_inc(ranks_done, 1)
                pe.wait_ge(wr_ready, 2)
                pe.wait_ge(w_ready, 1)
                first_products(0, 0)
                turn_gates(0)
                last_ranks(0, 0)
                pe.wait_ge(w_ready, KB + 2)
                with pe.Fori(0, TILES // 2 - 1) as i:
                    tile(2 * i, 0)
                    tile(2 * i + 1, 1)
                tile(TILES - 2, 0)
                tile(TILES - 1, 1, ahead=False)


def layer2_phase(nc, keep, io):
    ctx, sb, ps, sem = scope(nc)
    with ctx:
        w_hi, w_lo = both(nc, "w2", [P, 2, KB, D], ctx)
        w_raw = sb("w2_raw", [P, 4, D])
        x_raw = sb("x2_raw", [P, 2, 2, KB, STEPS])
        x_parts = [both(nc, f"x2_{i}", [P, KB, P], ctx) for i in range(2)]
        x3_out = sb("x3_out", [P, 2, D])
        p_out = [ps(f"p_x3_{i}", [P, 2 * HALF]) for i in range(4)]

        w_loaded = [sem(f"w2_loaded{i}") for i in range(4)]
        w_diag = sem("w2_diag")
        w_hi_ready = sem("w2_hi_ready")
        w_ready = sem("w2_ready")
        w_chunk = sem("w2_chunk")
        x_loaded = [sem(f"x2_loaded{i}") for i in range(2)]
        x_hi_ready = sem("x2_hi_ready")
        x_ready = sem("x2_ready")
        pool_passed = sem("pool_passed2")
        slot_done = sem("slot_done")
        left_copied = sem("left_copied")
        right_copied = sem("right_copied")
        stored = [sem(f"x3_stored{i}") for i in range(2)]
        tbl = keep["tbl"]

        with nc.Block() as block:

            @block.sync
            def _(sp):
                def load(s, par):
                    a, b = [sp.value_load(tbl[0:1, bass.ds(s * 2 + (T_READ + n), 1)], min_val=0,
                                          max_val=BATCHES - 1) for n in range(2)]
                    sp.wait_ge(x_ready, s + 1)
                    for n, batch in enumerate((a, b)):
                        sp.dma_start(x_raw[:, par, n].rearrange("p k n -> p (k n)"),
                                     io["x2"][bass.ds(batch, 1)].rearrange("a p k n -> p (a k n)")
                                     ).then_inc(x_loaded[par], 16)

                with sp.Fori(0, SLOTS // 2) as i:
                    load(2 * i, 0)
                    load(2 * i + 1, 1)

            @block.gpsimd
            def _(pool):
                def expert(u, par):
                    e = pool.value_load(tbl[0:1, bass.ds(u + T_EXPERT, 1)], min_val=0, max_val=EXPERTS2 - 1)
                    free = pool.value_load(tbl[0:1, bass.ds(u + T_FREE, 1)], min_val=1, max_val=SLOTS + 1)

                    def load(k):
                        pool.wait_ge(w_chunk, u * KB + k + 1)
                        pool.dma_start(w_raw[:, k % 4, :],
                                       io["w2t"][bass.ds(e, 1), k].rearrange("a p c -> p (a c)")
                                       ).then_inc(w_loaded[k % 4], 16)

                    for k in range(4):
                        load(k)
                    pool.wait_ge(slot_done, free)
                    for k in range(KB):
                        pool.wait_ge(w_loaded[k % 4], u * 32 + (k // 4 + 1) * 16)
                        raw = w_raw[:, k % 4, :]
                        diag = w_raw[:, k % 4, k * P:(k + 1) * P]
                        pool.tensor_tensor(diag, diag, keep["anti"][:], ALU.add).then_inc(w_diag, 1)
                        pool.wait_ge(w_diag, u * KB + k + 1)
                        pool.sem_inc(pool_passed, 1)
                        pool.tensor_scalar(w_hi[:, par, k, :], raw, 1.0, 0.0, ALU.mult, ALU.add
                                           ).then_inc(w_hi_ready, 1)
                        pool.wait_ge(w_hi_ready, u * KB + k + 1)
                        pool.tensor_tensor(w_lo[:, par, k, :], raw, w_hi[:, par, k, :], ALU.subtract
                                           ).then_inc(w_chunk, 1)
                        if k + 4 < KB:
                            load(k + 4)

                pool.sem_inc(w_chunk, 4)
                count = pool.value_load(tbl[0:1, T_COUNT:T_COUNT + 1], min_val=1, max_val=EXPERTS2)
                with pool.Fori(0, EXPERTS2 // 2) as i:
                    for par in range(2):
                        with pool.If(count > 2 * i + par):
                            expert(2 * i + par, par)

            @block.scalar
            def _(act):
                def x_hi(s, par, n):
                    act.wait_ge(x_loaded[par], n * 32)
                    act.wait_ge(slot_done, s)
                    act.copy(x_parts[par][0][:].rearrange("p k (b n) -> p b k n", b=2), x_raw[:, par]
                             ).then_inc(x_hi_ready, 1)

                def take(s, par, n):
                    a, b = [act.value_load(tbl[0:1, bass.ds(s * 2 + (T_WRITE + m), 1)], min_val=0,
                                           max_val=PLACES - 1) for m in range(2)]
                    act.wait_ge(slot_done, s + 2)
                    act.wait_ge(stored[par], n * 32)
                    act.copy(x3_out[:, par, 0:HALF], p_out[par][:, 0:HALF]).then_inc(left_copied, 1)
                    act.wait_ge(left_copied, s + 5)
                    act.wait_ge(right_copied, s + 5)
                    for m, batch in enumerate((a, b)):
                        act.dma_start(io["x3"][bass.ds(batch, 1)].rearrange("a t c -> (a t) c"),
                                      x3_out[m * STEPS:(m + 1) * STEPS, par, :]).then_inc(stored[par], 16)

                act.sem_inc(left_copied, 4)
                for n in range(2):
                    act.sem_inc(stored[n], 32)
                act.wait_ge(x_loaded[0], 32)
                act.copy(x_parts[0][0][:].rearrange("p k (b n) -> p b k n", b=2), x_raw[:, 0]
                         ).then_inc(x_hi_ready, 1)
                with act.Fori(0, SLOTS // 2 - 1) as i:
                    x_hi(2 * i + 1, 1, i + 1)
                    take(2 * i, 0, i + 1)
                    x_hi(2 * i + 2, 0, i + 2)
                    take(2 * i + 1, 1, i + 1)
                x_hi(SLOTS - 1, 1, SLOTS // 2)
                take(SLOTS - 2, 0, SLOTS // 2)
                take(SLOTS - 1, 1, SLOTS // 2)
                for n in range(2):
                    act.wait_ge(stored[n], 32 * (SLOTS // 2 + 1))

            @block.vector
            def _(dve):
                def x_lo(s, par):
                    dve.wait_ge(x_hi_ready, s + 1)
                    hi, lo = [part[:].rearrange("p k (b n) -> p b k n", b=2) for part in x_parts[par]]
                    dve.tensor_tensor(lo, x_raw[:, par], hi, ALU.subtract).then_inc(x_ready, 1)

                def take(s, par, n):
                    dve.wait_ge(slot_done, s + 2)
                    dve.wait_ge(stored[par], n * 32)
                    dve.tensor_copy(x3_out[:, par, HALF:D], p_out[par][:, HALF:D]).then_inc(right_copied, 1)

                dve.sem_inc(x_ready, 2)
                dve.sem_inc(right_copied, 4)
                x_lo(0, 0)
                with dve.Fori(0, SLOTS // 2 - 1) as i:
                    x_lo(2 * i + 1, 1)
                    take(2 * i, 0, i + 1)
                    x_lo(2 * i + 2, 0)
                    take(2 * i + 1, 1, i + 1)
                x_lo(SLOTS - 1, 1)
                take(SLOTS - 2, 0, SLOTS // 2)
                take(SLOTS - 1, 1, SLOTS // 2)

            @block.tensor
            def _(pe):
                def slot(s, par):
                    wpar = pe.value_load(tbl[0:1, bass.ds(s + T_PAR, 1)], min_val=0, max_val=1)
                    rank = pe.value_load(tbl[0:1, bass.ds(s + T_RANK, 1)], min_val=0, max_val=EXPERTS2 - 1)
                    pe.wait_ge(left_copied, s + 3)
                    pe.wait_ge(right_copied, s + 3)
                    pe.wait_ge(x_ready, s + 3)
                    x_hi, x_lo = x_parts[par]
                    for n in range(2):
                        out = p_out[par][:, n * HALF:(n + 1) * HALF]
                        cols = slice(n * HALF, (n + 1) * HALF)
                        for k in range(KB):
                            if n == 0:
                                pe.wait_ge(w_chunk, rank * KB + (k + 5))
                            hi = w_hi[:, bass.ds(wpar, 1), k, cols].rearrange("p a c -> p (a c)")
                            lo = w_lo[:, bass.ds(wpar, 1), k, cols].rearrange("p a c -> p (a c)")
                            pe.matmul(out, x_hi[:, k, :], hi, start=(k == 0), stop=False)
                            pe.matmul(out, x_hi[:, k, :], lo, start=False, stop=False)
                            last = pe.matmul(out, x_lo[:, k, :], hi, start=False, stop=(k == KB - 1))
                    last.then_inc(slot_done, 1)

                pe.sem_inc(slot_done, 1)
                with pe.Fori(0, SLOTS // 2) as i:
                    slot(2 * i, 0)
                    slot(2 * i + 1, 1)


def layer3_phase(nc, keep, io):
    ctx, sb, ps, sem = scope(nc)
    with ctx:
        t_raw = sb("t_raw", [P, 2, D])
        t_parts = [both(nc, f"t{i}", [P, D], ctx) for i in range(2)]
        x_raw = sb("x3_raw", [P, 4, D])
        u_parts = [both(nc, f"u{i}", [P, KB, P], ctx) for i in range(2)]
        masked = sb("masked", [P, 2, D])
        out_sb = sb("out_sb", [P, 2, D])
        iota_l = sb("iota_l", [P, D])
        mask = sb("mask", [P, D])
        p_u = [ps(f"p_u{i}", [P, KB * P]) for i in range(2)]
        p_y = [ps(f"p_y{i}", [P, D]) for i in range(2)]

        t_loaded = [sem(f"t_loaded{i}") for i in range(2)]
        x_loaded = [sem(f"x3_loaded{i}") for i in range(4)]
        t_hi_ready = sem("t_hi_ready")
        t_ready = sem("t_ready")
        turned = sem("turned")
        u_hi_ready = sem("u_hi_ready")
        u_ready = sem("u_ready")
        pool_passed = sem("pool_passed3")
        y_done = sem("y_done")
        masked_ready = sem("masked_ready")
        out_ready = sem("out_ready")
        stored = [sem(f"out_stored{i}") for i in range(2)]
        iota_ready = sem("iota_ready")
        mask_ready = sem("mask_ready")

        with nc.Block() as block:

            @block.sync
            def _(sp):
                def load(h, t_slot, x_slot):
                    sp.wait_ge(out_ready, h + 1)
                    sp.dma_start(x_raw[:, x_slot, :],
                                 io["x3"][0:BATCHES, bass.ds(h, 1), :].rearrange("b a c -> b (a c)")
                                 ).then_inc(x_loaded[x_slot], 16)
                    sp.wait_ge(t_ready, h + 1)
                    sp.dma_start(t_raw[:, t_slot, :],
                                 io["toeplitz"][bass.ds(h, 1)].rearrange("a p c -> p (a c)")
                                 ).then_inc(t_loaded[t_slot], 16)

                with sp.Fori(0, STEPS // 4) as i:
                    for n in range(4):
                        load(4 * i + n, n % 2, n)

            @block.gpsimd
            def _(pool):
                pool.iota(iota_l[:], [[1, D]], base=0, channel_multiplier=0,
                          allow_small_or_imprecise_dtypes=True).then_inc(iota_ready, 1)
                pool.sem_inc(t_ready, 2)

                def split(h, par, n):
                    pool.wait_ge(t_loaded[par], 16 * n)
                    pool.wait_ge(y_done, h + 1)
                    pool.sem_inc(pool_passed, 1)
                    pool.tensor_scalar(t_parts[par][0][:], t_raw[:, par, :], 1.0, 0.0, ALU.mult, ALU.add).then_inc(t_hi_ready, 1)
                    pool.wait_ge(t_hi_ready, h + 1)
                    pool.tensor_tensor(t_parts[par][1][:], t_raw[:, par, :], t_parts[par][0][:], ALU.subtract
                                       ).then_inc(t_ready, 1)

                with pool.Fori(0, STEPS // 2) as i:
                    split(2 * i, 0, i + 1)
                    split(2 * i + 1, 1, i + 1)

            @block.scalar
            def _(act):
                def u_hi(h, par):
                    act.wait_ge(turned, h + 1)
                    act.wait_ge(y_done, h + 1)
                    act.copy(u_parts[par][0][:].rearrange("p k b -> p (k b)"), p_u[par][:]
                             ).then_inc(u_hi_ready, 1)

                def store(h, par):
                    act.wait_ge(out_ready, h + 5)
                    act.dma_start(io["out"][:, bass.ds(h, 1), :].rearrange("b a c -> b (a c)"),
                                  out_sb[:, par, :]).then_inc(stored[par], 16)

                for n in range(2):
                    act.sem_inc(stored[n], 16)
                u_hi(0, 0)
                with act.Fori(0, STEPS // 2 - 1) as i:
                    u_hi(2 * i + 1, 1)
                    store(2 * i, 0)
                    u_hi(2 * i + 2, 0)
                    store(2 * i + 1, 1)
                u_hi(STEPS - 1, 1)
                store(STEPS - 2, 0)
                store(STEPS - 1, 1)
                for n in range(2):
                    act.wait_ge(stored[n], 16 * (STEPS // 2 + 1))

            @block.vector
            def _(dve):
                def u_lo(h, par):
                    dve.wait_ge(u_hi_ready, h + 1)
                    dve.tensor_tensor(u_parts[par][1][:].rearrange("p k b -> p (k b)"), p_u[par][:],
                                      u_parts[par][0][:].rearrange("p k b -> p (k b)"), ALU.subtract
                                      ).then_inc(u_ready, 1)

                def finish(h, par, x_slot, n):
                    dve.wait_ge(y_done, h + 3)
                    dve.tensor_tensor(masked[:, par, :], p_y[par][:], mask[:], ALU.mult).then_inc(masked_ready, 1)
                    dve.wait_ge(masked_ready, h + 3)
                    dve.wait_ge(stored[par], 16 * n)
                    x3 = x_raw[:, x_slot, :].rearrange("p (k c) -> p k c", c=P)[:, :, ::-1]
                    dve.tensor_tensor(out_sb[:, par, :].rearrange("p (k c) -> p k c", c=P),
                                      masked[:, par, :].rearrange("p (k c) -> p k c", c=P), x3, ALU.add
                                      ).then_inc(out_ready, 1)

                dve.sem_inc(u_ready, 2)
                dve.sem_inc(masked_ready, 2)
                dve.sem_inc(out_ready, 4)
                dve.wait_ge(iota_ready, 1)
                dve.tensor_scalar(mask[:], iota_l[:], keep["length"][:, 0:1], None, ALU.is_lt
                                  ).then_inc(mask_ready, 1)
                dve.wait_ge(mask_ready, 1)
                u_lo(0, 0)
                with dve.Fori(0, STEPS // 4 - 1) as i:
                    for n in range(4):
                        u_lo(4 * i + n + 1, 1 - n % 2)
                        finish(4 * i + n, n % 2, n, 2 * i + n // 2 + 1)
                for n in range(4):
                    h = STEPS - 4 + n
                    if n < 3:
                        u_lo(h + 1, 1 - n % 2)
                    finish(h, n % 2, n, STEPS // 2 - 2 + n // 2 + 1)

            @block.tensor
            def _(pe):
                def turn(h, par, x_slot, n):
                    pe.wait_ge(x_loaded[x_slot], 16 * n)
                    pe.wait_ge(u_ready, h + 1)
                    for k in range(KB):
                        last = pe.transpose(p_u[par][:, k * P:(k + 1) * P], x_raw[:, x_slot, k * P:(k + 1) * P],
                                            keep["ident"][:])
                    last.then_inc(turned, 1)

                def convolve(h, par):
                    pe.wait_ge(u_ready, h + 3)
                    pe.wait_ge(t_ready, h + 3)
                    pe.wait_ge(masked_ready, h + 1)
                    u_hi, u_lo = u_parts[par]
                    t_hi, t_lo = t_parts[par]
                    for k in range(KB):
                        for w, t in ((u_hi, t_hi), (u_hi, t_lo), (u_lo, t_hi)):
                            for bank in range(k * P // HALF, D // HALF):
                                lo, hi = max(k * P, bank * HALF), (bank + 1) * HALF
                                first = k == 0 and w is u_hi and t is t_hi
                                done = (k + 1) * P == hi if k >= KB // 2 else (bank == 0 and k == KB // 2 - 1)
                                last = pe.matmul(p_y[par][:, lo:hi], w[:, k, :], t[:, lo - k * P:hi - k * P],
                                                 start=first, stop=done and w is u_lo)
                    last.then_inc(y_done, 1)

                pe.sem_inc(y_done, 2)
                turn(0, 0, 0, 1)
                with pe.Fori(0, STEPS // 4 - 1) as i:
                    for n in range(4):
                        turn(4 * i + n + 1, 1 - n % 2, (n + 1) % 4, i + 1 + (n + 1) // 4)
                        convolve(4 * i + n, n % 2)
                for n in range(4):
                    h = STEPS - 4 + n
                    if n < 3:
                        turn(h + 1, 1 - n % 2, n + 1, STEPS // 4)
                    convolve(h, n % 2)


def bass_cond_resid(nc, io, phases=5):
    ctx = ExitStack()
    with ctx:
        def sb(name, shape, dt=F32):
            return ctx.enter_context(nc.sbuf_tensor(name, shape, dt))

        keep = {
            "ident": sb("ident", [P, P]),
            "anti": sb("anti", [P, P]),
            "iota8": sb("iota8", [P, 8]),
            "own2": sb("own2", [P, TB, STEPS], BF16),
            "gate_bias": sb("gate_bias", [P, STEPS, 8], BF16),
            "b1": sb("b1", [P, KB]),
            "length": sb("length", [P, 1]),
            "zero": sb("zero", [P, 1]),
            "adapter": sb("adapter", [1, BATCHES], I32),
            "tbl": sb("tbl", [1, T_WIDTH], I32),
        }
        tables_phase(nc, keep, io)
        if phases > 1:
            products_phase(nc, keep, io)
        if phases > 2:
            layers01_phase(nc, keep, io)
        if phases > 3:
            layer2_phase(nc, keep, io)
        if phases > 4:
            layer3_phase(nc, keep, io)


def kernel(**inputs):
    import numpy as np
    import concourse.bacc as bacc
    from concourse.bass_utils import run_bass_kernel_spmd

    a = {name: np.asarray(value) for name, value in inputs.items()}
    arrays = {
        "xt": a["x"].reshape(TILES, TOK, KB, P).transpose(0, 3, 2, 1),
        "lang": a["itok_B_0_7"].reshape(1, BATCHES),
        "adapter": a["itok_B_0_23"].reshape(1, BATCHES),
        "expert": a["itok_B_3_7"].reshape(BATCHES, 1),
        "length": a["itok_B_78_3631"].reshape(BATCHES, 1),
        "s0": np.concatenate([
            a["L0_cond_W"].reshape(KB, P, KB, P).transpose(2, 1, 0, 3),
            a["L0_cond_B"].transpose(1, 0, 2).reshape(1, KB, P, ER).transpose(0, 2, 1, 3)]),
        "a0": a["L0_cond_A"].reshape(ER, KB, P).transpose(2, 1, 0).reshape(P, KB * ER),
        "wr": a["L0_cond_Wr"].reshape(EXPERTS0, KB, P).transpose(2, 1, 0),
        "w1t": a["L1_cond_W"].T.reshape(KB, P, D),
        "b1": a["L1_cond_b"].reshape(KB, P).T,
        "a1": a["L1_cond_lora_As"].transpose(1, 0, 2).reshape(KB, P, ADAPTERS * RANK),
        "b1r": a["L1_cond_lora_Bs"],
        "w2t": a["L2_cond_weight"].transpose(0, 2, 1).reshape(EXPERTS2, KB, P, KB, P)[..., ::-1]
        .reshape(EXPERTS2, KB, P, D),
        "log_dt": a["L3_cond_log_dt"].reshape(1, STEPS),
        "c": a["L3_cond_C"].transpose(2, 1, 0),
        "log_a": a["L3_cond_log_A_real"].T,
        "a_imag": a["L3_cond_A_imag"].T,
        "d": a["L3_cond_D"].reshape(1, STEPS),
    }
    arrays = {name: np.ascontiguousarray(value) for name, value in arrays.items()}
    nc = bacc.Bacc("TRN2", target_bir_lowering=False, num_devices=1)
    io = {name: nc.dram_tensor(name + "_dram", value.shape, mybir.dt.from_np(value.dtype), kind="ExternalInput").ap()
          for name, value in arrays.items()}
    io["out"] = nc.dram_tensor("out_dram", (BATCHES, STEPS, D), F32, kind="ExternalOutput").ap()
    for name, shape in (("m01", (KB + 1, P, D)), ("pa", (ADAPTERS, P, AW)), ("x2", (BATCHES, P, KB, STEPS)),
                        ("x3", (PLACES, STEPS, D)), ("kpad", (STEPS, KROW))):
        io[name] = nc.dram_tensor(name + "_dram", shape, F32, kind="Internal").ap()
    k = io["kpad"]
    io["toeplitz"] = bass.AP(tensor=k.tensor, offset=0, ap=[[KROW, STEPS], [1, P], [1, D]])
    bass_cond_resid(nc, io)
    r = run_bass_kernel_spmd(nc, [{name + "_dram": value for name, value in arrays.items()}], core_ids=[0])
    return r.results[0]["out_dram"]
```

```python
from contextlib import ExitStack

import concourse.bass as bass
from concourse import mybir

ALU = mybir.AluOpType
ACT = mybir.ActivationFunctionType
AX = mybir.AxisListType
F32 = mybir.dt.float32
F32R = mybir.dt.float32r
I32 = mybir.dt.int32
U32 = mybir.dt.uint32
BF16 = mybir.dt.bfloat16

P = 128
BATCHES, STEPS, D = 128, 64, 1024
KB = D // P
EXPERTS0, RANK = 8, 16
ADAPTERS = 32
ER = EXPERTS0 * RANK
EXPERTS2 = 8
TOK = 512
TILES = BATCHES * STEPS // TOK
TB = TOK // STEPS
SUB = TOK // P
AW = (KB + 1) * RANK
HALF = 512

SLOTS = (BATCHES + EXPERTS2) // 2
PLACES = 2 * SLOTS
T_READ, T_WRITE, T_PAR, T_RANK, T_FREE = 0, 144, 288, 360, 432
T_EXPERT, T_COUNT = 440, 448
T_WIDTH = 449

NS = 64
QN, RN = 32, 32
HT = STEPS // TILES
KROW = 1152
ROUND = 12582912.0
TWO_PI = 6.283185307179586
TWO_PI_HI = 6.28125
TWO_PI_LO = TWO_PI - TWO_PI_HI
LN2_HI = 0.693359375
LN2_LO = -2.12194440054690583e-4


def both(nc, name, shape, ctx):
    return (ctx.enter_context(nc.sbuf_tensor(name + "_hi", shape, F32R)),
            ctx.enter_context(nc.sbuf_tensor(name + "_lo", shape, F32R)))


def scope(nc):
    ctx = ExitStack()

    def sb(name, shape, dt=F32):
        return ctx.enter_context(nc.sbuf_tensor(name, shape, dt))

    def ps(name, shape):
        return ctx.enter_context(nc.psum_tensor(name, shape, F32))

    def sem(name):
        return ctx.enter_context(nc.semaphore(name))

    return ctx, sb, ps, sem


TABLES = 15


def products_phase(nc, keep, io):
    ctx, sb, ps, sem = scope(nc)
    QW = D + ADAPTERS * RANK
    NCH = QW // HALF
    with ctx:
        q_hi, q_lo = both(nc, "q", [P, KB, QW], ctx)
        q_raw = sb("q_raw", [P, 2, QW])
        s_raw = [sb(f"s_raw{i}", [P, KB, P]) for i in range(2)]
        s_parts = [both(nc, f"s{i}", [P, KB, P], ctx) for i in range(2)]
        prod = sb("prod", [P, 2, D])
        pa = sb("pa", [P, ADAPTERS, KB + 1, RANK])
        ones = sb("ones", [P, P])
        before = sb("before", [P, P])
        zrow = sb("zrow", [STEPS, P])
        iota_f = sb("iota_f", [P, 144])
        iota_p = sb("iota_p", [P, 1])
        tri = sb("tri", [P, 8, 8])
        eid_i = sb("eid_i", [P, 1], I32)
        eid = sb("eid", [P, 1])
        lang_i = sb("lang_i", [P, BATCHES], I32)
        lang = sb("lang", [P, BATCHES])
        langs = sb("langs", [P, STEPS])
        len_i = sb("len_i", [P, 1], I32)
        oh = sb("oh", [P, 8])
        cum = sb("cum", [P, 2, 8])
        nslot = sb("nslot", [P, 8])
        cum3 = sb("cum3", [P, 8, 8])
        end = sb("end", [P, 8])
        t8 = sb("t8", [P, 8])
        pos = sb("pos", [P, 1])
        ohp = sb("ohp", [P, PLACES])
        ltp = sb("ltp", [P, PLACES])
        row = sb("row", [1, 6, 144])
        cmp3 = sb("cmp3", [1, SLOTS, 8])
        es = sb("es", [1, 4, SLOTS])
        tf = sb("tf", [1, T_WIDTH])
        used = sb("used", [1, 5, 8])
        rank3 = sb("rank3", [1, 8, 8])
        cmp8 = sb("cmp8", [1, 8, 8])
        adp_i = sb("adp_i", [1, BATCHES], I32)
        ldt = sb("ldt", [P, STEPS])
        aim = sb("aim", [P, STEPS])
        cre = sb("cre", [P, STEPS])
        cim = sb("cim", [P, STEPS])
        lar = sb("lar", [P, STEPS])
        sk = sb("sk", [P, 16, STEPS])
        bits = sb("bits", [P, STEPS], I32)
        co = keep["co"]
        DT, AR, DIM, EM, T0, T1, MAG, SI, CO, NR, NI, IV, SH, T2, T3 = range(15)
        DRE, UF, CR, CI = range(4)
        p_g = [ps(f"p_g{i}", [P, NCH * HALF]) for i in range(2)]
        p_cum = ps("p_cum", [P, HALF])
        p_row = ps("p_row", [P, HALF])

        q_loaded = [sem(f"q_loaded{i}") for i in range(2)]
        s_loaded = [sem(f"s_loaded{i}") for i in range(2)]
        q_diag = sem("q_diag")
        s_diag = sem("s_diag")
        q_hi_ready = sem("q_hi_ready")
        q_ready = sem("q_ready")
        s_hi_ready = sem("s_hi_ready")
        s_ready = sem("s_ready")
        block_done = sem("block_done")
        m_copied = sem("m_copied")
        a_copied = sem("a_copied")
        m_stored = [sem(f"m_stored{i}") for i in range(2)]
        a_stored = sem("a_stored")
        tables_loaded = sem("tables_loaded")
        zeros_ready = sem("zeros_ready")
        zeros_stored = sem("zeros_stored")
        pool_step = sem("pool_step")
        consts_ready = sem("consts_ready")
        dve_step = sem("dve_step")
        onehot_ready = sem("onehot_ready")
        counted = sem("counted")
        places_ready = sem("places_ready")
        placed = sem("placed")
        decay_rates = sem("decay_rates")
        angles_ready = sem("angles_ready")
        sines_ready = sem("sines_ready")

        with nc.Block() as block:

            @block.sync
            def _(sp):
                def load_s(m, par):
                    sp.wait_ge(s_ready, m + 1)
                    sp.dma_start(s_raw[par][:], io["s0"][bass.ds(m, 1)].rearrange("a p j c -> p (a j) c")
                                 ).then_inc(s_loaded[par], 16)

                load_s(0, 0)
                for j in range(KB):
                    if j >= 2:
                        sp.wait_ge(q_ready, j - 1)
                    sp.dma_start(q_raw[:, j % 2, 0:D], io["w1t"][j]).then_inc(q_loaded[j % 2], 16)
                    sp.dma_start(q_raw[:, j % 2, D:QW], io["a1"][j]).then_inc(q_loaded[j % 2], 16)
                    if j == 1:
                        load_s(1, 1)
                halves = [(0, NS), (NS, 2 * NS)]
                for lo, hi in halves:
                    sp.dma_start(lar[lo:hi, :], io["log_a"]).then_inc(tables_loaded, 16)
                    sp.dma_start(aim[lo:hi, :], io["a_imag"]).then_inc(tables_loaded, 16)
                    sp.dma_start(cre[lo:hi, :], io["c"][0]).then_inc(tables_loaded, 16)
                    sp.dma_start(cim[lo:hi, :], io["c"][1]).then_inc(tables_loaded, 16)
                sp.dma_start(ldt[:], io["log_dt"].to_broadcast([P, STEPS])).then_inc(tables_loaded, 16)
                sp.dma_start(lang_i[:], io["lang"].to_broadcast([P, BATCHES])).then_inc(tables_loaded, 16)
                sp.dma_start(eid_i[:], io["expert"]).then_inc(tables_loaded, 16)
                sp.dma_start(len_i[:], io["length"]).then_inc(tables_loaded, 16)
                sp.dma_start(adp_i[:], io["adapter"]).then_inc(tables_loaded, 16)
                sp.dma_start(keep["dskip"][:], io["d"]).then_inc(tables_loaded, 16)
                sp.dma_start(keep["b1"][:], io["b1"]).then_inc(tables_loaded, 16)
                sp.wait_ge(zeros_ready, 1)
                sp.dma_start(io["kpad"][:, 0:P - 1], zrow[:, 0:P - 1]).then_inc(zeros_stored, 16)
                with sp.Fori(1, 4) as i:
                    load_s(2 * i, 0)
                    load_s(2 * i + 1, 1)
                load_s(8, 0)
                sp.wait_ge(a_copied, 2 + KB + 1)
                sp.dma_start(io["pa"].rearrange("s p c -> p s c"), pa[:].rearrange("p s k r -> p s (k r)")
                             ).then_inc(a_stored, 16)
                sp.wait_ge(a_stored, 16)
                sp.wait_ge(zeros_stored, 16)

            @block.gpsimd
            def _(pool):
                n = [0]

                def step(ins):
                    n[0] += 1
                    ins.then_inc(pool_step, 1)
                    pool.wait_ge(pool_step, n[0])

                ident = keep["ident"]
                step(pool.memset(ones[:], 1.0))
                step(pool.affine_select(out=keep["ident"][:], in_=ones[:], pattern=[[-1, P]], base=0,
                                        channel_multiplier=1, compare_op=ALU.is_equal, fill=0.0))

                def diag_s(m, par, n):
                    pool.wait_ge(s_loaded[par], 16 * n)
                    blk = s_raw[par][:, bass.ds(m, 1), :].rearrange("p a c -> p (a c)")
                    pool.tensor_tensor(blk, blk, ident[:], ALU.add).then_inc(s_diag, 1)

                diag_s(0, 0, 1)
                for j in range(KB):
                    pool.wait_ge(q_loaded[j % 2], 32 * (j // 2 + 1))
                    blk = q_raw[:, j % 2, j * P:(j + 1) * P]
                    pool.tensor_tensor(blk, blk, ident[:], ALU.add).then_inc(q_diag, 1)
                diag_s(1, 1, 1)
                pool.memset(zrow[:], 0.0).then_inc(zeros_ready, 1)
                step(pool.memset(keep["zero"][:], 0.0))
                step(pool.memset(keep["off"][0:NS, 0:1], 0.25))
                step(pool.memset(keep["off"][NS:P, 0:1], 0.5))
                step(pool.memset(keep["off"][0:NS, 1:2], 0.25))
                step(pool.memset(keep["off"][NS:P, 1:2], 0.0))
                step(pool.memset(keep["off"][0:NS, 2:3], 0.5))
                step(pool.memset(keep["off"][NS:P, 2:3], 0.25))
                step(pool.iota(iota_f[:], [[1, 144]], base=0, channel_multiplier=0,
                          allow_small_or_imprecise_dtypes=True))
                step(pool.iota(iota_p[:], [[0, 1]], base=0, channel_multiplier=1,
                          allow_small_or_imprecise_dtypes=True))
                step(pool.iota(keep["iota8"][:], [[1, 8]], base=0, channel_multiplier=0,
                          allow_small_or_imprecise_dtypes=True))
                step(pool.iota(keep["lq"][:, 0, :], [[1, 32]], base=0, channel_multiplier=0,
                          allow_small_or_imprecise_dtypes=True))
                step(pool.iota(keep["lq"][:, 1, :], [[RN, 32]], base=0, channel_multiplier=0,
                          allow_small_or_imprecise_dtypes=True))
                step(pool.affine_select(out=keep["anti"][:], in_=ones[:], pattern=[[1, P]], base=1 - P,
                                   channel_multiplier=1, compare_op=ALU.is_equal, fill=0.0))
                step(pool.affine_select(out=before[:], in_=ones[:], pattern=[[1, P]], base=0,
                                   channel_multiplier=-1, compare_op=ALU.is_gt, fill=0.0))
                step(pool.affine_select(out=tri[:], in_=ones[:, 0:64].rearrange("p (a b) -> p a b", a=8),
                                   pattern=[[1, 8], [-1, 8]], base=0, channel_multiplier=0,
                                   compare_op=ALU.is_ge, fill=0.0))
                own = keep["own2"]
                step(pool.memset(own[:], 2.0))
                step(pool.affine_select(out=own[:], in_=own[:], pattern=[[-RANK, TB], [0, STEPS]], base=0,
                                   channel_multiplier=1, compare_op=ALU.is_ge, fill=0.0))
                pool.affine_select(out=own[:], in_=own[:], pattern=[[RANK, TB], [0, STEPS]], base=RANK,
                                   channel_multiplier=-1, compare_op=ALU.is_gt, fill=0.0).then_inc(consts_ready, 1)
                with pool.Fori(1, 4) as i:
                    diag_s(2 * i, 0, i + 1)
                    diag_s(2 * i + 1, 1, i + 1)

            @block.scalar
            def _(act):
                def split_s(m, par, last=False):
                    if last:
                        act.wait_ge(s_loaded[par], 16 * 5)
                    else:
                        act.wait_ge(s_diag, m + 1)
                    act.wait_ge(block_done, m)
                    act.copy(s_parts[par][0][:], s_raw[par][:]).then_inc(s_hi_ready, 1)

                def take_m(m, par, n):
                    act.wait_ge(block_done, m + 2)
                    act.wait_ge(m_stored[par], 16 * n)
                    act.copy(prod[:, par, :], p_g[par][:, 0:D]).then_inc(m_copied, 1)
                    act.wait_ge(m_copied, m + 3)
                    act.dma_start(io["m01"][bass.ds(m, 1)].rearrange("a p c -> p (a c)"), prod[:, par, :]
                                  ).then_inc(m_stored[par], 16)

                act.sem_inc(m_copied, 2)
                act.sem_inc(m_stored[0], 16)
                act.sem_inc(m_stored[1], 16)
                act.wait_ge(s_diag, 1)
                act.copy(s_parts[0][0][:], s_raw[0][:]).then_inc(s_hi_ready, 1)
                for j in range(KB):
                    act.wait_ge(q_diag, j + 1)
                    act.copy(q_hi[:, j, :], q_raw[:, j % 2, :]).then_inc(q_hi_ready, 1)
                for m in range(KB):
                    split_s(m + 1, (m + 1) % 2, last=(m == KB - 1))
                    take_m(m, m % 2, m // 2 + 1)
                    if m == 0:
                        act.wait_ge(tables_loaded, 16 * TABLES)
                        act.wait_ge(consts_ready, 1)
                        act.activation(sk[:, AR, :], lar[:], ACT.Exp, bias=keep["zero"][:]).then_inc(decay_rates, 1)
                    if m == 2:
                        act.wait_ge(angles_ready, 1)
                        zero = keep["zero"][:]
                        act.activation(sk[:, MAG, :], co[:, DRE, :], ACT.Exp, bias=zero).then_inc(sines_ready, 1)
                        act.activation(sk[:, SI, :], co[:, UF, :], ACT.Sin, bias=zero, scale=TWO_PI
                                       ).then_inc(sines_ready, 1)
                        act.activation(sk[:, SH, :], co[:, UF, :], ACT.Sin, bias=zero, scale=TWO_PI / 2
                                       ).then_inc(sines_ready, 1)
                take_m(8, 0, 5)
                act.wait_ge(m_stored[0], 16 * 6)
                act.wait_ge(m_stored[1], 16 * 5)

            @block.vector
            def _(dve):
                def rest_s(m, par):
                    dve.wait_ge(s_hi_ready, m + 1)
                    dve.tensor_tensor(s_parts[par][1][:], s_raw[par][:], s_parts[par][0][:], ALU.subtract
                                      ).then_inc(s_ready, 1)

                def take_a(m, par):
                    dve.wait_ge(block_done, m + 2)
                    dst = pa[:, :, bass.ds(m, 1), :].rearrange("p s a r -> p s (a r)")
                    dve.tensor_copy(dst, p_g[par][:, D:QW].rearrange("p (s r) -> p s r", r=RANK)
                                    ).then_inc(a_copied, 1)

                counts = {}

                def step(ins, signal=dve_step):
                    counts[signal] = counts.get(signal, 0) + 1
                    ins.then_inc(signal, 1)
                    dve.wait_ge(signal, counts[signal])

                def series(a):
                    step(dve.memset(sk[:, EM, :], 1.0))
                    for n in range(9, 1, -1):
                        step(dve.tensor_tensor(sk[:, EM, :], sk[:, EM, :], sk[:, a, :], ALU.mult))
                        step(dve.tensor_scalar(sk[:, EM, :], sk[:, EM, :], 1.0 / n, 1.0, ALU.mult, ALU.add))
                    step(dve.tensor_tensor(sk[:, EM, :], sk[:, EM, :], sk[:, a, :], ALU.mult))

                def batch_experts():
                    step(dve.tensor_copy(eid[:], eid_i[:]))
                    step(dve.tensor_scalar(eid[:], eid[:], 0.0, float(EXPERTS2 - 1), ALU.max, ALU.min))
                    step(dve.tensor_scalar(oh[:], keep["iota8"][:], eid[:, 0:1], None, ALU.is_equal), onehot_ready)

                def batch_places():
                    dve.wait_ge(counted, 1)
                    step(dve.tensor_copy(cum[:, :, :], p_cum[:, 0:16].rearrange("p (a b) -> p a b", a=2)))
                    step(dve.tensor_scalar(nslot[:], cum[:, 1, :], 0.5, 0.25, ALU.mult, ALU.add))
                    step(dve.tensor_scalar(nslot[:], nslot[:], ROUND, ROUND, ALU.add, ALU.subtract))
                    step(dve.tensor_tensor(cum3[:], tri[:], nslot[:, None, :].to_broadcast([P, 8, 8]), ALU.mult))
                    step(dve.tensor_reduce(end[:], cum3[:], AX.X, ALU.add))
                    step(dve.tensor_tensor(t8[:], end[:], nslot[:], ALU.subtract))
                    step(dve.scalar_tensor_tensor(t8[:], t8[:], 2.0, cum[:, 0, :], ALU.mult, ALU.add))
                    step(dve.tensor_tensor(t8[:], t8[:], oh[:], ALU.mult))
                    step(dve.tensor_reduce(pos[:], t8[:], AX.X, ALU.add))
                    step(dve.tensor_scalar(ohp[:], iota_f[:, 0:PLACES], pos[:, 0:1], None, ALU.is_equal))
                    step(dve.tensor_scalar(ltp[:], iota_f[:, 0:PLACES], pos[:, 0:1], None, ALU.is_gt), places_ready)

                def slot_tables():
                    dve.wait_ge(placed, 1)
                    step(dve.tensor_copy(row[:, 0:3, 0:PLACES],
                                         p_row[0:1, 0:3 * PLACES].rearrange("p (a b) -> p a b", a=3)))
                    step(dve.tensor_tensor(row[:, 3, 0:PLACES], iota_f[0:1, 0:PLACES], row[:, 2, 0:PLACES], ALU.subtract))
                    step(dve.tensor_scalar(row[:, 3, 0:PLACES], row[:, 3, 0:PLACES], float(BATCHES), None, ALU.add))
                    step(dve.tensor_scalar(row[:, 4, 0:PLACES], row[:, 1, 0:PLACES], -1.0, 1.0, ALU.mult, ALU.add))
                    step(dve.tensor_tensor(row[:, 3, 0:PLACES], row[:, 3, 0:PLACES], row[:, 4, 0:PLACES], ALU.mult))
                    step(dve.tensor_tensor(row[:, 3, 0:PLACES], row[:, 3, 0:PLACES], row[:, 0, 0:PLACES], ALU.add))
                    step(dve.memset(tf[:], 1.0))
                    step(dve.tensor_copy(tf[:, T_READ:T_READ + PLACES], row[:, 0, 0:PLACES]))
                    step(dve.tensor_copy(tf[:, T_WRITE:T_WRITE + PLACES], row[:, 3, 0:PLACES]))
                    step(dve.tensor_scalar(used[:, 0, :], nslot[0:1, :], 0.5, None, ALU.is_ge))
                    step(dve.tensor_tensor(rank3[:], tri[0:1], used[:, 0, None, :].to_broadcast([1, 8, 8]), ALU.mult))
                    step(dve.tensor_reduce(used[:, 1, :], rank3[:], AX.X, ALU.add))
                    step(dve.tensor_tensor(rank3[:], used[:, 1, None, :].to_broadcast([1, 8, 8]),
                                           iota_f[0:1, 1:9, None].to_broadcast([1, 8, 8]), ALU.is_equal))
                    step(dve.tensor_tensor(rank3[:], rank3[:], used[:, 0, None, :].to_broadcast([1, 8, 8]), ALU.mult))
                    step(dve.tensor_tensor(cmp8[:], rank3[:], iota_f[0:1, None, 0:8].to_broadcast([1, 8, 8]), ALU.mult))
                    step(dve.tensor_reduce(used[:, 2, :], cmp8[:], AX.X, ALU.add))
                    step(dve.tensor_tensor(cmp8[:], rank3[:], end[0:1, None, :].to_broadcast([1, 8, 8]), ALU.mult))
                    step(dve.tensor_reduce(used[:, 3, :], cmp8[:], AX.X, ALU.add))
                    step(dve.tensor_tensor(cmp3[:], iota_f[0:1, 0:SLOTS, None].to_broadcast([1, SLOTS, 8]),
                                           end[0:1, None, :].to_broadcast([1, SLOTS, 8]), ALU.is_ge))
                    step(dve.tensor_tensor(cmp3[:], cmp3[:], used[:, 0, None, :].to_broadcast([1, SLOTS, 8]), ALU.mult))
                    step(dve.tensor_reduce(es[:, 0, :], cmp3[:], AX.X, ALU.add))
                    step(dve.tensor_scalar(used[:, 4, 0:1], used[:, 1, 7:8], -1.0, None, ALU.add))
                    step(dve.tensor_scalar(es[:, 0, :], es[:, 0, :], used[:, 4, 0:1], None, ALU.min))
                    step(dve.tensor_scalar(es[:, 1, :], es[:, 0, :], 0.5, 0.25, ALU.mult, ALU.subtract))
                    step(dve.tensor_scalar(es[:, 1, :], es[:, 1, :], ROUND, ROUND, ALU.add, ALU.subtract))
                    step(dve.scalar_tensor_tensor(tf[:, T_PAR:T_PAR + SLOTS], es[:, 1, :], -2.0, es[:, 0, :],
                                                  ALU.mult, ALU.add))
                    step(dve.tensor_copy(tf[:, T_RANK:T_RANK + SLOTS], es[:, 0, :]))
                    step(dve.tensor_scalar(tf[:, T_FREE + 2:T_FREE + 8], used[:, 3, 0:6], 1.0, None, ALU.add))
                    step(dve.tensor_copy(tf[:, T_EXPERT:T_EXPERT + 8], used[:, 2, :]))
                    step(dve.tensor_copy(tf[:, T_COUNT:T_COUNT + 1], used[:, 1, 7:8]))
                    step(dve.tensor_copy(keep["tbl"][:], tf[:]))

                def gate_biases():
                    step(dve.tensor_scalar(keep["adapter"][:], adp_i[:], 0, ADAPTERS - 1, ALU.max, ALU.min))
                    step(dve.tensor_copy(keep["length"][:], len_i[:]))
                    step(dve.tensor_copy(lang[:], lang_i[:]))
                    lv = lang[:].rearrange("p (s two) -> p s two", two=2)
                    step(dve.tensor_copy(langs[0:STEPS, :], lv[0:STEPS, :, 0]))
                    step(dve.tensor_copy(langs[STEPS:P, :], lv[STEPS:P, :, 1]))
                    gb = keep["gate_bias"]
                    step(dve.tensor_tensor(gb[:], keep["iota8"][:, None, :].to_broadcast([P, STEPS, 8]),
                                           langs[:, :, None].to_broadcast([P, STEPS, 8]), ALU.is_equal))
                    step(dve.tensor_scalar(gb[:], gb[:], 5.0, None, ALU.mult))

                def decays_and_angles():
                    step(dve.tensor_scalar(sk[:, T0, :], ldt[:], 1.4426950408889634, None, ALU.mult))
                    step(dve.tensor_scalar(sk[:, T1, :], sk[:, T0, :], ROUND, ROUND, ALU.add, ALU.subtract))
                    step(dve.scalar_tensor_tensor(sk[:, T0, :], sk[:, T1, :], -LN2_HI, ldt[:], ALU.mult, ALU.add))
                    step(dve.scalar_tensor_tensor(sk[:, T0, :], sk[:, T1, :], -LN2_LO, sk[:, T0, :], ALU.mult, ALU.add))
                    series(T0)
                    step(dve.tensor_scalar(sk[:, T2, :], sk[:, EM, :], 1.0, None, ALU.add))
                    step(dve.tensor_scalar(sk[:, T1, :], sk[:, T1, :], 127.0, 8388608.0, ALU.add, ALU.mult))
                    step(dve.tensor_copy(bits[:], sk[:, T1, :]))
                    step(dve.tensor_tensor(sk[:, DT, :], sk[:, T2, :], bits[:].bitcast(F32), ALU.mult))
                    dve.wait_ge(decay_rates, 1)
                    step(dve.tensor_scalar(sk[:, AR, :], sk[:, AR, :], -1.0, None, ALU.mult))
                    step(dve.tensor_tensor(co[:, DRE, :], sk[:, AR, :], sk[:, DT, :], ALU.mult))
                    step(dve.tensor_tensor(sk[:, DIM, :], aim[:], sk[:, DT, :], ALU.mult))
                    step(dve.tensor_scalar(sk[:, T0, :], sk[:, DIM, :], 1.0 / TWO_PI, None, ALU.mult))
                    step(dve.tensor_scalar(sk[:, T1, :], sk[:, T0, :], ROUND, ROUND, ALU.add, ALU.subtract))
                    step(dve.scalar_tensor_tensor(sk[:, T0, :], sk[:, T1, :], -TWO_PI_HI, sk[:, DIM, :], ALU.mult, ALU.add))
                    step(dve.scalar_tensor_tensor(sk[:, T0, :], sk[:, T1, :], -TWO_PI_LO, sk[:, T0, :], ALU.mult, ALU.add))
                    step(dve.tensor_scalar(co[:, UF, :], sk[:, T0, :], 1.0 / TWO_PI, None, ALU.mult), angles_ready)

                def exp_minus_one():
                    dve.wait_ge(sines_ready, 3)
                    step(dve.tensor_scalar(sk[:, T0, :], co[:, DRE, :], -0.25, None, ALU.max))
                    series(T0)
                    step(dve.tensor_scalar(sk[:, T3, :], co[:, DRE, :], -0.25, None, ALU.is_ge))
                    step(dve.tensor_scalar(sk[:, MAG, :], sk[:, MAG, :], -1.0, None, ALU.add))
                    step(dve.tensor_tensor(sk[:, T1, :], sk[:, EM, :], sk[:, MAG, :], ALU.subtract))
                    step(dve.tensor_tensor(sk[:, T1, :], sk[:, T1, :], sk[:, T3, :], ALU.mult))
                    step(dve.tensor_tensor(sk[:, EM, :], sk[:, MAG, :], sk[:, T1, :], ALU.add))
                    step(dve.tensor_scalar(sk[:, MAG, :], sk[:, EM, :], 1.0, None, ALU.add))
                    step(dve.tensor_tensor(sk[:, T0, :], sk[:, SH, :], sk[:, SH, :], ALU.mult))
                    step(dve.tensor_scalar(sk[:, T0, :], sk[:, T0, :], 2.0, None, ALU.mult))
                    step(dve.tensor_scalar(sk[:, CO, :], sk[:, T0, :], -1.0, 1.0, ALU.mult, ALU.add))
                    step(dve.tensor_tensor(sk[:, NR, :], sk[:, EM, :], sk[:, CO, :], ALU.mult))
                    step(dve.tensor_tensor(sk[:, NR, :], sk[:, NR, :], sk[:, T0, :], ALU.subtract))

                def state_coefficients():
                    step(dve.tensor_tensor(sk[:, NI, :], sk[:, MAG, :], sk[:, SI, :], ALU.mult))
                    step(dve.tensor_tensor(sk[:, T0, :], sk[:, AR, :], sk[:, AR, :], ALU.mult))
                    step(dve.tensor_tensor(sk[:, T1, :], aim[:], aim[:], ALU.mult))
                    step(dve.tensor_tensor(sk[:, T0, :], sk[:, T0, :], sk[:, T1, :], ALU.add))
                    step(dve.tensor_scalar(sk[:, T0, :], sk[:, T0, :], 0.5, None, ALU.mult))
                    step(dve.reciprocal(sk[:, IV, :], sk[:, T0, :]))
                    step(dve.tensor_tensor(sk[:, T0, :], cre[:], sk[:, NR, :], ALU.mult))
                    step(dve.tensor_tensor(sk[:, T1, :], cim[:], sk[:, NI, :], ALU.mult))
                    step(dve.tensor_tensor(sk[:, T0, :], sk[:, T0, :], sk[:, T1, :], ALU.subtract))
                    step(dve.tensor_tensor(sk[:, T1, :], cre[:], sk[:, NI, :], ALU.mult))
                    step(dve.tensor_tensor(sk[:, T2, :], cim[:], sk[:, NR, :], ALU.mult))
                    step(dve.tensor_tensor(sk[:, T1, :], sk[:, T1, :], sk[:, T2, :], ALU.add))
                    step(dve.tensor_tensor(co[:, CR, :], sk[:, T0, :], sk[:, AR, :], ALU.mult))
                    step(dve.tensor_tensor(sk[:, T2, :], sk[:, T1, :], aim[:], ALU.mult))
                    step(dve.tensor_tensor(co[:, CR, :], co[:, CR, :], sk[:, T2, :], ALU.add))
                    step(dve.tensor_tensor(co[:, CR, :], co[:, CR, :], sk[:, IV, :], ALU.mult))
                    step(dve.tensor_tensor(co[:, CI, :], sk[:, T1, :], sk[:, AR, :], ALU.mult))
                    step(dve.tensor_tensor(sk[:, T2, :], sk[:, T0, :], aim[:], ALU.mult))
                    step(dve.tensor_tensor(co[:, CI, :], co[:, CI, :], sk[:, T2, :], ALU.subtract))
                    step(dve.tensor_tensor(co[:, CI, :], co[:, CI, :], sk[:, IV, :], ALU.mult))

                between = {0: [batch_experts], 1: [decays_and_angles], 2: [batch_places], 3: [exp_minus_one],
                           4: [state_coefficients], 5: [gate_biases], 7: [slot_tables]}
                dve.sem_inc(a_copied, 2)
                dve.sem_inc(s_ready, 2)
                rest_s(0, 0)
                for j in range(KB):
                    dve.wait_ge(q_hi_ready, j + 1)
                    dve.tensor_tensor(q_lo[:, j, :], q_raw[:, j % 2, :], q_hi[:, j, :], ALU.subtract
                                      ).then_inc(q_ready, 1)
                for m in range(KB):
                    rest_s(m + 1, (m + 1) % 2)
                    take_a(m, m % 2)
                    if m == 0:
                        dve.wait_ge(tables_loaded, 16 * TABLES)
                        dve.wait_ge(consts_ready, 1)
                    for stage in between.get(m, []):
                        stage()
                take_a(KB, 0)

            @block.tensor
            def _(pe):
                def product(m, par, first=False):
                    pe.wait_ge(s_ready, m + 3)
                    pe.wait_ge(m_copied, m + 1)
                    pe.wait_ge(a_copied, m + 1)
                    hi, lo = s_parts[par]
                    for j in range(KB):
                        if first:
                            pe.wait_ge(q_ready, j + 1)
                        for w, q, start, stop in ((hi, q_hi, j == 0, False), (hi, q_lo, False, False),
                                                  (lo, q_hi, False, j == KB - 1)):
                            for n in range(NCH):
                                last = pe.matmul(p_g[par][:, n * HALF:(n + 1) * HALF], w[:, j, :],
                                                 q[:, j, n * HALF:(n + 1) * HALF], start=start, stop=stop)
                    last.then_inc(block_done, 1)

                pe.sem_inc(block_done, 1)
                product(0, 0, first=True)
                product(1, 1)
                pe.wait_ge(onehot_ready, 1)
                pe.matmul(p_cum[:, 0:8], before[:], oh[:], start=True, stop=True)
                pe.matmul(p_cum[:, 8:16], ones[:], oh[:], start=True, stop=True).then_inc(counted, 1)
                with pe.Fori(1, 4) as i:
                    product(2 * i, 0)
                    product(2 * i + 1, 1)
                pe.wait_ge(places_ready, 1)
                pe.matmul(p_row[0:1, 0:PLACES], iota_p[:], ohp[:], start=True, stop=True)
                pe.matmul(p_row[0:1, PLACES:2 * PLACES], ones[:, 0:1], ohp[:], start=True, stop=True)
                pe.matmul(p_row[0:1, 2 * PLACES:3 * PLACES], ones[:, 0:1], ltp[:], start=True,
                          stop=True).then_inc(placed, 1)
                product(8, 0)


def layers01_phase(nc, keep, io):
    ctx, sb, ps, sem = scope(nc)
    with ctx:
        m_hi, m_lo = both(nc, "m01", [P, KB + 1, D], ctx)
        x_parts = [both(nc, f"x{i}", [P, KB, TOK], ctx) for i in range(2)]
        x_raw = sb("x_raw", [P, 2, TOK])
        a0_hi, a0_lo = both(nc, "a0", [P, KB, P], ctx)
        wr = sb("wr_hi_lo", [P, (KB - 1) * 16 + P], F32R)
        wr_k = wr[:, 0:KB * 16].rearrange("p (k c) -> p k c", c=16)
        pa_raw = sb("pa_raw", [P, TB, AW])
        pa_hi, pa_lo = both(nc, "pa_tile", [P, KB + 1, TB * RANK], ctx)
        w_raw = sb("w_raw", [P, D])
        b_hi, b_lo = both(nc, "b1_tile", [P, D], ctx)
        g_parts = [both(nc, f"g{i}", [P, TOK], ctx) for i in range(2)]
        h1_hi, h1_lo = both(nc, "h1", [P, TOK], ctx)
        scratch = sb("scratch", [P, TOK])
        wr_raw = scratch[:, 0:KB * 8].rearrange("p (k c) -> p k c", c=8)
        h0 = sb("h0", [P, TOK])
        gexp = sb("gexp", [P, SUB, P])
        logits_t = gexp[0:16].rearrange("p s c -> p (s c)")
        x2_out = sb("x2_out", [P, 2, TOK])
        lg = sb("lg", [P, 3, SUB, 8])
        top = sb("top", [P, SUB, 8])
        topi = sb("topi", [P, SUB, 8], U32)
        topf = sb("topf", [P, SUB, 2])
        wt = sb("wt", [P, 5, SUB])

        staged = [w_raw[:], x2_out[:].rearrange("p a n -> p (a n)")]

        turns = sb("turns", [P, 3, HT, QN])
        decay = sb("decay", [P, 2, HT, QN])
        whole = scratch[:, 0:3 * HT * QN].rearrange("p (i h q) -> p i h q", i=3, h=HT)
        acoef = turns[:, 1]
        kout = decay[0:QN, 0]

        p_out = [ps(f"p_out{i}", [P, TOK]) for i in range(4)]
        p_lg = ps("p_lg", [P, TOK])
        p_h0 = ps("p_h0", [P, TOK])
        p_h1 = ps("p_h1", [P, TOK])
        p_gt = ps("p_gt", [P, TOK])

        wr_loaded = sem("wr_loaded")
        w_loaded = [sem(f"w_loaded{i}") for i in range(2)]
        x_loaded = [sem(f"x_loaded{i}") for i in range(2)]
        pa_loaded = sem("pa_loaded")
        b_loaded = sem("b_loaded")
        wr_hi_ready = sem("wr_hi_ready")
        wr_ready = sem("wr_ready")
        w_hi_ready = sem("w_hi_ready")
        w_ready = sem("w_ready")
        x_hi_ready = sem("x_hi_ready")
        x_ready = sem("x_ready")
        pa_hi_ready = sem("pa_hi_ready")
        pa_ready = sem("pa_ready")
        b_hi_ready = sem("b_hi_ready")
        b_ready = sem("b_ready")
        ranks_done = sem("ranks_done")
        out_done = sem("out_done")
        out_copied = sem("out_copied")
        out_stored = [sem(f"out_stored{i}") for i in range(2)]
        logits_done = sem("logits_done")
        logits_copied = sem("logits_copied")
        logits_turned = sem("logits_turned")
        h0_done = sem("h0_done")
        h0_copied = sem("h0_copied")
        gap_ready = sem("gap_ready")
        exp_ready = sem("exp_ready")
        gexp_ready = sem("gexp_ready")
        gates_turned = sem("gates_turned")
        g_product = sem("g_product")
        g_hi_ready = sem("g_hi_ready")
        h1_product = sem("h1_product")
        h1_hi_ready = sem("h1_hi_ready")
        g_ready = sem("g_ready")
        h1_ready = sem("h1_ready")
        dve_step = sem("dve_step01")
        k_phases = sem("k_phases")
        k_waves = sem("k_waves")
        k_coefs = sem("k_coefs")
        k_done = sem("k_done")
        k_ready = sem("k_ready")
        k_stored = sem("k_stored")
        k_free = sem("k_free")
        k_step = sem("k_step")
        k_parts = sem("k_parts")
        k_copied = sem("k_copied")
        dve_passed = sem("dve_passed")
        pe_passed = sem("pe_passed")
        pool_passed = sem("pool_passed01")
        adapter = keep["adapter"]

        with nc.Block() as block:

            @block.sync
            def _(sp):
                def adapters_of(t):
                    return [sp.value_load(adapter[0:1, bass.ds(t * TB + b, 1)], min_val=0,
                                          max_val=ADAPTERS - 1) for b in range(TB)]

                def load_pa(t, slots):
                    sp.wait_ge(pa_ready, t + 1)
                    for b in range(TB):
                        sp.dma_start(pa_raw[:, b, :], io["pa"][bass.ds(slots[b], 1)].rearrange("a p c -> p (a c)")
                                     ).then_inc(pa_loaded, 16)

                def load_b(t, slots):
                    sp.wait_ge(b_ready, t + 1)
                    for b in range(TB):
                        sp.dma_start(w_raw[b * RANK:(b + 1) * RANK, :],
                                     io["b1r"][bass.ds(slots[b], 1)].rearrange("a r c -> (a r) c")
                                     ).then_inc(b_loaded, 16)

                def load_x(t):
                    for k in range(KB):
                        sp.wait_ge(x_ready, t * KB + k + 1)
                        sp.dma_start(x_raw[:, k % 2, :],
                                     io["xt"][bass.ds(t, 1), :, k, :].rearrange("a p n -> p (a n)")
                                     ).then_inc(x_loaded[k % 2], 16)

                sp.dma_start(wr_raw, io["wr"]).then_inc(wr_loaded, 16)
                sp.dma_start(staged[0], io["a0"]).then_inc(w_loaded[0], 16)
                slots = adapters_of(0)
                load_pa(0, slots)
                load_x(0)
                for n in range(1, KB + 2):
                    if n >= 2:
                        sp.wait_ge(w_ready, n - 1)
                    sp.dma_start(staged[n % 2], io["m01"][n - 1]).then_inc(w_loaded[n % 2], 16)
                sp.wait_ge(w_ready, KB + 1)
                load_b(0, slots)
                with sp.Fori(1, TILES) as t:
                    slots = adapters_of(t)
                    load_pa(t, slots)
                    load_x(t)
                    load_b(t, slots)

            @block.gpsimd
            def _(pool):
                pool.sem_inc(pa_ready, 1)
                pool.sem_inc(b_ready, 1)

                def split_pa(t):
                    pool.wait_ge(pa_loaded, 16 * TB * (t + 1))
                    pool.wait_ge(ranks_done, t + 1)
                    raw = pa_raw[:].rearrange("p b (k r) -> p b k r", r=RANK)
                    hi, lo = [part[:].rearrange("p k (b r) -> p b k r", r=RANK) for part in (pa_hi, pa_lo)]
                    pool.sem_inc(pool_passed, 1)
                    pool.tensor_scalar(hi, raw, 1.0, 0.0, ALU.mult, ALU.add).then_inc(pa_hi_ready, 1)
                    pool.wait_ge(pa_hi_ready, t + 1)
                    pool.tensor_tensor(lo, raw, hi, ALU.subtract).then_inc(pa_ready, 1)

                def split_b(t):
                    pool.wait_ge(b_loaded, 16 * TB * (t + 1))
                    pool.wait_ge(out_done, t * KB + KB)
                    pool.sem_inc(pool_passed, 1)
                    pool.tensor_scalar(b_hi[:], w_raw[:], 1.0, 0.0, ALU.mult, ALU.add).then_inc(b_hi_ready, 1)
                    pool.wait_ge(b_hi_ready, t + 1)
                    pool.tensor_tensor(b_lo[:], w_raw[:], b_hi[:], ALU.subtract).then_inc(b_ready, 1)

                def store_k(t):
                    pool.wait_ge(k_ready, t + 1)
                    pool.dma_start(io["kpad"][bass.ds(t * HT, HT), P - 1:P - 1 + D].rearrange(
                        "h (q r) -> q h r", q=QN), kout).then_inc(k_stored, 16)
                    pool.wait_ge(k_stored, 16 * (t + 1))
                    pool.sem_inc(k_free, 1)

                pool.sem_inc(k_free, 1)
                split_pa(0)
                with pool.Fori(0, TILES - 1) as t:
                    split_b(t)
                    split_pa(t + 1)
                    store_k(t)
                split_b(TILES - 1)
                store_k(TILES - 1)

            @block.scalar
            def _(act):
                def x_hi(t, par, chunks):
                    for k in chunks:
                        if k == 0:
                            act.wait_ge(out_done, t * KB)
                        act.wait_ge(x_loaded[k % 2], t * (KB // 2) * 16 + (k // 2 + 1) * 16)
                        act.copy(x_parts[par][0][:, k, :], x_raw[:, k % 2, :]).then_inc(x_hi_ready, 1)

                def gates(t):
                    act.wait_ge(logits_done, t + 1)
                    act.copy(logits_t, p_lg[0:16, :]).then_inc(logits_copied, 1)
                    act.wait_ge(h0_done, t + 1)
                    act.copy(h0[:], p_h0[:]).then_inc(h0_copied, 1)
                    act.wait_ge(gap_ready, t + 1)
                    act.activation(wt[:, 1, :], wt[:, 0, :], ACT.Exp, bias=keep["zero"][:]).then_inc(exp_ready, 1)

                def take(t, o):
                    act.wait_ge(out_done, t * KB + o + KB + 1)
                    act.wait_ge(out_stored[o % 2], t * (KB // 2) * 16 + (o // 2 + 1) * 16)
                    act.activation(x2_out[:, o % 2, :], p_out[o % 4][:], ACT.Identity,
                                   bias=keep["b1"][:, o:o + 1]).then_inc(out_copied, 1)
                    act.wait_ge(out_copied, t * KB + o + 5)
                    act.dma_start(io["x2"][bass.ds(t * TB, TB), :, o, :].rearrange("b p n -> p b n"),
                                  x2_out[:, o % 2, :].rearrange("p (b n) -> p b n", b=TB)
                                  ).then_inc(out_stored[o % 2], 16)

                def waves(t):
                    act.wait_ge(k_phases, t + 1)
                    act.activation(turns[:], turns[:], ACT.Sin, bias=keep["zero"][:], scale=TWO_PI).then_inc(k_waves, 1)
                    act.activation(decay[:], decay[:], ACT.Exp, bias=keep["zero"][:]).then_inc(k_waves, 1)

                def tile(t, par, ahead=True):
                    for o in range(KB):
                        if ahead and o < 2:
                            x_hi(t + 1, 1 - par, range(4 * o, 4 * o + 4))
                        if ahead and o == 3:
                            gates(t + 1)
                        take(t, o)
                        if o == 1:
                            waves(t)

                act.sem_inc(out_copied, 4)
                act.sem_inc(out_stored[0], 16)
                act.sem_inc(out_stored[1], 16)
                act.wait_ge(wr_loaded, 16)
                act.copy(wr_k[:, :, 0:8], wr_raw).then_inc(wr_hi_ready, 1)
                act.wait_ge(w_loaded[0], 16)
                act.copy(a0_hi[:].rearrange("p k c -> p (k c)"), staged[0]).then_inc(w_hi_ready, 1)
                for k in range(KB):
                    act.wait_ge(x_loaded[k % 2], (k // 2 + 1) * 16)
                    act.copy(x_parts[0][0][:, k, :], x_raw[:, k % 2, :]).then_inc(x_hi_ready, 1)
                for n in range(1, KB + 2):
                    act.wait_ge(w_loaded[n % 2], 16 * (n // 2 + 1))
                    act.copy(m_hi[:, n - 1, :], staged[n % 2]).then_inc(w_hi_ready, 1)
                gates(0)
                with act.Fori(0, TILES // 2 - 1) as i:
                    tile(2 * i, 0)
                    tile(2 * i + 1, 1)
                tile(TILES - 2, 0)
                tile(TILES - 1, 1, ahead=False)
                for n in range(2):
                    act.wait_ge(out_stored[n], 16 * (TILES * KB // 2 + 1))

            @block.vector
            def _(dve):
                def x_lo(t, par):
                    for k in range(KB):
                        dve.wait_ge(x_hi_ready, t * KB + k + 1)
                        dve.tensor_tensor(x_parts[par][1][:, k, :], x_raw[:, k % 2, :],
                                          x_parts[par][0][:, k, :], ALU.subtract).then_inc(x_ready, 1)

                GATE_STEPS = 11 + 2 * SUB

                def gates(t):
                    n = [0]

                    def step(ins, signal=None):
                        if signal is not None:
                            ins.then_inc(signal, 1)
                            dve.wait_ge(signal, t + 1)
                        else:
                            n[0] += 1
                            ins.then_inc(dve_step, 1)
                            dve.wait_ge(dve_step, t * GATE_STEPS + n[0])

                    bias = keep["gate_bias"][:, bass.ds(t * SUB, SUB), :]
                    wide = [P, SUB, 8]
                    iota8 = keep["iota8"][:, None, :].to_broadcast(wide)
                    turned = p_gt[:, 0:SUB * 16].rearrange("p (s c) -> p s c", c=16)
                    dve.wait_ge(logits_turned, t + 1)
                    step(dve.tensor_tensor(lg[:, 0], turned[:, :, 8:16], bias, ALU.add))
                    step(dve.tensor_tensor(lg[:, 1], turned[:, :, 0:8], lg[:, 0], ALU.add))
                    for s in range(SUB):
                        dve.sem_inc(dve_passed, 1)
                        step(dve.max(top[:, s, :], lg[:, 1, s, :]))
                        dve.sem_inc(dve_passed, 1)
                        step(dve.max_index(topi[:, s, :], top[:, s, :], lg[:, 1, s, :]))
                    step(dve.tensor_tensor(wt[:, 0, :], top[:, :, 1], top[:, :, 0], ALU.subtract), gap_ready)
                    step(dve.tensor_copy(topf[:], topi[:, :, 0:2]))
                    step(dve.tensor_tensor(lg[:, 0], iota8, topf[:, :, 0:1].to_broadcast(wide), ALU.is_equal))
                    step(dve.tensor_tensor(lg[:, 1], iota8, topf[:, :, 1:2].to_broadcast(wide), ALU.is_equal))
                    dve.wait_ge(exp_ready, t + 1)
                    step(dve.tensor_scalar(wt[:, 2, :], wt[:, 1, :], 1.0, None, ALU.add))
                    step(dve.reciprocal(wt[:, 3, :], wt[:, 2, :]))
                    step(dve.tensor_tensor(wt[:, 4, :], wt[:, 1, :], wt[:, 3, :], ALU.mult))
                    step(dve.tensor_tensor(lg[:, 0], lg[:, 0], wt[:, 3, :, None].to_broadcast(wide), ALU.mult))
                    step(dve.tensor_tensor(lg[:, 1], lg[:, 1], wt[:, 4, :, None].to_broadcast(wide), ALU.mult))
                    step(dve.tensor_tensor(lg[:, 2], lg[:, 0], lg[:, 1], ALU.add))
                    step(dve.tensor_scalar(gexp[:].rearrange("p s (e r) -> p s e r", r=RANK),
                                           lg[:, 2, :, :, None].to_broadcast([P, SUB, 8, RANK]), 2.0, None,
                                           ALU.mult), gexp_ready)
                    assert n[0] == GATE_STEPS, n[0]

                def parts(product, hi, lo, product_ready, hi_ready, ready, t):
                    product.then_inc(product_ready, 1)
                    dve.wait_ge(product_ready, t + 1)
                    dve.tensor_copy(hi, scratch[:]).then_inc(hi_ready, 1)
                    dve.wait_ge(hi_ready, t + 1)
                    dve.tensor_tensor(lo, scratch[:], hi, ALU.subtract).then_inc(ready, 1)
                    dve.wait_ge(ready, t + 1)

                def gated(t, par):
                    dve.wait_ge(gates_turned, t + 1)
                    dve.wait_ge(h0_copied, t + 1)
                    parts(dve.tensor_tensor(scratch[:], p_gt[:], h0[:], ALU.mult), g_parts[par][0][:],
                          g_parts[par][1][:], g_product, g_hi_ready, g_ready, t)

                def ranks1(t):
                    dve.wait_ge(ranks_done, t + 2)
                    dve.wait_ge(out_done, t * KB + KB)
                    parts(dve.tensor_tensor(scratch[:], p_h1[:], keep["own2"][:].rearrange("p b n -> p (b n)"),
                                            ALU.mult), h1_hi[:], h1_lo[:], h1_product, h1_hi_ready, h1_ready, t)

                DRE, UF, CR, CI = range(4)
                K_STEPS = 9
                wide = [P, HT, QN]

                def k_angles(t):
                    co = keep["co"][:, :, bass.ds(t * HT, HT)]
                    dve.wait_ge(k_free, t + 1)
                    for i, which in enumerate((0, 1, 1)):
                        dve.tensor_tensor(turns[:, i], co[:, UF, :, None].to_broadcast(wide),
                                          keep["lq"][:, which, None, :].to_broadcast(wide), ALU.mult
                                          ).then_inc(k_step, 1)
                    for i in range(2):
                        dve.tensor_tensor(decay[:, i], co[:, DRE, :, None].to_broadcast(wide),
                                          keep["lq"][:, i, None, :].to_broadcast(wide), ALU.mult
                                          ).then_inc(k_step, 1)
                    dve.wait_ge(k_step, t * K_STEPS + 5)
                    for i in range(3):
                        dve.tensor_scalar(turns[:, i], turns[:, i], keep["off"][:, i:i + 1], None, ALU.add
                                          ).then_inc(k_step, 1)
                    dve.wait_ge(k_step, t * K_STEPS + 8)
                    dve.tensor_scalar(whole, turns[:], ROUND, ROUND, ALU.add, ALU.subtract).then_inc(k_step, 1)
                    dve.wait_ge(k_step, t * K_STEPS + K_STEPS)
                    dve.tensor_tensor(turns[:], turns[:], whole, ALU.subtract).then_inc(k_phases, 1)

                def k_tables(t):
                    co = keep["co"][:, :, bass.ds(t * HT, HT)]
                    dve.wait_ge(k_waves, 2 * t + 2)
                    for i in range(3):
                        dve.tensor_tensor(turns[:, i], turns[:, i], decay[:, min(i, 1)], ALU.mult
                                          ).then_inc(k_parts, 1)
                    dve.wait_ge(k_parts, t * 5 + 3)
                    for i, part in ((1, CR), (2, CI)):
                        dve.tensor_tensor(turns[:, i], turns[:, i], co[:, part, :, None].to_broadcast(wide),
                                          ALU.mult).then_inc(k_parts, 1)
                    dve.wait_ge(k_parts, t * 5 + 5)
                    dve.tensor_tensor(acoef, turns[:, 1], turns[:, 2], ALU.add).then_inc(k_coefs, 1)

                def k_take(t):
                    dve.wait_ge(k_done, t + 1)
                    dve.tensor_copy(kout, p_lg[0:QN, 0:HT * RN].rearrange(
                        "q (h r) -> q h r", r=RN)).then_inc(k_copied, 1)
                    dve.wait_ge(k_copied, t + 2)
                    dve.tensor_tensor(kout[0:1, :, 0], kout[0:1, :, 0], keep["dskip"][:, bass.ds(t * HT, HT)],
                                      ALU.add).then_inc(k_ready, 1)

                def tile(t, par, ahead=True):
                    ranks1(t)
                    k_angles(t)
                    if ahead:
                        x_lo(t + 1, 1 - par)
                    k_tables(t)
                    if ahead:
                        gates(t + 1)
                    k_take(t)
                    if ahead:
                        gated(t + 1, 1 - par)

                dve.sem_inc(k_copied, 1)
                dve.sem_inc(x_ready, 2)
                dve.wait_ge(wr_hi_ready, 1)
                dve.memset(wr[:, KB * 16:].bitcast(F32), 0.0).then_inc(wr_ready, 1)
                dve.tensor_tensor(wr_k[:, :, 8:16], wr_raw, wr_k[:, :, 0:8], ALU.subtract).then_inc(wr_ready, 1)
                dve.wait_ge(w_hi_ready, 1)
                dve.tensor_tensor(a0_lo[:].rearrange("p k c -> p (k c)"), staged[0],
                                  a0_hi[:].rearrange("p k c -> p (k c)"), ALU.subtract).then_inc(w_ready, 1)
                x_lo(0, 0)
                for n in range(1, KB + 2):
                    dve.wait_ge(w_hi_ready, n + 1)
                    dve.tensor_tensor(m_lo[:, n - 1, :], staged[n % 2], m_hi[:, n - 1, :], ALU.subtract
                                      ).then_inc(w_ready, 1)
                gates(0)
                gated(0, 0)
                with dve.Fori(0, TILES // 2 - 1) as i:
                    tile(2 * i, 0)
                    tile(2 * i + 1, 1)
                tile(TILES - 2, 0)
                tile(TILES - 1, 1, ahead=False)

            @block.tensor
            def _(pe):
                def three(out, w_hi, w_lo, v_hi, v_lo, start=False, stop=False):
                    pe.matmul(out, w_hi, v_hi, start=start, stop=False)
                    pe.matmul(out, w_hi, v_lo, start=False, stop=False)
                    return pe.matmul(out, w_lo, v_hi, start=False, stop=stop)

                def first_products(t, par, first=False):
                    x_hi, x_lo = x_parts[par]
                    pe.wait_ge(x_ready, t * KB + KB + 2)
                    if not first:
                        pe.wait_ge(k_copied, t)
                    for part in (x_hi, x_lo):
                        for k in range(KB):
                            last = pe.matmul(p_lg[:], wr[:, k * 16:k * 16 + P], part[:, k, :],
                                             start=(k == 0 and part is x_hi), stop=(k == KB - 1 and part is x_lo))
                    last.then_inc(logits_done, 1)
                    for k in range(KB):
                        last = three(p_h0[:], a0_hi[:, k, :], a0_lo[:, k, :], x_hi[:, k, :], x_lo[:, k, :],
                                     start=(k == 0), stop=(k == KB - 1))
                    last.then_inc(h0_done, 1)
                    pe.wait_ge(logits_copied, t + 1)
                    pe.sem_inc(pe_passed, 1)
                    for s in range(SUB):
                        last = pe.transpose(p_gt[:, s * 16:s * 16 + 16], logits_t[:, s * P:(s + 1) * P],
                                            keep["ident"][0:16, 0:16])
                    last.then_inc(logits_turned, 1)
                    pe.wait_ge(pa_ready, t + 2)
                    for k in range(KB):
                        three(p_h1[:], pa_hi[:, k, :], pa_lo[:, k, :], x_hi[:, k, :], x_lo[:, k, :],
                              start=(k == 0))

                def kernel_rows(t):
                    pe.wait_ge(k_coefs, t + 1)
                    pe.sem_inc(pe_passed, 1)
                    for h in range(HT):
                        last = pe.matmul(p_lg[0:QN, h * RN:(h + 1) * RN], acoef[:, h, :], turns[:, 0, h, :],
                                         start=True, stop=True)
                    last.then_inc(k_done, 1)

                def turn_gates(t):
                    pe.wait_ge(gexp_ready, t + 1)
                    for s in range(SUB):
                        last = pe.transpose(p_gt[:, s * P:(s + 1) * P], gexp[:, s, :], keep["ident"][:])
                    last.then_inc(gates_turned, 1)

                def last_ranks(t, par):
                    pe.wait_ge(g_ready, t + 1)
                    three(p_h1[:], pa_hi[:, KB, :], pa_lo[:, KB, :], g_parts[par][0][:], g_parts[par][1][:],
                          stop=True).then_inc(ranks_done, 1)

                def tile(t, par, ahead=True):
                    x_hi, x_lo = x_parts[par]
                    for o in range(KB):
                        if ahead and o == 3:
                            first_products(t + 1, 1 - par)
                        if o == 4:
                            kernel_rows(t)
                        if ahead and o == 5:
                            turn_gates(t + 1)
                        if ahead and o == 7:
                            last_ranks(t + 1, 1 - par)
                        cols = slice(o * P, (o + 1) * P)
                        out = p_out[o % 4][:]
                        pe.wait_ge(out_copied, t * KB + o + 1)
                        for k in range(KB):
                            three(out, m_hi[:, k, cols], m_lo[:, k, cols], x_hi[:, k, :], x_lo[:, k, :],
                                  start=(k == 0))
                        three(out, m_hi[:, KB, cols], m_lo[:, KB, cols], g_parts[par][0][:], g_parts[par][1][:])
                        if o == 0:
                            pe.wait_ge(h1_ready, t + 1)
                            pe.wait_ge(b_ready, t + 2)
                        three(out, b_hi[:, cols], b_lo[:, cols], h1_hi[:], h1_lo[:], stop=True
                              ).then_inc(out_done, 1)

                pe.sem_inc(out_done, KB)
                pe.sem_inc(ranks_done, 1)
                pe.wait_ge(wr_ready, 2)
                pe.wait_ge(w_ready, 1)
                first_products(0, 0, first=True)
                turn_gates(0)
                last_ranks(0, 0)
                pe.wait_ge(w_ready, KB + 2)
                with pe.Fori(0, TILES // 2 - 1) as i:
                    tile(2 * i, 0)
                    tile(2 * i + 1, 1)
                tile(TILES - 2, 0)
                tile(TILES - 1, 1, ahead=False)


def layer2_phase(nc, keep, io):
    ctx, sb, ps, sem = scope(nc)
    with ctx:
        w_hi, w_lo = both(nc, "w2", [P, 2, KB, D], ctx)
        w_raw = sb("w2_raw", [P, 4, D])
        x_raw = sb("x2_raw", [P, 2, 2, KB, STEPS])
        x_parts = [both(nc, f"x2_{i}", [P, KB, P], ctx) for i in range(2)]
        x3_out = sb("x3_out", [P, 2, D])
        p_out = [ps(f"p_x3_{i}", [P, 2 * HALF]) for i in range(4)]

        w_loaded = [sem(f"w2_loaded{i}") for i in range(4)]
        w_diag = sem("w2_diag")
        w_hi_ready = sem("w2_hi_ready")
        w_ready = sem("w2_ready")
        w_chunk = sem("w2_chunk")
        x_loaded = [sem(f"x2_loaded{i}") for i in range(2)]
        x_hi_ready = sem("x2_hi_ready")
        x_ready = sem("x2_ready")
        pool_passed = sem("pool_passed2")
        slot_done = sem("slot_done")
        left_copied = sem("left_copied")
        right_copied = sem("right_copied")
        stored = [sem(f"x3_stored{i}") for i in range(2)]
        tbl = keep["tbl"]

        with nc.Block() as block:

            @block.sync
            def _(sp):
                def load(s, par):
                    a, b = [sp.value_load(tbl[0:1, bass.ds(s * 2 + (T_READ + n), 1)], min_val=0,
                                          max_val=BATCHES - 1) for n in range(2)]
                    sp.wait_ge(x_ready, s + 1)
                    for n, batch in enumerate((a, b)):
                        sp.dma_start(x_raw[:, par, n].rearrange("p k n -> p (k n)"),
                                     io["x2"][bass.ds(batch, 1)].rearrange("a p k n -> p (a k n)")
                                     ).then_inc(x_loaded[par], 16)

                with sp.Fori(0, SLOTS // 2) as i:
                    load(2 * i, 0)
                    load(2 * i + 1, 1)

            @block.gpsimd
            def _(pool):
                def expert(u, par):
                    e = pool.value_load(tbl[0:1, bass.ds(u + T_EXPERT, 1)], min_val=0, max_val=EXPERTS2 - 1)
                    free = pool.value_load(tbl[0:1, bass.ds(u + T_FREE, 1)], min_val=1, max_val=SLOTS + 1)

                    def load(k):
                        pool.wait_ge(w_chunk, u * KB + k + 1)
                        pool.dma_start(w_raw[:, k % 4, :],
                                       io["w2t"][bass.ds(e, 1), k].rearrange("a p c -> p (a c)")
                                       ).then_inc(w_loaded[k % 4], 16)

                    for k in range(4):
                        load(k)
                    pool.wait_ge(slot_done, free)
                    for k in range(KB):
                        pool.wait_ge(w_loaded[k % 4], u * 32 + (k // 4 + 1) * 16)
                        raw = w_raw[:, k % 4, :]
                        diag = w_raw[:, k % 4, k * P:(k + 1) * P]
                        pool.tensor_tensor(diag, diag, keep["anti"][:], ALU.add).then_inc(w_diag, 1)
                        pool.wait_ge(w_diag, u * KB + k + 1)
                        pool.sem_inc(pool_passed, 1)
                        pool.tensor_scalar(w_hi[:, par, k, :], raw, 1.0, 0.0, ALU.mult, ALU.add
                                           ).then_inc(w_hi_ready, 1)
                        pool.wait_ge(w_hi_ready, u * KB + k + 1)
                        pool.tensor_tensor(w_lo[:, par, k, :], raw, w_hi[:, par, k, :], ALU.subtract
                                           ).then_inc(w_chunk, 1)
                        if k + 4 < KB:
                            load(k + 4)

                pool.sem_inc(w_chunk, 4)
                count = pool.value_load(tbl[0:1, T_COUNT:T_COUNT + 1], min_val=1, max_val=EXPERTS2)
                with pool.Fori(0, EXPERTS2 // 2) as i:
                    for par in range(2):
                        with pool.If(count > 2 * i + par):
                            expert(2 * i + par, par)

            @block.scalar
            def _(act):
                def x_hi(s, par, n):
                    act.wait_ge(x_loaded[par], n * 32)
                    act.wait_ge(slot_done, s)
                    act.copy(x_parts[par][0][:].rearrange("p k (b n) -> p b k n", b=2), x_raw[:, par]
                             ).then_inc(x_hi_ready, 1)

                def take(s, par, n):
                    a, b = [act.value_load(tbl[0:1, bass.ds(s * 2 + (T_WRITE + m), 1)], min_val=0,
                                           max_val=PLACES - 1) for m in range(2)]
                    act.wait_ge(slot_done, s + 2)
                    act.wait_ge(stored[par], n * 32)
                    act.copy(x3_out[:, par, 0:HALF], p_out[par][:, 0:HALF]).then_inc(left_copied, 1)
                    act.wait_ge(left_copied, s + 5)
                    act.wait_ge(right_copied, s + 5)
                    for m, batch in enumerate((a, b)):
                        act.dma_start(io["x3"][bass.ds(batch, 1)].rearrange("a t c -> (a t) c"),
                                      x3_out[m * STEPS:(m + 1) * STEPS, par, :]).then_inc(stored[par], 16)

                act.sem_inc(left_copied, 4)
                for n in range(2):
                    act.sem_inc(stored[n], 32)
                act.wait_ge(x_loaded[0], 32)
                act.copy(x_parts[0][0][:].rearrange("p k (b n) -> p b k n", b=2), x_raw[:, 0]
                         ).then_inc(x_hi_ready, 1)
                with act.Fori(0, SLOTS // 2 - 1) as i:
                    x_hi(2 * i + 1, 1, i + 1)
                    take(2 * i, 0, i + 1)
                    x_hi(2 * i + 2, 0, i + 2)
                    take(2 * i + 1, 1, i + 1)
                x_hi(SLOTS - 1, 1, SLOTS // 2)
                take(SLOTS - 2, 0, SLOTS // 2)
                take(SLOTS - 1, 1, SLOTS // 2)
                for n in range(2):
                    act.wait_ge(stored[n], 32 * (SLOTS // 2 + 1))

            @block.vector
            def _(dve):
                def x_lo(s, par):
                    dve.wait_ge(x_hi_ready, s + 1)
                    hi, lo = [part[:].rearrange("p k (b n) -> p b k n", b=2) for part in x_parts[par]]
                    dve.tensor_tensor(lo, x_raw[:, par], hi, ALU.subtract).then_inc(x_ready, 1)

                def take(s, par, n):
                    dve.wait_ge(slot_done, s + 2)
                    dve.wait_ge(stored[par], n * 32)
                    dve.tensor_copy(x3_out[:, par, HALF:D], p_out[par][:, HALF:D]).then_inc(right_copied, 1)

                dve.sem_inc(x_ready, 2)
                dve.sem_inc(right_copied, 4)
                x_lo(0, 0)
                with dve.Fori(0, SLOTS // 2 - 1) as i:
                    x_lo(2 * i + 1, 1)
                    take(2 * i, 0, i + 1)
                    x_lo(2 * i + 2, 0)
                    take(2 * i + 1, 1, i + 1)
                x_lo(SLOTS - 1, 1)
                take(SLOTS - 2, 0, SLOTS // 2)
                take(SLOTS - 1, 1, SLOTS // 2)

            @block.tensor
            def _(pe):
                def slot(s, par):
                    wpar = pe.value_load(tbl[0:1, bass.ds(s + T_PAR, 1)], min_val=0, max_val=1)
                    rank = pe.value_load(tbl[0:1, bass.ds(s + T_RANK, 1)], min_val=0, max_val=EXPERTS2 - 1)
                    pe.wait_ge(left_copied, s + 3)
                    pe.wait_ge(right_copied, s + 3)
                    pe.wait_ge(x_ready, s + 3)
                    x_hi, x_lo = x_parts[par]
                    for n in range(2):
                        out = p_out[par][:, n * HALF:(n + 1) * HALF]
                        cols = slice(n * HALF, (n + 1) * HALF)
                        for k in range(KB):
                            if n == 0:
                                pe.wait_ge(w_chunk, rank * KB + (k + 5))
                            hi = w_hi[:, bass.ds(wpar, 1), k, cols].rearrange("p a c -> p (a c)")
                            lo = w_lo[:, bass.ds(wpar, 1), k, cols].rearrange("p a c -> p (a c)")
                            pe.matmul(out, x_hi[:, k, :], hi, start=(k == 0), stop=False)
                            pe.matmul(out, x_hi[:, k, :], lo, start=False, stop=False)
                            last = pe.matmul(out, x_lo[:, k, :], hi, start=False, stop=(k == KB - 1))
                    last.then_inc(slot_done, 1)

                pe.sem_inc(slot_done, 1)
                with pe.Fori(0, SLOTS // 2) as i:
                    slot(2 * i, 0)
                    slot(2 * i + 1, 1)


def layer3_phase(nc, keep, io):
    ctx, sb, ps, sem = scope(nc)
    with ctx:
        t_raw = sb("t_raw", [P, 2, D])
        t_parts = [both(nc, f"t{i}", [P, D], ctx) for i in range(2)]
        x_raw = sb("x3_raw", [P, 4, D])
        u_parts = [both(nc, f"u{i}", [P, KB, P], ctx) for i in range(2)]
        masked = sb("masked", [P, 2, D])
        out_sb = sb("out_sb", [P, 2, D])
        iota_l = sb("iota_l", [P, D])
        mask = sb("mask", [P, D])
        p_u = [ps(f"p_u{i}", [P, KB * P]) for i in range(2)]
        p_y = [ps(f"p_y{i}", [P, D]) for i in range(2)]

        t_loaded = [sem(f"t_loaded{i}") for i in range(2)]
        x_loaded = [sem(f"x3_loaded{i}") for i in range(4)]
        t_hi_ready = sem("t_hi_ready")
        t_ready = sem("t_ready")
        turned = sem("turned")
        u_hi_ready = sem("u_hi_ready")
        u_ready = sem("u_ready")
        pool_passed = sem("pool_passed3")
        y_done = sem("y_done")
        masked_ready = sem("masked_ready")
        out_ready = sem("out_ready")
        stored = [sem(f"out_stored{i}") for i in range(2)]
        iota_ready = sem("iota_ready")
        mask_ready = sem("mask_ready")

        with nc.Block() as block:

            @block.sync
            def _(sp):
                def load(h, t_slot, x_slot):
                    sp.wait_ge(out_ready, h + 1)
                    sp.dma_start(x_raw[:, x_slot, :],
                                 io["x3"][0:BATCHES, bass.ds(h, 1), :].rearrange("b a c -> b (a c)")
                                 ).then_inc(x_loaded[x_slot], 16)
                    sp.wait_ge(t_ready, h + 1)
                    sp.dma_start(t_raw[:, t_slot, :],
                                 io["toeplitz"][bass.ds(h, 1)].rearrange("a p c -> p (a c)")
                                 ).then_inc(t_loaded[t_slot], 16)

                with sp.Fori(0, STEPS // 4) as i:
                    for n in range(4):
                        load(4 * i + n, n % 2, n)

            @block.gpsimd
            def _(pool):
                pool.iota(iota_l[:], [[1, D]], base=0, channel_multiplier=0,
                          allow_small_or_imprecise_dtypes=True).then_inc(iota_ready, 1)
                pool.sem_inc(t_ready, 2)

                def split(h, par, n):
                    pool.wait_ge(t_loaded[par], 16 * n)
                    pool.wait_ge(y_done, h + 1)
                    pool.sem_inc(pool_passed, 1)
                    pool.tensor_scalar(t_parts[par][0][:], t_raw[:, par, :], 1.0, 0.0, ALU.mult, ALU.add).then_inc(t_hi_ready, 1)
                    pool.wait_ge(t_hi_ready, h + 1)
                    pool.tensor_tensor(t_parts[par][1][:], t_raw[:, par, :], t_parts[par][0][:], ALU.subtract
                                       ).then_inc(t_ready, 1)

                with pool.Fori(0, STEPS // 2) as i:
                    split(2 * i, 0, i + 1)
                    split(2 * i + 1, 1, i + 1)

            @block.scalar
            def _(act):
                def u_hi(h, par):
                    act.wait_ge(turned, h + 1)
                    act.wait_ge(y_done, h + 1)
                    act.copy(u_parts[par][0][:].rearrange("p k b -> p (k b)"), p_u[par][:]
                             ).then_inc(u_hi_ready, 1)

                def store(h, par):
                    act.wait_ge(out_ready, h + 5)
                    act.dma_start(io["out"][:, bass.ds(h, 1), :].rearrange("b a c -> b (a c)"),
                                  out_sb[:, par, :]).then_inc(stored[par], 16)

                for n in range(2):
                    act.sem_inc(stored[n], 16)
                u_hi(0, 0)
                with act.Fori(0, STEPS // 2 - 1) as i:
                    u_hi(2 * i + 1, 1)
                    store(2 * i, 0)
                    u_hi(2 * i + 2, 0)
                    store(2 * i + 1, 1)
                u_hi(STEPS - 1, 1)
                store(STEPS - 2, 0)
                store(STEPS - 1, 1)
                for n in range(2):
                    act.wait_ge(stored[n], 16 * (STEPS // 2 + 1))

            @block.vector
            def _(dve):
                def u_lo(h, par):
                    dve.wait_ge(u_hi_ready, h + 1)
                    dve.tensor_tensor(u_parts[par][1][:].rearrange("p k b -> p (k b)"), p_u[par][:],
                                      u_parts[par][0][:].rearrange("p k b -> p (k b)"), ALU.subtract
                                      ).then_inc(u_ready, 1)

                def finish(h, par, x_slot, n):
                    dve.wait_ge(y_done, h + 3)
                    dve.tensor_tensor(masked[:, par, :], p_y[par][:], mask[:], ALU.mult).then_inc(masked_ready, 1)
                    dve.wait_ge(masked_ready, h + 3)
                    dve.wait_ge(stored[par], 16 * n)
                    x3 = x_raw[:, x_slot, :].rearrange("p (k c) -> p k c", c=P)[:, :, ::-1]
                    dve.tensor_tensor(out_sb[:, par, :].rearrange("p (k c) -> p k c", c=P),
                                      masked[:, par, :].rearrange("p (k c) -> p k c", c=P), x3, ALU.add
                                      ).then_inc(out_ready, 1)

                dve.sem_inc(u_ready, 2)
                dve.sem_inc(masked_ready, 2)
                dve.sem_inc(out_ready, 4)
                dve.wait_ge(iota_ready, 1)
                dve.tensor_scalar(mask[:], iota_l[:], keep["length"][:, 0:1], None, ALU.is_lt
                                  ).then_inc(mask_ready, 1)
                dve.wait_ge(mask_ready, 1)
                u_lo(0, 0)
                with dve.Fori(0, STEPS // 4 - 1) as i:
                    for n in range(4):
                        u_lo(4 * i + n + 1, 1 - n % 2)
                        finish(4 * i + n, n % 2, n, 2 * i + n // 2 + 1)
                for n in range(4):
                    h = STEPS - 4 + n
                    if n < 3:
                        u_lo(h + 1, 1 - n % 2)
                    finish(h, n % 2, n, STEPS // 2 - 2 + n // 2 + 1)

            @block.tensor
            def _(pe):
                def turn(h, par, x_slot, n):
                    pe.wait_ge(x_loaded[x_slot], 16 * n)
                    pe.wait_ge(u_ready, h + 1)
                    for k in range(KB):
                        last = pe.transpose(p_u[par][:, k * P:(k + 1) * P], x_raw[:, x_slot, k * P:(k + 1) * P],
                                            keep["ident"][:])
                    last.then_inc(turned, 1)

                def convolve(h, par):
                    pe.wait_ge(u_ready, h + 3)
                    pe.wait_ge(t_ready, h + 3)
                    pe.wait_ge(masked_ready, h + 1)
                    u_hi, u_lo = u_parts[par]
                    t_hi, t_lo = t_parts[par]
                    for k in range(KB):
                        for w, t in ((u_hi, t_hi), (u_hi, t_lo), (u_lo, t_hi)):
                            for bank in range(k * P // HALF, D // HALF):
                                lo, hi = max(k * P, bank * HALF), (bank + 1) * HALF
                                first = k == 0 and w is u_hi and t is t_hi
                                done = (k + 1) * P == hi if k >= KB // 2 else (bank == 0 and k == KB // 2 - 1)
                                last = pe.matmul(p_y[par][:, lo:hi], w[:, k, :], t[:, lo - k * P:hi - k * P],
                                                 start=first, stop=done and w is u_lo)
                    last.then_inc(y_done, 1)

                pe.sem_inc(y_done, 2)
                turn(0, 0, 0, 1)
                with pe.Fori(0, STEPS // 4 - 1) as i:
                    for n in range(4):
                        turn(4 * i + n + 1, 1 - n % 2, (n + 1) % 4, i + 1 + (n + 1) // 4)
                        convolve(4 * i + n, n % 2)
                for n in range(4):
                    h = STEPS - 4 + n
                    if n < 3:
                        turn(h + 1, 1 - n % 2, n + 1, STEPS // 4)
                    convolve(h, n % 2)


def bass_cond_resid(nc, io, phases=5):
    ctx = ExitStack()
    with ctx:
        def sb(name, shape, dt=F32):
            return ctx.enter_context(nc.sbuf_tensor(name, shape, dt))

        keep = {
            "ident": sb("ident", [P, P]),
            "anti": sb("anti", [P, P]),
            "iota8": sb("iota8", [P, 8]),
            "own2": sb("own2", [P, TB, STEPS], BF16),
            "gate_bias": sb("gate_bias", [P, STEPS, 8], BF16),
            "b1": sb("b1", [P, KB]),
            "length": sb("length", [P, 1]),
            "zero": sb("zero", [P, 1]),
            "adapter": sb("adapter", [1, BATCHES], I32),
            "tbl": sb("tbl", [1, T_WIDTH], I32),
            "co": sb("co", [P, 4, STEPS]),
            "lq": sb("lq", [P, 2, QN]),
            "off": sb("off", [P, 3]),
            "dskip": sb("dskip", [1, STEPS]),
        }
        products_phase(nc, keep, io)
        if phases > 2:
            layers01_phase(nc, keep, io)
        if phases > 3:
            layer2_phase(nc, keep, io)
        if phases > 4:
            layer3_phase(nc, keep, io)


def kernel(**inputs):
    import numpy as np
    import concourse.bacc as bacc
    from concourse.bass_utils import run_bass_kernel_spmd

    a = {name: np.asarray(value) for name, value in inputs.items()}
    arrays = {
        "xt": a["x"].reshape(TILES, TOK, KB, P).transpose(0, 3, 2, 1),
        "lang": a["itok_B_0_7"].reshape(1, BATCHES),
        "adapter": a["itok_B_0_23"].reshape(1, BATCHES),
        "expert": a["itok_B_3_7"].reshape(BATCHES, 1),
        "length": a["itok_B_78_3631"].reshape(BATCHES, 1),
        "s0": np.concatenate([
            a["L0_cond_W"].reshape(KB, P, KB, P).transpose(2, 1, 0, 3),
            a["L0_cond_B"].transpose(1, 0, 2).reshape(1, KB, P, ER).transpose(0, 2, 1, 3)]),
        "a0": a["L0_cond_A"].reshape(ER, KB, P).transpose(2, 1, 0).reshape(P, KB * ER),
        "wr": a["L0_cond_Wr"].reshape(EXPERTS0, KB, P).transpose(2, 1, 0),
        "w1t": a["L1_cond_W"].T.reshape(KB, P, D),
        "b1": a["L1_cond_b"].reshape(KB, P).T,
        "a1": a["L1_cond_lora_As"].transpose(1, 0, 2).reshape(KB, P, ADAPTERS * RANK),
        "b1r": a["L1_cond_lora_Bs"],
        "w2t": a["L2_cond_weight"].transpose(0, 2, 1).reshape(EXPERTS2, KB, P, KB, P)[..., ::-1]
        .reshape(EXPERTS2, KB, P, D),
        "log_dt": a["L3_cond_log_dt"].reshape(1, STEPS),
        "c": a["L3_cond_C"].transpose(2, 1, 0),
        "log_a": a["L3_cond_log_A_real"].T,
        "a_imag": a["L3_cond_A_imag"].T,
        "d": a["L3_cond_D"].reshape(1, STEPS),
    }
    arrays = {name: np.ascontiguousarray(value) for name, value in arrays.items()}
    nc = bacc.Bacc("TRN2", target_bir_lowering=False, num_devices=1)
    io = {name: nc.dram_tensor(name + "_dram", value.shape, mybir.dt.from_np(value.dtype), kind="ExternalInput").ap()
          for name, value in arrays.items()}
    io["out"] = nc.dram_tensor("out_dram", (BATCHES, STEPS, D), F32, kind="ExternalOutput").ap()
    for name, shape in (("m01", (KB + 1, P, D)), ("pa", (ADAPTERS, P, AW)), ("x2", (BATCHES, P, KB, STEPS)),
                        ("x3", (PLACES, STEPS, D)), ("kpad", (STEPS, KROW))):
        io[name] = nc.dram_tensor(name + "_dram", shape, F32, kind="Internal").ap()
    k = io["kpad"]
    io["toeplitz"] = bass.AP(tensor=k.tensor, offset=0, ap=[[KROW, STEPS], [1, P], [1, D]])
    bass_cond_resid(nc, io)
    r = run_bass_kernel_spmd(nc, [{name + "_dram": value for name, value in arrays.items()}], core_ids=[0])
    return r.results[0]["out_dram"]
```

```python
from contextlib import ExitStack

import concourse.bass as bass
from concourse import mybir

ALU = mybir.AluOpType
ACT = mybir.ActivationFunctionType
AX = mybir.AxisListType
F32 = mybir.dt.float32
F32R = mybir.dt.float32r
I32 = mybir.dt.int32
U32 = mybir.dt.uint32
BF16 = mybir.dt.bfloat16

P = 128
BATCHES, STEPS, D = 128, 64, 1024
KB = D // P
EXPERTS0, RANK = 8, 16
ADAPTERS = 32
ER = EXPERTS0 * RANK
EXPERTS2 = 8
TOK = 512
TILES = BATCHES * STEPS // TOK
TB = TOK // STEPS
SUB = TOK // P
AW = (KB + 1) * RANK
HALF = 512
FW = EXPERTS0 + ER
TW = FW + TB // 2 * RANK
XK = 2
XC = KB // XK

SLOTS = (BATCHES + EXPERTS2) // 2
PLACES = 2 * SLOTS
T_READ, T_WRITE, T_PAR, T_RANK, T_FREE = 0, 144, 288, 360, 432
T_EXPERT, T_COUNT, T_SLOTS = 440, 448, 449
T_WIDTH = 450
FULL = BATCHES // 2

NS = 64
QN, RN = 32, 32
HT = STEPS // TILES
KROW = 1152
ROUND = 12582912.0
TWO_PI = 6.283185307179586
TWO_PI_HI = 6.28125
TWO_PI_LO = TWO_PI - TWO_PI_HI
LN2_HI = 0.693359375
LN2_LO = -2.12194440054690583e-4


def both(nc, name, shape, ctx):
    return (ctx.enter_context(nc.sbuf_tensor(name + "_hi", shape, F32R)),
            ctx.enter_context(nc.sbuf_tensor(name + "_lo", shape, F32R)))


def raw_under(nc, name, shape):
    size = 4
    for n in shape[1:]:
        size *= n
    return nc.alloc_sbuf_tensor_at(name, shape, F32, offset=nc.sbuf_base - size)


def scope(nc):
    ctx = ExitStack()

    def sb(name, shape, dt=F32):
        return ctx.enter_context(nc.sbuf_tensor(name, shape, dt))

    def ps(name, shape):
        return ctx.enter_context(nc.psum_tensor(name, shape, F32))

    def sem(name):
        return ctx.enter_context(nc.semaphore(name))

    return ctx, sb, ps, sem


TABLES = 15


def products_phase(nc, keep, across, io):
    ctx, sb, ps, sem = scope(nc)
    QW = D + ADAPTERS * RANK
    NCH = QW // HALF
    with ctx:
        s_parts = [both(nc, f"s{i}", [P, KB, P], ctx) for i in range(2)]
        pa = sb("pa", [P, ADAPTERS, KB + 1, RANK])
        prod = sb("prod", [P, 2, D])
        q_hi, q_lo = both(nc, "q", [P, KB, QW], ctx)
        q_raw = raw_under(nc, "q_raw", [P, KB, QW])
        s_raw = [sb(f"s_raw{i}", [P, KB, P]) for i in range(2)]
        ones = sb("ones", [P, P])
        before = sb("before", [P, P])
        zrow = sb("zrow", [STEPS, P])
        iota_f = sb("iota_f", [P, 144])
        iota_p = sb("iota_p", [P, 1])
        tri = sb("tri", [P, 8, 8])
        eid_i = sb("eid_i", [P, 1], I32)
        eid = sb("eid", [P, 1])
        lang_i = sb("lang_i", [P, BATCHES], I32)
        lang = sb("lang", [P, BATCHES])
        langs = sb("langs", [P, STEPS])
        len_i = sb("len_i", [P, 1], I32)
        oh = sb("oh", [P, 8])
        cum = sb("cum", [P, 2, 8])
        nslot = sb("nslot", [P, 8])
        cum3 = sb("cum3", [P, 8, 8])
        end = sb("end", [P, 8])
        t8 = sb("t8", [P, 8])
        pos = sb("pos", [P, 1])
        ohp = sb("ohp", [P, PLACES])
        ltp = sb("ltp", [P, PLACES])
        row = sb("row", [1, 6, 144])
        cmp3 = sb("cmp3", [1, SLOTS, 8])
        es = sb("es", [1, 4, SLOTS])
        tf = sb("tf", [1, T_WIDTH])
        used = sb("used", [1, 5, 8])
        rank3 = sb("rank3", [1, 8, 8])
        cmp8 = sb("cmp8", [1, 8, 8])
        adp_i = sb("adp_i", [1, BATCHES], I32)
        ldt = sb("ldt", [P, STEPS])
        aim = sb("aim", [P, STEPS])
        cre = sb("cre", [P, STEPS])
        cim = sb("cim", [P, STEPS])
        lar = sb("lar", [P, STEPS])
        sk = sb("sk", [P, 16, STEPS])
        bits = sb("bits", [P, STEPS], I32)
        co = keep["co"]
        DT, AR, DIM, EM, T0, T1, MAG, SI, CO, NR, NI, IV, SH, T2, T3 = range(15)
        DRE, UF, CR, CI = range(4)
        p_g = [ps(f"p_g{i}", [P, NCH * HALF]) for i in range(2)]
        p_cum = ps("p_cum", [P, HALF])
        p_row = ps("p_row", [P, HALF])

        q_loaded = [sem(f"q_loaded{j}") for j in range(KB)]
        s_loaded = [sem(f"s_loaded{i}") for i in range(2)]
        q_diag = sem("q_diag")
        s_diag = sem("s_diag")
        q_hi_ready = sem("q_hi_ready")
        q_ready = sem("q_ready")
        s_hi_ready = sem("s_hi_ready")
        s_ready = sem("s_ready")
        block_done = sem("block_done")
        m_copied = sem("m_copied")
        a_copied = sem("a_copied")
        m_stored, a_stored = across["m_stored"], across["a_stored"]
        tables_loaded = sem("tables_loaded")
        zeros_ready = sem("zeros_ready")
        zeros_stored = sem("zeros_stored")
        pool_step = sem("pool_step")
        consts_ready = sem("consts_ready")
        dve_step = sem("dve_step")
        onehot_ready = sem("onehot_ready")
        counted = sem("counted")
        places_ready = sem("places_ready")
        placed = sem("placed")
        decay_rates = sem("decay_rates")
        angles_ready = sem("angles_ready")
        sines_ready = sem("sines_ready")

        with nc.Block() as block:

            @block.sync
            def _(sp):
                def load_s(m, par):
                    sp.wait_ge(s_ready, m + 1)
                    sp.dma_start(s_raw[par][:], io["s0"][bass.ds(m, 1)].rearrange("a p j c -> p (a j) c")
                                 ).then_inc(s_loaded[par], 16)

                load_s(0, 0)
                for j in range(KB):
                    sp.dma_start(q_raw[:, j, 0:D], io["w1t"][j]).then_inc(q_loaded[j], 16)
                    sp.dma_start(q_raw[:, j, D:QW], io["a1"][j]).then_inc(q_loaded[j], 16)
                    if j == 1:
                        load_s(1, 1)
                halves = [(0, NS), (NS, 2 * NS)]
                for lo, hi in halves:
                    sp.dma_start(lar[lo:hi, :], io["log_a"]).then_inc(tables_loaded, 16)
                    sp.dma_start(aim[lo:hi, :], io["a_imag"]).then_inc(tables_loaded, 16)
                    sp.dma_start(cre[lo:hi, :], io["c"][0]).then_inc(tables_loaded, 16)
                    sp.dma_start(cim[lo:hi, :], io["c"][1]).then_inc(tables_loaded, 16)
                sp.dma_start(ldt[:], io["log_dt"].to_broadcast([P, STEPS])).then_inc(tables_loaded, 16)
                sp.dma_start(lang_i[:], io["lang"].to_broadcast([P, BATCHES])).then_inc(tables_loaded, 16)
                sp.dma_start(eid_i[:], io["expert"]).then_inc(tables_loaded, 16)
                sp.dma_start(len_i[:], io["length"]).then_inc(tables_loaded, 16)
                sp.dma_start(adp_i[:], io["adapter"]).then_inc(tables_loaded, 16)
                sp.dma_start(keep["dskip"][:], io["d"]).then_inc(tables_loaded, 16)
                sp.dma_start(keep["b1"][:], io["b1"]).then_inc(tables_loaded, 16)
                sp.wait_ge(zeros_ready, 1)
                sp.dma_start(io["kpad"][:, 0:P - 1], zrow[:, 0:P - 1]).then_inc(zeros_stored, 16)
                with sp.Fori(1, 4) as i:
                    load_s(2 * i, 0)
                    load_s(2 * i + 1, 1)
                load_s(8, 0)
                for c in range(XC):
                    sp.dma_start(across["x0_raw"][:, c * XK:(c + 1) * XK, :],
                                 io["xt"][0, :, c * XK:(c + 1) * XK, :]).then_inc(across["x_loaded"][c], 16)
                for rows, blocks in ((KB, slice(0, KB)), (KB + 1, slice(KB, KB + 1))):
                    sp.wait_ge(a_copied, 2 + rows)
                    sp.dma_start(io["pa"].rearrange("s p (k r) -> p s k r", r=RANK)[:, :, blocks, :],
                                 pa[:, :, blocks, :]).then_inc(a_stored, 16)
                sp.wait_ge(zeros_stored, 16)

            @block.gpsimd
            def _(pool):
                n = [0]

                def step(ins):
                    n[0] += 1
                    ins.then_inc(pool_step, 1)
                    pool.wait_ge(pool_step, n[0])

                ident = keep["ident"]
                step(pool.memset(ones[:], 1.0))
                step(pool.affine_select(out=keep["ident"][:], in_=ones[:], pattern=[[-1, P]], base=0,
                                        channel_multiplier=1, compare_op=ALU.is_equal, fill=0.0))

                def diag_s(m, par, n):
                    pool.wait_ge(s_loaded[par], 16 * n)
                    blk = s_raw[par][:, bass.ds(m, 1), :].rearrange("p a c -> p (a c)")
                    pool.tensor_tensor(blk, blk, ident[:], ALU.add).then_inc(s_diag, 1)

                diag_s(0, 0, 1)
                for j in range(KB):
                    pool.wait_ge(q_loaded[j], 32)
                    blk = q_raw[:, j, j * P:(j + 1) * P]
                    pool.tensor_tensor(blk, blk, ident[:], ALU.add).then_inc(q_diag, 1)
                diag_s(1, 1, 1)
                pool.memset(zrow[:], 0.0).then_inc(zeros_ready, 1)
                step(pool.memset(keep["zero"][:], 0.0))
                step(pool.memset(keep["off"][0:NS, 0:1], 0.25))
                step(pool.memset(keep["off"][NS:P, 0:1], 0.5))
                step(pool.memset(keep["off"][0:NS, 1:2], 0.25))
                step(pool.memset(keep["off"][NS:P, 1:2], 0.0))
                step(pool.memset(keep["off"][0:NS, 2:3], 0.5))
                step(pool.memset(keep["off"][NS:P, 2:3], 0.25))
                step(pool.iota(iota_f[:], [[1, 144]], base=0, channel_multiplier=0,
                          allow_small_or_imprecise_dtypes=True))
                step(pool.iota(iota_p[:], [[0, 1]], base=0, channel_multiplier=1,
                          allow_small_or_imprecise_dtypes=True))
                step(pool.iota(keep["iota8"][:], [[1, 8]], base=0, channel_multiplier=0,
                          allow_small_or_imprecise_dtypes=True))
                step(pool.iota(keep["lq"][:, 0, :], [[1, 32]], base=0, channel_multiplier=0,
                          allow_small_or_imprecise_dtypes=True))
                step(pool.iota(keep["lq"][:, 1, :], [[RN, 32]], base=0, channel_multiplier=0,
                          allow_small_or_imprecise_dtypes=True))
                step(pool.affine_select(out=keep["anti"][:], in_=ones[:], pattern=[[1, P]], base=1 - P,
                                   channel_multiplier=1, compare_op=ALU.is_equal, fill=0.0))
                step(pool.affine_select(out=before[:], in_=ones[:], pattern=[[1, P]], base=0,
                                   channel_multiplier=-1, compare_op=ALU.is_gt, fill=0.0))
                step(pool.affine_select(out=tri[:], in_=ones[:, 0:64].rearrange("p (a b) -> p a b", a=8),
                                   pattern=[[1, 8], [-1, 8]], base=0, channel_multiplier=0,
                                   compare_op=ALU.is_ge, fill=0.0))
                own = keep["own2"]
                step(pool.memset(own[:], 2.0))
                step(pool.affine_select(out=own[:], in_=own[:], pattern=[[-RANK, TB], [0, STEPS]], base=0,
                                   channel_multiplier=1, compare_op=ALU.is_ge, fill=0.0))
                pool.affine_select(out=own[:], in_=own[:], pattern=[[RANK, TB], [0, STEPS]], base=RANK,
                                   channel_multiplier=-1, compare_op=ALU.is_gt, fill=0.0).then_inc(consts_ready, 1)
                with pool.Fori(1, 4) as i:
                    diag_s(2 * i, 0, i + 1)
                    diag_s(2 * i + 1, 1, i + 1)

            @block.scalar
            def _(act):
                def split_s(m, par, last=False):
                    if last:
                        act.wait_ge(s_loaded[par], 16 * 5)
                    else:
                        act.wait_ge(s_diag, m + 1)
                    act.wait_ge(block_done, m)
                    act.copy(s_parts[par][0][:], s_raw[par][:]).then_inc(s_hi_ready, 1)

                def take_m(m, par, n):
                    act.wait_ge(block_done, m + 2)
                    act.wait_ge(m_stored[par], 16 * n)
                    act.copy(prod[:, par, :], p_g[par][:, 0:D]).then_inc(m_copied, 1)
                    act.wait_ge(m_copied, m + 3)
                    act.dma_start(io["m01"][bass.ds(m, 1)].rearrange("a p c -> p (a c)"), prod[:, par, :]
                                  ).then_inc(m_stored[par], 16)

                act.sem_inc(m_copied, 2)
                act.sem_inc(m_stored[0], 16)
                act.sem_inc(m_stored[1], 16)
                act.wait_ge(s_diag, 1)
                act.copy(s_parts[0][0][:], s_raw[0][:]).then_inc(s_hi_ready, 1)
                for j in range(KB):
                    act.wait_ge(q_diag, j + 1)
                    act.copy(q_hi[:, j, :], q_raw[:, j, :]).then_inc(q_hi_ready, 1)
                for m in range(KB):
                    split_s(m + 1, (m + 1) % 2, last=(m == KB - 1))
                    take_m(m, m % 2, m // 2 + 1)
                    if m == 0:
                        act.wait_ge(tables_loaded, 16 * TABLES)
                        act.wait_ge(consts_ready, 1)
                        act.activation(sk[:, AR, :], lar[:], ACT.Exp, bias=keep["zero"][:]).then_inc(decay_rates, 1)
                    if m == 2:
                        act.wait_ge(angles_ready, 1)
                        zero = keep["zero"][:]
                        act.activation(sk[:, MAG, :], co[:, DRE, :], ACT.Exp, bias=zero).then_inc(sines_ready, 1)
                        act.activation(sk[:, SI, :], co[:, UF, :], ACT.Sin, bias=zero, scale=TWO_PI
                                       ).then_inc(sines_ready, 1)
                        act.activation(sk[:, SH, :], co[:, UF, :], ACT.Sin, bias=zero, scale=TWO_PI / 2
                                       ).then_inc(sines_ready, 1)
                take_m(8, 0, 5)

            @block.vector
            def _(dve):
                def rest_s(m, par):
                    dve.wait_ge(s_hi_ready, m + 1)
                    dve.tensor_tensor(s_parts[par][1][:], s_raw[par][:], s_parts[par][0][:], ALU.subtract
                                      ).then_inc(s_ready, 1)

                def take_a(m, par):
                    dve.wait_ge(block_done, m + 2)
                    dst = pa[:, :, bass.ds(m, 1), :].rearrange("p s a r -> p s (a r)")
                    dve.tensor_copy(dst, p_g[par][:, D:QW].rearrange("p (s r) -> p s r", r=RANK)
                                    ).then_inc(a_copied, 1)

                counts = {}

                def step(ins, signal=dve_step):
                    counts[signal] = counts.get(signal, 0) + 1
                    ins.then_inc(signal, 1)
                    dve.wait_ge(signal, counts[signal])

                def series(a):
                    step(dve.memset(sk[:, EM, :], 1.0))
                    for n in range(9, 1, -1):
                        step(dve.tensor_tensor(sk[:, EM, :], sk[:, EM, :], sk[:, a, :], ALU.mult))
                        step(dve.tensor_scalar(sk[:, EM, :], sk[:, EM, :], 1.0 / n, 1.0, ALU.mult, ALU.add))
                    step(dve.tensor_tensor(sk[:, EM, :], sk[:, EM, :], sk[:, a, :], ALU.mult))

                def batch_experts():
                    step(dve.tensor_copy(eid[:], eid_i[:]))
                    step(dve.tensor_scalar(eid[:], eid[:], 0.0, float(EXPERTS2 - 1), ALU.max, ALU.min))
                    step(dve.tensor_scalar(oh[:], keep["iota8"][:], eid[:, 0:1], None, ALU.is_equal), onehot_ready)

                def batch_places():
                    dve.wait_ge(counted, 1)
                    step(dve.tensor_copy(cum[:, :, :], p_cum[:, 0:16].rearrange("p (a b) -> p a b", a=2)))
                    step(dve.tensor_scalar(nslot[:], cum[:, 1, :], 0.5, 0.25, ALU.mult, ALU.add))
                    step(dve.tensor_scalar(nslot[:], nslot[:], ROUND, ROUND, ALU.add, ALU.subtract))
                    step(dve.tensor_tensor(cum3[:], tri[:], nslot[:, None, :].to_broadcast([P, 8, 8]), ALU.mult))
                    step(dve.tensor_reduce(end[:], cum3[:], AX.X, ALU.add))
                    step(dve.tensor_tensor(t8[:], end[:], nslot[:], ALU.subtract))
                    step(dve.scalar_tensor_tensor(t8[:], t8[:], 2.0, cum[:, 0, :], ALU.mult, ALU.add))
                    step(dve.tensor_tensor(t8[:], t8[:], oh[:], ALU.mult))
                    step(dve.tensor_reduce(pos[:], t8[:], AX.X, ALU.add))
                    step(dve.tensor_scalar(ohp[:], iota_f[:, 0:PLACES], pos[:, 0:1], None, ALU.is_equal))
                    step(dve.tensor_scalar(ltp[:], iota_f[:, 0:PLACES], pos[:, 0:1], None, ALU.is_gt), places_ready)

                def slot_tables():
                    dve.wait_ge(placed, 1)
                    step(dve.tensor_copy(row[:, 0:3, 0:PLACES],
                                         p_row[0:1, 0:3 * PLACES].rearrange("p (a b) -> p a b", a=3)))
                    step(dve.tensor_tensor(row[:, 3, 0:PLACES], iota_f[0:1, 0:PLACES], row[:, 2, 0:PLACES], ALU.subtract))
                    step(dve.tensor_scalar(row[:, 3, 0:PLACES], row[:, 3, 0:PLACES], float(BATCHES), None, ALU.add))
                    step(dve.tensor_scalar(row[:, 4, 0:PLACES], row[:, 1, 0:PLACES], -1.0, 1.0, ALU.mult, ALU.add))
                    step(dve.tensor_tensor(row[:, 3, 0:PLACES], row[:, 3, 0:PLACES], row[:, 4, 0:PLACES], ALU.mult))
                    step(dve.tensor_tensor(row[:, 3, 0:PLACES], row[:, 3, 0:PLACES], row[:, 0, 0:PLACES], ALU.add))
                    step(dve.memset(tf[:], 1.0))
                    step(dve.tensor_copy(tf[:, T_READ:T_READ + PLACES], row[:, 0, 0:PLACES]))
                    step(dve.tensor_copy(tf[:, T_WRITE:T_WRITE + PLACES], row[:, 3, 0:PLACES]))
                    step(dve.tensor_scalar(used[:, 0, :], nslot[0:1, :], 0.5, None, ALU.is_ge))
                    step(dve.tensor_tensor(rank3[:], tri[0:1], used[:, 0, None, :].to_broadcast([1, 8, 8]), ALU.mult))
                    step(dve.tensor_reduce(used[:, 1, :], rank3[:], AX.X, ALU.add))
                    step(dve.tensor_tensor(rank3[:], used[:, 1, None, :].to_broadcast([1, 8, 8]),
                                           iota_f[0:1, 1:9, None].to_broadcast([1, 8, 8]), ALU.is_equal))
                    step(dve.tensor_tensor(rank3[:], rank3[:], used[:, 0, None, :].to_broadcast([1, 8, 8]), ALU.mult))
                    step(dve.tensor_tensor(cmp8[:], rank3[:], iota_f[0:1, None, 0:8].to_broadcast([1, 8, 8]), ALU.mult))
                    step(dve.tensor_reduce(used[:, 2, :], cmp8[:], AX.X, ALU.add))
                    step(dve.tensor_tensor(cmp8[:], rank3[:], end[0:1, None, :].to_broadcast([1, 8, 8]), ALU.mult))
                    step(dve.tensor_reduce(used[:, 3, :], cmp8[:], AX.X, ALU.add))
                    step(dve.tensor_tensor(cmp3[:], iota_f[0:1, 0:SLOTS, None].to_broadcast([1, SLOTS, 8]),
                                           end[0:1, None, :].to_broadcast([1, SLOTS, 8]), ALU.is_ge))
                    step(dve.tensor_tensor(cmp3[:], cmp3[:], used[:, 0, None, :].to_broadcast([1, SLOTS, 8]), ALU.mult))
                    step(dve.tensor_reduce(es[:, 0, :], cmp3[:], AX.X, ALU.add))
                    step(dve.tensor_scalar(used[:, 4, 0:1], used[:, 1, 7:8], -1.0, None, ALU.add))
                    step(dve.tensor_scalar(es[:, 0, :], es[:, 0, :], used[:, 4, 0:1], None, ALU.min))
                    step(dve.tensor_scalar(es[:, 1, :], es[:, 0, :], 0.5, 0.25, ALU.mult, ALU.subtract))
                    step(dve.tensor_scalar(es[:, 1, :], es[:, 1, :], ROUND, ROUND, ALU.add, ALU.subtract))
                    step(dve.scalar_tensor_tensor(tf[:, T_PAR:T_PAR + SLOTS], es[:, 1, :], -2.0, es[:, 0, :],
                                                  ALU.mult, ALU.add))
                    step(dve.tensor_copy(tf[:, T_RANK:T_RANK + SLOTS], es[:, 0, :]))
                    step(dve.tensor_scalar(tf[:, T_FREE + 2:T_FREE + 8], used[:, 3, 0:6], 1.0, None, ALU.add))
                    step(dve.tensor_copy(tf[:, T_EXPERT:T_EXPERT + 8], used[:, 2, :]))
                    step(dve.tensor_copy(tf[:, T_COUNT:T_COUNT + 1], used[:, 1, 7:8]))
                    step(dve.tensor_copy(tf[:, T_SLOTS:T_SLOTS + 1], end[0:1, 7:8]))
                    step(dve.tensor_copy(keep["tbl"][:], tf[:]))

                def gate_biases():
                    step(dve.tensor_scalar(keep["adapter"][:], adp_i[:], 0, ADAPTERS - 1, ALU.max, ALU.min))
                    step(dve.tensor_copy(keep["length"][:], len_i[:]))
                    step(dve.tensor_copy(lang[:], lang_i[:]))
                    lv = lang[:].rearrange("p (s two) -> p s two", two=2)
                    step(dve.tensor_copy(langs[0:STEPS, :], lv[0:STEPS, :, 0]))
                    step(dve.tensor_copy(langs[STEPS:P, :], lv[STEPS:P, :, 1]))
                    gb = keep["gate_bias"]
                    step(dve.tensor_tensor(gb[:], keep["iota8"][:, None, :].to_broadcast([P, STEPS, 8]),
                                           langs[:, :, None].to_broadcast([P, STEPS, 8]), ALU.is_equal))
                    step(dve.tensor_scalar(gb[:], gb[:], 5.0, None, ALU.mult))

                def decays_and_angles():
                    step(dve.tensor_scalar(sk[:, T0, :], ldt[:], 1.4426950408889634, None, ALU.mult))
                    step(dve.tensor_scalar(sk[:, T1, :], sk[:, T0, :], ROUND, ROUND, ALU.add, ALU.subtract))
                    step(dve.scalar_tensor_tensor(sk[:, T0, :], sk[:, T1, :], -LN2_HI, ldt[:], ALU.mult, ALU.add))
                    step(dve.scalar_tensor_tensor(sk[:, T0, :], sk[:, T1, :], -LN2_LO, sk[:, T0, :], ALU.mult, ALU.add))
                    series(T0)
                    step(dve.tensor_scalar(sk[:, T2, :], sk[:, EM, :], 1.0, None, ALU.add))
                    step(dve.tensor_scalar(sk[:, T1, :], sk[:, T1, :], 127.0, 8388608.0, ALU.add, ALU.mult))
                    step(dve.tensor_copy(bits[:], sk[:, T1, :]))
                    step(dve.tensor_tensor(sk[:, DT, :], sk[:, T2, :], bits[:].bitcast(F32), ALU.mult))
                    dve.wait_ge(decay_rates, 1)
                    step(dve.tensor_scalar(sk[:, AR, :], sk[:, AR, :], -1.0, None, ALU.mult))
                    step(dve.tensor_tensor(co[:, DRE, :], sk[:, AR, :], sk[:, DT, :], ALU.mult))
                    step(dve.tensor_tensor(sk[:, DIM, :], aim[:], sk[:, DT, :], ALU.mult))
                    step(dve.tensor_scalar(sk[:, T0, :], sk[:, DIM, :], 1.0 / TWO_PI, None, ALU.mult))
                    step(dve.tensor_scalar(sk[:, T1, :], sk[:, T0, :], ROUND, ROUND, ALU.add, ALU.subtract))
                    step(dve.scalar_tensor_tensor(sk[:, T0, :], sk[:, T1, :], -TWO_PI_HI, sk[:, DIM, :], ALU.mult, ALU.add))
                    step(dve.scalar_tensor_tensor(sk[:, T0, :], sk[:, T1, :], -TWO_PI_LO, sk[:, T0, :], ALU.mult, ALU.add))
                    step(dve.tensor_scalar(co[:, UF, :], sk[:, T0, :], 1.0 / TWO_PI, None, ALU.mult), angles_ready)

                def exp_minus_one():
                    dve.wait_ge(sines_ready, 3)
                    step(dve.tensor_scalar(sk[:, T0, :], co[:, DRE, :], -0.25, None, ALU.max))
                    series(T0)
                    step(dve.tensor_scalar(sk[:, T3, :], co[:, DRE, :], -0.25, None, ALU.is_ge))
                    step(dve.tensor_scalar(sk[:, MAG, :], sk[:, MAG, :], -1.0, None, ALU.add))
                    step(dve.tensor_tensor(sk[:, T1, :], sk[:, EM, :], sk[:, MAG, :], ALU.subtract))
                    step(dve.tensor_tensor(sk[:, T1, :], sk[:, T1, :], sk[:, T3, :], ALU.mult))
                    step(dve.tensor_tensor(sk[:, EM, :], sk[:, MAG, :], sk[:, T1, :], ALU.add))
                    step(dve.tensor_scalar(sk[:, MAG, :], sk[:, EM, :], 1.0, None, ALU.add))
                    step(dve.tensor_tensor(sk[:, T0, :], sk[:, SH, :], sk[:, SH, :], ALU.mult))
                    step(dve.tensor_scalar(sk[:, T0, :], sk[:, T0, :], 2.0, None, ALU.mult))
                    step(dve.tensor_scalar(sk[:, CO, :], sk[:, T0, :], -1.0, 1.0, ALU.mult, ALU.add))
                    step(dve.tensor_tensor(sk[:, NR, :], sk[:, EM, :], sk[:, CO, :], ALU.mult))
                    step(dve.tensor_tensor(sk[:, NR, :], sk[:, NR, :], sk[:, T0, :], ALU.subtract))

                def state_coefficients():
                    step(dve.tensor_tensor(sk[:, NI, :], sk[:, MAG, :], sk[:, SI, :], ALU.mult))
                    step(dve.tensor_tensor(sk[:, T0, :], sk[:, AR, :], sk[:, AR, :], ALU.mult))
                    step(dve.tensor_tensor(sk[:, T1, :], aim[:], aim[:], ALU.mult))
                    step(dve.tensor_tensor(sk[:, T0, :], sk[:, T0, :], sk[:, T1, :], ALU.add))
                    step(dve.tensor_scalar(sk[:, T0, :], sk[:, T0, :], 0.5, None, ALU.mult))
                    step(dve.reciprocal(sk[:, IV, :], sk[:, T0, :]))
                    step(dve.tensor_tensor(sk[:, T0, :], cre[:], sk[:, NR, :], ALU.mult))
                    step(dve.tensor_tensor(sk[:, T1, :], cim[:], sk[:, NI, :], ALU.mult))
                    step(dve.tensor_tensor(sk[:, T0, :], sk[:, T0, :], sk[:, T1, :], ALU.subtract))
                    step(dve.tensor_tensor(sk[:, T1, :], cre[:], sk[:, NI, :], ALU.mult))
                    step(dve.tensor_tensor(sk[:, T2, :], cim[:], sk[:, NR, :], ALU.mult))
                    step(dve.tensor_tensor(sk[:, T1, :], sk[:, T1, :], sk[:, T2, :], ALU.add))
                    step(dve.tensor_tensor(co[:, CR, :], sk[:, T0, :], sk[:, AR, :], ALU.mult))
                    step(dve.tensor_tensor(sk[:, T2, :], sk[:, T1, :], aim[:], ALU.mult))
                    step(dve.tensor_tensor(co[:, CR, :], co[:, CR, :], sk[:, T2, :], ALU.add))
                    step(dve.tensor_tensor(co[:, CR, :], co[:, CR, :], sk[:, IV, :], ALU.mult))
                    step(dve.tensor_tensor(co[:, CI, :], sk[:, T1, :], sk[:, AR, :], ALU.mult))
                    step(dve.tensor_tensor(sk[:, T2, :], sk[:, T0, :], aim[:], ALU.mult))
                    step(dve.tensor_tensor(co[:, CI, :], co[:, CI, :], sk[:, T2, :], ALU.subtract))
                    step(dve.tensor_tensor(co[:, CI, :], co[:, CI, :], sk[:, IV, :], ALU.mult))

                between = {0: [batch_experts], 1: [decays_and_angles], 2: [batch_places], 3: [exp_minus_one],
                           4: [state_coefficients], 5: [gate_biases], 7: [slot_tables]}
                dve.sem_inc(a_copied, 2)
                dve.sem_inc(s_ready, 2)
                rest_s(0, 0)
                for j in range(KB):
                    dve.wait_ge(q_hi_ready, j + 1)
                    dve.tensor_tensor(q_lo[:, j, :], q_raw[:, j, :], q_hi[:, j, :], ALU.subtract
                                      ).then_inc(q_ready, 1)
                for m in range(KB):
                    rest_s(m + 1, (m + 1) % 2)
                    take_a(m, m % 2)
                    if m == 0:
                        dve.wait_ge(tables_loaded, 16 * TABLES)
                        dve.wait_ge(consts_ready, 1)
                    for stage in between.get(m, []):
                        stage()
                take_a(KB, 0)

            @block.tensor
            def _(pe):
                def product(m, par, first=False):
                    pe.wait_ge(s_ready, m + 3)
                    pe.wait_ge(m_copied, m + 1)
                    pe.wait_ge(a_copied, m + 1)
                    hi, lo = s_parts[par]
                    for j in range(KB):
                        if first:
                            pe.wait_ge(q_ready, j + 1)
                        for w, q, start, stop in ((hi, q_hi, j == 0, False), (hi, q_lo, False, False),
                                                  (lo, q_hi, False, j == KB - 1)):
                            for n in range(NCH):
                                last = pe.matmul(p_g[par][:, n * HALF:(n + 1) * HALF], w[:, j, :],
                                                 q[:, j, n * HALF:(n + 1) * HALF], start=start, stop=stop)
                    last.then_inc(block_done, 1)

                pe.sem_inc(block_done, 1)
                product(0, 0, first=True)
                product(1, 1)
                pe.wait_ge(onehot_ready, 1)
                pe.matmul(p_cum[:, 0:8], before[:], oh[:], start=True, stop=True)
                pe.matmul(p_cum[:, 8:16], ones[:], oh[:], start=True, stop=True).then_inc(counted, 1)
                with pe.Fori(1, 4) as i:
                    product(2 * i, 0)
                    product(2 * i + 1, 1)
                pe.wait_ge(places_ready, 1)
                pe.matmul(p_row[0:1, 0:PLACES], iota_p[:], ohp[:], start=True, stop=True)
                pe.matmul(p_row[0:1, PLACES:2 * PLACES], ones[:, 0:1], ohp[:], start=True, stop=True)
                pe.matmul(p_row[0:1, 2 * PLACES:3 * PLACES], ones[:, 0:1], ltp[:], start=True,
                          stop=True).then_inc(placed, 1)
                product(8, 0)


def layers01_phase(nc, keep, across, io):
    ctx, sb, ps, sem = scope(nc)
    with ctx:
        x_parts = [(sb("x0_hi", [P, KB, TOK], F32R), across["x0_lo"])]
        m_hi, m_lo = both(nc, "m01", [P, KB + 1, D], ctx)
        m_raw = raw_under(nc, "m01_raw", [P, KB + 1, D])
        x_parts.append(both(nc, "x1", [P, KB, TOK], ctx))
        x_raw = [across["x0_raw"], raw_under(nc, "x1_raw", [P, KB, TOK])]
        by_token = sb("by_token", [P, 2, KB, 2, TW], F32R)
        by_token_raw = raw_under(nc, "by_token_raw", [P, 2, KB, 2, TW])
        pa_raw = sb("pa_raw", [P, TB // 2, AW])
        ba_hi, ba_lo = both(nc, "ba_tile", [P, TB * RANK], ctx)
        w_raw = sb("w_raw", [P, D])
        b_hi, b_lo = both(nc, "b1_tile", [P, D], ctx)
        g_parts = [both(nc, f"g{i}", [P, TOK], ctx) for i in range(2)]
        h1_hi, h1_lo = both(nc, "h1", [P, TOK], ctx)
        ranks0 = sb("ranks0", [P, SUB, FW])
        scratch = ranks0[:].rearrange("p s c -> p (s c)")[:, 0:TOK]
        ranks1_by_token = sb("ranks1_by_token", [P, SUB, P])
        with_lo = sb("with_lo", [P, TW])
        x2_out = sb("x2_out", [P, 2, TOK])
        lg = sb("lg", [P, 3, SUB, 8])
        top = sb("top", [P, SUB, 8])
        topi = sb("topi", [P, SUB, 8], U32)
        topf = sb("topf", [P, SUB, 2])
        wt = sb("wt", [P, 5, SUB])

        turns = sb("turns", [P, 3, HT, QN])
        decay = sb("decay", [P, 2, HT, QN])
        whole = scratch[:, 0:3 * HT * QN].rearrange("p (i h q) -> p i h q", i=3, h=HT)
        acoef = turns[:, 1]
        kout = decay[0:QN, 0]

        p_out = [ps(f"p_out{i}", [P, TOK]) for i in range(4)]
        p_tok = [ps(f"p_tok{i}", [P, TOK]) for i in range(2)]
        p_h1 = ps("p_h1", [P, TOK])
        p_gt = ps("p_gt", [P, TOK])

        fixed_loaded = sem("fixed_loaded")
        m_loaded = [sem(f"m_loaded{n}") for n in range(KB + 1)]
        x_loaded = across["x_loaded"]
        pa_loaded = sem("pa_loaded")
        b_loaded = sem("b_loaded")
        fixed_hi_ready = sem("fixed_hi_ready")
        fixed_ready = sem("fixed_ready")
        m_hi_ready = sem("m_hi_ready")
        m_ready = sem("m_ready")
        zeros_ready = sem("rank_zeros_ready")
        x_hi_ready = sem("x_hi_ready")
        x_ready = sem("x_ready")
        pa_hi_ready = sem("pa_hi_ready")
        pa_ready = sem("pa_ready")
        b_hi_ready = sem("b_hi_ready")
        b_ready = sem("b_ready")
        ranks_done = sem("ranks_done")
        out_done = sem("out_done")
        out_copied = sem("out_copied")
        out_stored = [sem(f"out_stored{i}") for i in range(2)]
        tok_done = sem("tok_done")
        lo_copied = sem("lo_copied")
        tok_taken = sem("tok_taken")
        gap_ready = sem("gap_ready")
        exp_ready = sem("exp_ready")
        gexp_ready = sem("gexp_ready")
        gates_turned = sem("gates_turned")
        g_hi_ready = sem("g_hi_ready")
        h1_product = sem("h1_product")
        h1_hi_ready = sem("h1_hi_ready")
        g_ready = sem("g_ready")
        h1_ready = sem("h1_ready")
        dve_step = sem("dve_step01")
        k_phases = sem("k_phases")
        k_waves = sem("k_waves")
        k_coefs = sem("k_coefs")
        k_done = sem("k_done")
        k_ready = sem("k_ready")
        k_stored = sem("k_stored")
        k_free = sem("k_free")
        k_step = sem("k_step")
        k_parts = sem("k_parts")
        k_copied = sem("k_copied")
        dve_passed = sem("dve_passed")
        pe_passed = sem("pe_passed")
        pool_passed = sem("pool_passed01")
        adapter = keep["adapter"]
        fixed = by_token[:, :, :, :, 0:FW].rearrange("p a k h c -> p (a k) h c")

        fixed_raw = by_token_raw[:, :, :, 1, 0:FW].rearrange("p a k c -> p (a k) c")

        def x_chunk(par, part, c):
            return x_parts[par][part][:, c * XK:(c + 1) * XK, :]

        first_pa_raw = [pa_raw[:], w_raw[:, 0:TB // 2 * AW].rearrange("p (b c) -> p b c", c=AW)]

        def raw_chunk(par, c):
            return x_raw[par][:, c * XK:(c + 1) * XK, :]


        with nc.Block() as block:

            @block.sync
            def _(sp):
                def adapters_of(t):
                    return [sp.value_load(adapter[0:1, bass.ds(t * TB + b, 1)], min_val=0,
                                          max_val=ADAPTERS - 1) for b in range(TB)]

                def load_pa(t, slots):
                    for half in range(2):
                        sp.wait_ge(pa_ready, t * 4 + (2 * half + 2))
                        for b in range(TB // 2):
                            sp.dma_start(pa_raw[:, b, :],
                                         io["pa"][bass.ds(slots[half * TB // 2 + b], 1)].rearrange("a p c -> p (a c)")
                                         ).then_inc(pa_loaded, 16)

                def load_b(t, slots):
                    sp.wait_ge(b_ready, t + 1)
                    for b in range(TB):
                        sp.dma_start(w_raw[b * RANK:(b + 1) * RANK, :],
                                     io["b1r"][bass.ds(slots[b], 1)].rearrange("a r c -> (a r) c")
                                     ).then_inc(b_loaded, 16)

                def load_x(t, par):
                    sp.wait_ge(out_done, t * KB)
                    for c in range(XC):
                        sp.dma_start(raw_chunk(par, c),
                                     io["xt"][bass.ds(t, 1), :, c * XK:(c + 1) * XK, :].rearrange("a p k n -> p (a k) n")
                                     ).then_inc(x_loaded[c], 16)

                for half in range(2):
                    sp.dma_start(by_token_raw[:, half, :, 1, 0:FW], io["fixed"]).then_inc(fixed_loaded, 16)
                slots = adapters_of(0)
                sp.wait_ge(across["a_stored"], 32)
                for b in range(TB):
                    sp.dma_start(first_pa_raw[b // 4][:, b % 4, :],
                                 io["pa"][bass.ds(slots[b], 1)].rearrange("a p c -> p (a c)")).then_inc(pa_loaded, 16)
                sp.wait_ge(across["m_stored"][0], 16 * 6)
                sp.wait_ge(across["m_stored"][1], 16 * 5)
                for n in range(KB + 1):
                    sp.dma_start(m_raw[:, n, :], io["m01"][n]).then_inc(m_loaded[n], 16)

                sp.wait_ge(pa_ready, 6)
                load_b(0, slots)

                def ahead(t, par):
                    slots = adapters_of(t)
                    load_pa(t, slots)
                    load_x(t, par)
                    load_b(t, slots)

                with sp.Fori(0, TILES // 2 - 1) as i:
                    ahead(2 * i + 1, 1)
                    ahead(2 * i + 2, 0)
                ahead(TILES - 1, 1)
                sp.wait_ge(out_done, TILES * KB)
                first = sp.value_load(keep["tbl"][0:1, T_EXPERT:T_EXPERT + 1], min_val=0, max_val=EXPERTS2 - 1)
                for k in range(KB):
                    sp.dma_start(across["w2_raw"][:, k, :], io["w2t"][bass.ds(first, 1), k].rearrange("a p c -> p (a c)")
                                 ).then_inc(across["w2_loaded"][k], 16)

            @block.gpsimd
            def _(pool):
                pool.sem_inc(pa_ready, 2)
                pool.sem_inc(b_ready, 1)

                def split_pa(t, first=False):
                    for half in range(2):
                        batches = TB if first else TB // 2 * (half + 1)
                        pool.wait_ge(pa_loaded, t * (TB * 16) + 16 * batches)
                        pool.wait_ge(ranks_done, t + 1)
                        raw = (first_pa_raw[half] if first else pa_raw[:]).rearrange("p b (k r) -> p b k r", r=RANK)
                        hi, lo = [by_token[:, half, :, part, FW:TW].rearrange("p k (b r) -> p b k r", r=RANK)
                                  for part in range(2)]
                        cols = slice(half * TB // 2 * RANK, (half + 1) * TB // 2 * RANK)
                        last_hi, last_lo = [part[:, cols].rearrange("p (b r) -> p b r", r=RANK)
                                            for part in (ba_hi, ba_lo)]
                        pool.sem_inc(pool_passed, 1)
                        pool.tensor_scalar(hi, raw[:, :, 0:KB, :], 1.0, 0.0, ALU.mult, ALU.add
                                           ).then_inc(pa_hi_ready, 1)
                        pool.tensor_scalar(last_hi, raw[:, :, KB, :], 1.0, 0.0, ALU.mult, ALU.add
                                           ).then_inc(pa_hi_ready, 1)
                        pool.wait_ge(pa_hi_ready, t * 4 + (2 * half + 2))
                        pool.tensor_tensor(lo, raw[:, :, 0:KB, :], hi, ALU.subtract).then_inc(pa_ready, 1)
                        pool.tensor_tensor(last_lo, raw[:, :, KB, :], last_hi, ALU.subtract).then_inc(pa_ready, 1)

                def split_b(t):
                    pool.wait_ge(b_loaded, 16 * TB * (t + 1))
                    pool.wait_ge(out_done, t * KB + KB)
                    pool.sem_inc(pool_passed, 1)
                    pool.tensor_scalar(b_hi[:], w_raw[:], 1.0, 0.0, ALU.mult, ALU.add).then_inc(b_hi_ready, 1)
                    pool.wait_ge(b_hi_ready, t + 1)
                    pool.tensor_tensor(b_lo[:], w_raw[:], b_hi[:], ALU.subtract).then_inc(b_ready, 1)

                def store_k(t):
                    pool.wait_ge(k_ready, t + 1)
                    pool.dma_start(io["kpad"][bass.ds(t * HT, HT), P - 1:P - 1 + D].rearrange(
                        "h (q r) -> q h r", q=QN), kout).then_inc(k_stored, 16)
                    pool.wait_ge(k_stored, 16 * (t + 1))
                    pool.sem_inc(k_free, 1)

                pool.sem_inc(k_free, 1)
                split_pa(0, first=True)
                with pool.Fori(0, TILES - 1) as t:
                    split_b(t)
                    split_pa(t + 1)
                    store_k(t)
                split_b(TILES - 1)
                store_k(TILES - 1)

            @block.scalar
            def _(act):
                def x_hi(t, par, chunks):
                    for c in chunks:
                        act.wait_ge(x_loaded[c], t * 16 + 16)
                        act.copy(x_chunk(par, 0, c), raw_chunk(par, c)).then_inc(x_hi_ready, 1)

                def m_hi_parts(blocks):
                    for n in blocks:
                        act.wait_ge(m_loaded[n], 16)
                        act.copy(m_hi[:, n, :], m_raw[:, n, :]).then_inc(m_hi_ready, 1)

                def gates(t, first=False):
                    for s in range(SUB):
                        act.wait_ge(tok_done, t * SUB + s + 1)
                        act.wait_ge(tok_taken, t * (2 * SUB) + (2 * s + 4))
                        act.copy(with_lo[:], p_tok[s % 2][:, TW:2 * TW]).then_inc(lo_copied, 1)
                        if first:
                            m_hi_parts(range(2 * s, 2 * s + 2))
                    act.wait_ge(gap_ready, t + 1)
                    act.activation(wt[:, 1, :], wt[:, 0, :], ACT.Exp, bias=keep["zero"][:]).then_inc(exp_ready, 1)

                def take(t, o):
                    act.wait_ge(out_done, t * KB + o + KB + 1)
                    act.wait_ge(out_stored[o % 2], t * (KB // 2) * 16 + (o // 2 + 1) * 16)
                    act.activation(x2_out[:, o % 2, :], p_out[o % 4][:], ACT.Identity,
                                   bias=keep["b1"][:, o:o + 1]).then_inc(out_copied, 1)
                    act.wait_ge(out_copied, t * KB + o + 5)
                    act.dma_start(io["x2"][bass.ds(t * TB, TB), :, o, :].rearrange("b p n -> p b n"),
                                  x2_out[:, o % 2, :].rearrange("p (b n) -> p b n", b=TB)
                                  ).then_inc(out_stored[o % 2], 16)

                def waves(t):
                    act.wait_ge(k_phases, t + 1)
                    act.activation(turns[:], turns[:], ACT.Sin, bias=keep["zero"][:], scale=TWO_PI).then_inc(k_waves, 1)
                    act.activation(decay[:], decay[:], ACT.Exp, bias=keep["zero"][:]).then_inc(k_waves, 1)

                def tile(t, par, ahead=True):
                    for o in range(KB):
                        if ahead and o < 2:
                            x_hi(t + 1, 1 - par, range(o * XC // 2, (o + 1) * XC // 2))
                        if ahead and o == 3:
                            gates(t + 1)
                        take(t, o)
                        if o == 3:
                            waves(t)

                act.sem_inc(out_copied, 4)
                act.sem_inc(out_stored[0], 16)
                act.sem_inc(out_stored[1], 16)
                x_hi(0, 0, range(XC))
                act.wait_ge(fixed_loaded, 32)
                act.copy(fixed[:, :, 0], fixed_raw).then_inc(fixed_hi_ready, 1)
                gates(0, first=True)
                m_hi_parts([KB])
                with act.Fori(0, TILES // 2 - 1) as i:
                    tile(2 * i, 0)
                    tile(2 * i + 1, 1)
                tile(TILES - 2, 0)
                tile(TILES - 1, 1, ahead=False)
                for n in range(2):
                    act.wait_ge(out_stored[n], 16 * (TILES * KB // 2 + 1))

            @block.vector
            def _(dve):
                def x_lo(t, par):
                    for c in range(XC):
                        dve.wait_ge(x_hi_ready, t * XC + c + 1)
                        dve.tensor_tensor(x_chunk(par, 1, c), raw_chunk(par, c), x_chunk(par, 0, c),
                                          ALU.subtract).then_inc(x_ready, 1)

                def m_lo_parts(blocks):
                    for n in blocks:
                        dve.wait_ge(m_hi_ready, n + 1)
                        dve.tensor_tensor(m_lo[:, n, :], m_raw[:, n, :], m_hi[:, n, :], ALU.subtract
                                          ).then_inc(m_ready, 1)

                def take_tokens(t, first=False):
                    for s in range(SUB):
                        dve.wait_ge(lo_copied, t * SUB + s + 1)
                        bank = p_tok[s % 2]
                        half = s * 2 // SUB
                        dve.tensor_tensor(ranks0[:, s, :], bank[:, 0:FW], with_lo[:, 0:FW], ALU.add
                                          ).then_inc(tok_taken, 1)
                        dve.tensor_tensor(ranks1_by_token[:, s, half * 64:(half + 1) * 64], bank[:, FW:TW],
                                          with_lo[:, FW:TW], ALU.add).then_inc(tok_taken, 1)
                        if first:
                            m_lo_parts(range(2 * s, 2 * s + 2))
                    dve.wait_ge(tok_taken, t * (2 * SUB) + 2 * SUB + 4)

                GATE_STEPS = 10 + 2 * SUB

                def gates(t):
                    n = [0]

                    def step(ins, signal=None):
                        if signal is not None:
                            ins.then_inc(signal, 1)
                            dve.wait_ge(signal, t + 1)
                        else:
                            n[0] += 1
                            ins.then_inc(dve_step, 1)
                            dve.wait_ge(dve_step, t * GATE_STEPS + n[0])

                    bias = keep["gate_bias"][:, bass.ds(t * SUB, SUB), :]
                    wide = [P, SUB, 8]
                    iota8 = keep["iota8"][:, None, :].to_broadcast(wide)
                    step(dve.tensor_tensor(lg[:, 1], ranks0[:, :, 0:8], bias, ALU.add))
                    for s in range(SUB):
                        dve.sem_inc(dve_passed, 1)
                        step(dve.max(top[:, s, :], lg[:, 1, s, :]))
                        dve.sem_inc(dve_passed, 1)
                        step(dve.max_index(topi[:, s, :], top[:, s, :], lg[:, 1, s, :]))
                    step(dve.tensor_tensor(wt[:, 0, :], top[:, :, 1], top[:, :, 0], ALU.subtract), gap_ready)
                    step(dve.tensor_copy(topf[:], topi[:, :, 0:2]))
                    step(dve.tensor_tensor(lg[:, 0], iota8, topf[:, :, 0:1].to_broadcast(wide), ALU.is_equal))
                    step(dve.tensor_tensor(lg[:, 1], iota8, topf[:, :, 1:2].to_broadcast(wide), ALU.is_equal))
                    dve.wait_ge(exp_ready, t + 1)
                    step(dve.tensor_scalar(wt[:, 2, :], wt[:, 1, :], 1.0, None, ALU.add))
                    step(dve.reciprocal(wt[:, 3, :], wt[:, 2, :]))
                    step(dve.tensor_tensor(wt[:, 4, :], wt[:, 1, :], wt[:, 3, :], ALU.mult))
                    step(dve.tensor_tensor(lg[:, 0], lg[:, 0], wt[:, 3, :, None].to_broadcast(wide), ALU.mult))
                    step(dve.tensor_tensor(lg[:, 1], lg[:, 1], wt[:, 4, :, None].to_broadcast(wide), ALU.mult))
                    step(dve.tensor_tensor(lg[:, 2], lg[:, 0], lg[:, 1], ALU.add))
                    h0 = ranks0[:, :, 8:FW].rearrange("p s (e r) -> p s e r", r=RANK)
                    step(dve.scalar_tensor_tensor(h0, h0, 2.0, lg[:, 2, :, :, None].to_broadcast([P, SUB, 8, RANK]),
                                                  ALU.mult, ALU.mult), gexp_ready)
                    assert n[0] == GATE_STEPS, n[0]

                def parts(product, hi, lo, product_ready, hi_ready, ready, t):
                    product.then_inc(product_ready, 1)
                    dve.wait_ge(product_ready, t + 1)
                    dve.tensor_copy(hi, scratch).then_inc(hi_ready, 1)
                    dve.wait_ge(hi_ready, t + 1)
                    dve.tensor_tensor(lo, scratch, hi, ALU.subtract).then_inc(ready, 1)
                    dve.wait_ge(ready, t + 1)

                def gated(t, par):
                    dve.wait_ge(gates_turned, t + 1)
                    dve.tensor_copy(g_parts[par][0][:], p_gt[:]).then_inc(g_hi_ready, 1)
                    dve.wait_ge(g_hi_ready, t + 1)
                    dve.tensor_tensor(g_parts[par][1][:], p_gt[:], g_parts[par][0][:], ALU.subtract
                                      ).then_inc(g_ready, 1)

                def ranks1(t):
                    dve.wait_ge(ranks_done, t + 2)
                    dve.wait_ge(out_done, t * KB + KB)
                    parts(dve.tensor_tensor(scratch, p_h1[:], keep["own2"][:].rearrange("p b n -> p (b n)"),
                                            ALU.mult), h1_hi[:], h1_lo[:], h1_product, h1_hi_ready, h1_ready, t)

                DRE, UF, CR, CI = range(4)
                K_STEPS = 9
                wide = [P, HT, QN]

                def k_angles(t):
                    co = keep["co"][:, :, bass.ds(t * HT, HT)]
                    dve.wait_ge(k_free, t + 1)
                    for i, which in enumerate((0, 1, 1)):
                        dve.tensor_tensor(turns[:, i], co[:, UF, :, None].to_broadcast(wide),
                                          keep["lq"][:, which, None, :].to_broadcast(wide), ALU.mult
                                          ).then_inc(k_step, 1)
                    for i in range(2):
                        dve.tensor_tensor(decay[:, i], co[:, DRE, :, None].to_broadcast(wide),
                                          keep["lq"][:, i, None, :].to_broadcast(wide), ALU.mult
                                          ).then_inc(k_step, 1)
                    dve.wait_ge(k_step, t * K_STEPS + 5)
                    for i in range(3):
                        dve.tensor_scalar(turns[:, i], turns[:, i], keep["off"][:, i:i + 1], None, ALU.add
                                          ).then_inc(k_step, 1)
                    dve.wait_ge(k_step, t * K_STEPS + 8)
                    dve.tensor_scalar(whole, turns[:], ROUND, ROUND, ALU.add, ALU.subtract).then_inc(k_step, 1)
                    dve.wait_ge(k_step, t * K_STEPS + K_STEPS)
                    dve.tensor_tensor(turns[:], turns[:], whole, ALU.subtract).then_inc(k_phases, 1)

                def k_tables(t):
                    co = keep["co"][:, :, bass.ds(t * HT, HT)]
                    dve.wait_ge(k_waves, 2 * t + 2)
                    for i in range(3):
                        dve.tensor_tensor(turns[:, i], turns[:, i], decay[:, min(i, 1)], ALU.mult
                                          ).then_inc(k_parts, 1)
                    dve.wait_ge(k_parts, t * 5 + 3)
                    for i, part in ((1, CR), (2, CI)):
                        dve.tensor_tensor(turns[:, i], turns[:, i], co[:, part, :, None].to_broadcast(wide),
                                          ALU.mult).then_inc(k_parts, 1)
                    dve.wait_ge(k_parts, t * 5 + 5)
                    dve.tensor_tensor(acoef, turns[:, 1], turns[:, 2], ALU.add).then_inc(k_coefs, 1)

                def k_take(t):
                    dve.wait_ge(k_done, t + 1)
                    dve.tensor_copy(kout, p_gt[0:QN, 0:HT * RN].rearrange(
                        "q (h r) -> q h r", r=RN)).then_inc(k_copied, 1)
                    dve.wait_ge(k_copied, t + 1)
                    dve.tensor_tensor(kout[0:1, :, 0], kout[0:1, :, 0], keep["dskip"][:, bass.ds(t * HT, HT)],
                                      ALU.add).then_inc(k_ready, 1)

                def tile(t, par, ahead=True):
                    ranks1(t)
                    k_angles(t)
                    if ahead:
                        x_lo(t + 1, 1 - par)
                    if ahead:
                        take_tokens(t + 1)
                        gates(t + 1)
                    k_tables(t)
                    if ahead:
                        gated(t + 1, 1 - par)
                    k_take(t)

                dve.sem_inc(tok_taken, 4)
                dve.memset(ranks1_by_token[:], 0.0).then_inc(zeros_ready, 1)
                x_lo(0, 0)
                dve.wait_ge(fixed_hi_ready, 1)
                dve.tensor_tensor(fixed[:, :, 1], fixed_raw, fixed[:, :, 0], ALU.subtract).then_inc(fixed_ready, 1)
                dve.wait_ge(zeros_ready, 1)
                take_tokens(0, first=True)
                gates(0)
                m_lo_parts([KB])
                gated(0, 0)
                with dve.Fori(0, TILES // 2 - 1) as i:
                    tile(2 * i, 0)
                    tile(2 * i + 1, 1)
                tile(TILES - 2, 0)
                tile(TILES - 1, 1, ahead=False)

            @block.tensor
            def _(pe):
                def three(out, w_hi, w_lo, v_hi, v_lo, start=False, stop=False):
                    pe.matmul(out, w_hi, v_hi, start=start, stop=False)
                    pe.matmul(out, w_hi, v_lo, start=False, stop=False)
                    return pe.matmul(out, w_lo, v_hi, start=False, stop=stop)

                def first_products(t, par):
                    x_hi, x_lo = x_parts[par]
                    pe.wait_ge(x_ready, t * XC + XC)
                    for s in range(SUB):
                        tokens = slice(s * P, (s + 1) * P)
                        both_parts = by_token[:, s * 2 // SUB].rearrange("p k h c -> p k (h c)")
                        if s % 2 == 0:
                            pe.wait_ge(pa_ready, t * 4 + (s + 4))
                        pe.wait_ge(tok_taken, t * (2 * SUB) + 2 * s + 2)
                        for k in range(KB):
                            def with_hi():
                                return pe.matmul(p_tok[s % 2][:, 0:2 * TW], x_hi[:, k, tokens], both_parts[:, k, :],
                                                 start=(k == 0), stop=(k == KB - 1))

                            if k < KB - 1:
                                with_hi()
                            pe.matmul(p_tok[s % 2][:, 0:TW], x_lo[:, k, tokens], both_parts[:, k, 0:TW],
                                      start=False, stop=False)
                        with_hi().then_inc(tok_done, 1)

                def turn_ranks(t):
                    pe.wait_ge(tok_taken, t * (2 * SUB) + (2 * SUB + 4))
                    for s in range(SUB):
                        pe.matmul(p_h1[:, s * P:(s + 1) * P], ranks1_by_token[:, s, :], keep["ident"][:],
                                  start=(s == 0), stop=False)

                def kernel_rows(t):
                    pe.wait_ge(k_coefs, t + 1)
                    pe.sem_inc(pe_passed, 1)
                    for h in range(HT):
                        last = pe.matmul(p_gt[0:QN, h * RN:(h + 1) * RN], acoef[:, h, :], turns[:, 0, h, :],
                                         start=True, stop=True)
                    last.then_inc(k_done, 1)

                def turn_gates(t):
                    pe.wait_ge(gexp_ready, t + 1)
                    for s in range(SUB):
                        last = pe.transpose(p_gt[:, s * P:(s + 1) * P], ranks0[:, s, 8:FW], keep["ident"][:])
                    last.then_inc(gates_turned, 1)

                def last_ranks(t, par):
                    pe.wait_ge(g_ready, t + 1)
                    three(p_h1[:], ba_hi[:], ba_lo[:], g_parts[par][0][:], g_parts[par][1][:],
                          stop=True).then_inc(ranks_done, 1)

                def tile(t, par, ahead=True):
                    x_hi, x_lo = x_parts[par]
                    for o in range(KB):
                        if ahead and o == 3:
                            first_products(t + 1, 1 - par)
                        if ahead and o == 4:
                            turn_ranks(t + 1)
                        if ahead and o == 5:
                            turn_gates(t + 1)
                        if ahead and o == 7:
                            last_ranks(t + 1, 1 - par)
                        if o == 7:
                            kernel_rows(t)
                        cols = slice(o * P, (o + 1) * P)
                        out = p_out[o % 4][:]
                        pe.wait_ge(out_copied, t * KB + o + 1)
                        for k in range(KB):
                            three(out, m_hi[:, k, cols], m_lo[:, k, cols], x_hi[:, k, :], x_lo[:, k, :],
                                  start=(k == 0))
                        three(out, m_hi[:, KB, cols], m_lo[:, KB, cols], g_parts[par][0][:], g_parts[par][1][:])
                        if o == 0:
                            pe.wait_ge(h1_ready, t + 1)
                            pe.wait_ge(b_ready, t + 2)
                        three(out, b_hi[:, cols], b_lo[:, cols], h1_hi[:], h1_lo[:], stop=True
                              ).then_inc(out_done, 1)

                pe.sem_inc(out_done, KB)
                pe.sem_inc(ranks_done, 1)
                pe.wait_ge(fixed_ready, 1)
                first_products(0, 0)
                turn_ranks(0)
                turn_gates(0)
                last_ranks(0, 0)
                pe.wait_ge(m_ready, KB + 1)
                with pe.Fori(0, TILES // 2 - 1) as i:
                    tile(2 * i, 0)
                    tile(2 * i + 1, 1)
                tile(TILES - 2, 0)
                tile(TILES - 1, 1, ahead=False)


def layer2_phase(nc, keep, across, io):
    ctx, sb, ps, sem = scope(nc)
    with ctx:
        w_lo = sb("w2_lo", [P, 2, KB, D], F32R)
        w_hi = sb("w2_hi", [P, 2, KB, D], F32R)
        w_raw = sb("w2_raw", [P, 4, D])
        x_raw = sb("x2_raw", [P, 2, 2, KB, STEPS])
        x_parts = [both(nc, f"x2_{i}", [P, KB, P], ctx) for i in range(2)]
        x3_out = sb("x3_out", [P, 2, D])
        p_out = [ps(f"p_x3_{i}", [P, 2 * HALF]) for i in range(4)]

        first_loaded = across["w2_loaded"]
        first_diag = sem("first_diag")
        first_hi = sem("first_hi")
        w_loaded = [sem(f"w2_loaded{i}") for i in range(4)]
        w_diag = sem("w2_diag")
        w_hi_ready = sem("w2_hi_ready")
        w_chunk = sem("w2_chunk")
        x_loaded = [sem(f"x2_loaded{i}") for i in range(2)]
        x_hi_ready = sem("x2_hi_ready")
        x_ready = sem("x2_ready")
        pool_passed = sem("pool_passed2")
        slot_done = sem("slot_done")
        left_copied = sem("left_copied")
        right_copied = sem("right_copied")
        stored = [sem(f"x3_stored{i}") for i in range(2)]
        tbl = keep["tbl"]
        first_raw = [across["w2_raw"][:, k, :] for k in range(KB)]

        def slots_taken(engine):
            return engine.value_load(tbl[0:1, T_SLOTS:T_SLOTS + 1], min_val=FULL, max_val=SLOTS)

        with nc.Block() as block:

            @block.sync
            def _(sp):
                def load(s, par):
                    a, b = [sp.value_load(tbl[0:1, bass.ds(s * 2 + (T_READ + n), 1)], min_val=0,
                                          max_val=BATCHES - 1) for n in range(2)]
                    sp.wait_ge(x_ready, s + 1)
                    for n, batch in enumerate((a, b)):
                        sp.dma_start(x_raw[:, par, n].rearrange("p k n -> p (k n)"),
                                     io["x2"][bass.ds(batch, 1)].rearrange("a p k n -> p (a k n)")
                                     ).then_inc(x_loaded[par], 16)

                with sp.Fori(0, FULL // 2 + 1) as i:
                    load(2 * i, 0)
                    load(2 * i + 1, 1)
                taken = slots_taken(sp)
                for s in range(FULL + 2, SLOTS):
                    with sp.If(taken > s):
                        load(s, s % 2)

            @block.gpsimd
            def _(pool):
                def expert(u, par):
                    e = pool.value_load(tbl[0:1, bass.ds(u + T_EXPERT, 1)], min_val=0, max_val=EXPERTS2 - 1)
                    free = pool.value_load(tbl[0:1, bass.ds(u + T_FREE, 1)], min_val=1, max_val=SLOTS + 1)

                    def load(k):
                        pool.wait_ge(w_chunk, u * KB + k + 1)
                        pool.dma_start(w_raw[:, k % 4, :],
                                       io["w2t"][bass.ds(e, 1), k].rearrange("a p c -> p (a c)")
                                       ).then_inc(w_loaded[k % 4], 16)

                    for k in range(4):
                        load(k)
                    pool.wait_ge(slot_done, free)
                    for k in range(KB):
                        pool.wait_ge(w_loaded[k % 4], u * 32 + (k // 4 - 1) * 16)
                        raw = w_raw[:, k % 4, :]
                        diag = w_raw[:, k % 4, k * P:(k + 1) * P]
                        pool.tensor_tensor(diag, diag, keep["anti"][:], ALU.add).then_inc(w_diag, 1)
                        pool.wait_ge(w_diag, u * KB + (k + 1 - KB))
                        pool.sem_inc(pool_passed, 1)
                        pool.tensor_scalar(w_hi[:, par, k, :], raw, 1.0, 0.0, ALU.mult, ALU.add
                                           ).then_inc(w_hi_ready, 1)
                        pool.wait_ge(w_hi_ready, u * KB + (k + 1 - KB))
                        pool.tensor_tensor(w_lo[:, par, k, :], raw, w_hi[:, par, k, :], ALU.subtract
                                           ).then_inc(w_chunk, 1)
                        if k + 4 < KB:
                            load(k + 4)

                pool.sem_inc(w_chunk, 4)
                count = pool.value_load(tbl[0:1, T_COUNT:T_COUNT + 1], min_val=1, max_val=EXPERTS2)
                for k in range(KB):
                    pool.wait_ge(first_loaded[k], 16)
                    diag = first_raw[k][:, k * P:(k + 1) * P]
                    pool.tensor_tensor(diag, diag, keep["anti"][:], ALU.add).then_inc(first_diag, 1)
                with pool.If(count > 1):
                    expert(1, 1)
                with pool.Fori(1, EXPERTS2 // 2) as i:
                    for par in range(2):
                        with pool.If(count > 2 * i + par):
                            expert(2 * i + par, par)

            @block.scalar
            def _(act):
                def x_hi(s, par, n):
                    act.wait_ge(x_loaded[par], n * 32)
                    act.wait_ge(slot_done, s)
                    act.copy(x_parts[par][0][:].rearrange("p k (b n) -> p b k n", b=2), x_raw[:, par]
                             ).then_inc(x_hi_ready, 1)

                def take(s, par, n):
                    a, b = [act.value_load(tbl[0:1, bass.ds(s * 2 + (T_WRITE + m), 1)], min_val=0,
                                           max_val=PLACES - 1) for m in range(2)]
                    act.wait_ge(slot_done, s + 2)
                    act.wait_ge(stored[par], n * 32)
                    act.copy(x3_out[:, par, 0:HALF], p_out[par][:, 0:HALF]).then_inc(left_copied, 1)
                    act.wait_ge(left_copied, s + 5)
                    act.wait_ge(right_copied, s + 5)
                    for m, batch in enumerate((a, b)):
                        act.dma_start(io["x3"][bass.ds(batch, 1)].rearrange("a t c -> (a t) c"),
                                      x3_out[m * STEPS:(m + 1) * STEPS, par, :]).then_inc(stored[par], 16)

                act.sem_inc(left_copied, 4)
                for n in range(2):
                    act.sem_inc(stored[n], 32)
                for k in range(KB):
                    if k == KB // 2:
                        act.wait_ge(x_loaded[0], 32)
                        act.copy(x_parts[0][0][:].rearrange("p k (b n) -> p b k n", b=2), x_raw[:, 0]
                                 ).then_inc(x_hi_ready, 1)
                    act.wait_ge(first_diag, k + 1)
                    act.copy(w_hi[:, 0, k, :], first_raw[k]).then_inc(first_hi, 1)
                with act.Fori(0, FULL // 2) as i:
                    x_hi(2 * i + 1, 1, i + 1)
                    take(2 * i, 0, i + 1)
                    x_hi(2 * i + 2, 0, i + 2)
                    take(2 * i + 1, 1, i + 1)
                x_hi(FULL + 1, 1, FULL // 2 + 1)
                for n in range(2):
                    act.wait_ge(stored[n], 32 * (FULL // 2 + 1))
                taken = slots_taken(act)
                for s in range(FULL, SLOTS):
                    with act.If(taken > s):
                        if s >= FULL + 2:
                            x_hi(s, s % 2, s // 2 + 1)
                        take(s, s % 2, s // 2 + 1)
                        act.wait_ge(stored[s % 2], 32 * (s // 2 + 2))

            @block.vector
            def _(dve):
                def x_lo(s, par):
                    dve.wait_ge(x_hi_ready, s + 1)
                    hi, lo = [part[:].rearrange("p k (b n) -> p b k n", b=2) for part in x_parts[par]]
                    dve.tensor_tensor(lo, x_raw[:, par], hi, ALU.subtract).then_inc(x_ready, 1)

                def take(s, par, n):
                    dve.wait_ge(slot_done, s + 2)
                    dve.wait_ge(stored[par], n * 32)
                    dve.tensor_copy(x3_out[:, par, HALF:D], p_out[par][:, HALF:D]).then_inc(right_copied, 1)

                dve.sem_inc(x_ready, 2)
                dve.sem_inc(right_copied, 4)
                for k in range(KB):
                    if k == KB // 2:
                        x_lo(0, 0)
                    dve.wait_ge(first_hi, k + 1)
                    dve.tensor_tensor(w_lo[:, 0, k, :], first_raw[k], w_hi[:, 0, k, :], ALU.subtract
                                      ).then_inc(w_chunk, 1)
                with dve.Fori(0, FULL // 2) as i:
                    x_lo(2 * i + 1, 1)
                    take(2 * i, 0, i + 1)
                    x_lo(2 * i + 2, 0)
                    take(2 * i + 1, 1, i + 1)
                x_lo(FULL + 1, 1)
                taken = slots_taken(dve)
                for s in range(FULL, SLOTS):
                    with dve.If(taken > s):
                        if s >= FULL + 2:
                            x_lo(s, s % 2)
                        take(s, s % 2, s // 2 + 1)

            @block.tensor
            def _(pe):
                def slot(s, par):
                    wpar = pe.value_load(tbl[0:1, bass.ds(s + T_PAR, 1)], min_val=0, max_val=1)
                    rank = pe.value_load(tbl[0:1, bass.ds(s + T_RANK, 1)], min_val=0, max_val=EXPERTS2 - 1)
                    pe.wait_ge(left_copied, s + 3)
                    pe.wait_ge(right_copied, s + 3)
                    pe.wait_ge(x_ready, s + 3)
                    x_hi, x_lo = x_parts[par]
                    for n in range(2):
                        out = p_out[par][:, n * HALF:(n + 1) * HALF]
                        cols = slice(n * HALF, (n + 1) * HALF)
                        for k in range(KB):
                            if n == 0:
                                pe.wait_ge(w_chunk, rank * KB + (k + 5))
                            hi = w_hi[:, bass.ds(wpar, 1), k, cols].rearrange("p a c -> p (a c)")
                            lo = w_lo[:, bass.ds(wpar, 1), k, cols].rearrange("p a c -> p (a c)")
                            pe.matmul(out, x_hi[:, k, :], hi, start=(k == 0), stop=False)
                            pe.matmul(out, x_hi[:, k, :], lo, start=False, stop=False)
                            last = pe.matmul(out, x_lo[:, k, :], hi, start=False, stop=(k == KB - 1))
                    last.then_inc(slot_done, 1)

                pe.sem_inc(slot_done, 1)
                with pe.Fori(0, FULL // 2) as i:
                    slot(2 * i, 0)
                    slot(2 * i + 1, 1)
                taken = slots_taken(pe)
                for s in range(FULL, SLOTS):
                    with pe.If(taken > s):
                        slot(s, s % 2)


def layer3_phase(nc, keep, io):
    ctx, sb, ps, sem = scope(nc)
    with ctx:
        t_raw = sb("t_raw", [P, 2, D])
        t_parts = [both(nc, f"t{i}", [P, D], ctx) for i in range(2)]
        x_raw = sb("x3_raw", [P, 4, D])
        u_parts = [both(nc, f"u{i}", [P, KB, P], ctx) for i in range(2)]
        masked = sb("masked", [P, 2, D])
        out_sb = sb("out_sb", [P, 2, D])
        iota_l = sb("iota_l", [P, D])
        mask = sb("mask", [P, D])
        p_u = [ps(f"p_u{i}", [P, KB * P]) for i in range(2)]
        p_y = [ps(f"p_y{i}", [P, D]) for i in range(2)]

        t_loaded = [sem(f"t_loaded{i}") for i in range(2)]
        x_loaded = [sem(f"x3_loaded{i}") for i in range(4)]
        t_hi_ready = sem("t_hi_ready")
        t_ready = sem("t_ready")
        turned = sem("turned")
        u_hi_ready = sem("u_hi_ready")
        u_ready = sem("u_ready")
        pool_passed = sem("pool_passed3")
        y_done = sem("y_done")
        masked_ready = sem("masked_ready")
        out_ready = sem("out_ready")
        stored = [sem(f"out_stored{i}") for i in range(2)]
        iota_ready = sem("iota_ready")
        mask_ready = sem("mask_ready")

        with nc.Block() as block:

            @block.sync
            def _(sp):
                def load(h, t_slot, x_slot):
                    sp.wait_ge(out_ready, h + 1)
                    sp.dma_start(x_raw[:, x_slot, :],
                                 io["x3"][0:BATCHES, bass.ds(h, 1), :].rearrange("b a c -> b (a c)")
                                 ).then_inc(x_loaded[x_slot], 16)
                    sp.wait_ge(t_ready, h + 1)
                    sp.dma_start(t_raw[:, t_slot, :],
                                 io["toeplitz"][bass.ds(h, 1)].rearrange("a p c -> p (a c)")
                                 ).then_inc(t_loaded[t_slot], 16)

                with sp.Fori(0, STEPS // 4) as i:
                    for n in range(4):
                        load(4 * i + n, n % 2, n)

            @block.gpsimd
            def _(pool):
                pool.iota(iota_l[:], [[1, D]], base=0, channel_multiplier=0,
                          allow_small_or_imprecise_dtypes=True).then_inc(iota_ready, 1)
                pool.sem_inc(t_ready, 2)

                def split(h, par, n):
                    pool.wait_ge(t_loaded[par], 16 * n)
                    pool.wait_ge(y_done, h + 1)
                    pool.sem_inc(pool_passed, 1)
                    pool.tensor_scalar(t_parts[par][0][:], t_raw[:, par, :], 1.0, 0.0, ALU.mult, ALU.add).then_inc(t_hi_ready, 1)
                    pool.wait_ge(t_hi_ready, h + 1)
                    pool.tensor_tensor(t_parts[par][1][:], t_raw[:, par, :], t_parts[par][0][:], ALU.subtract
                                       ).then_inc(t_ready, 1)

                with pool.Fori(0, STEPS // 2) as i:
                    split(2 * i, 0, i + 1)
                    split(2 * i + 1, 1, i + 1)

            @block.scalar
            def _(act):
                def u_hi(h, par):
                    act.wait_ge(turned, h + 1)
                    act.wait_ge(y_done, h + 1)
                    act.copy(u_parts[par][0][:].rearrange("p k b -> p (k b)"), p_u[par][:]
                             ).then_inc(u_hi_ready, 1)

                def store(h, par):
                    act.wait_ge(out_ready, h + 5)
                    act.dma_start(io["out"][:, bass.ds(h, 1), :].rearrange("b a c -> b (a c)"),
                                  out_sb[:, par, :]).then_inc(stored[par], 16)

                for n in range(2):
                    act.sem_inc(stored[n], 16)
                u_hi(0, 0)
                with act.Fori(0, STEPS // 2 - 1) as i:
                    u_hi(2 * i + 1, 1)
                    store(2 * i, 0)
                    u_hi(2 * i + 2, 0)
                    store(2 * i + 1, 1)
                u_hi(STEPS - 1, 1)
                store(STEPS - 2, 0)
                store(STEPS - 1, 1)
                for n in range(2):
                    act.wait_ge(stored[n], 16 * (STEPS // 2 + 1))

            @block.vector
            def _(dve):
                def u_lo(h, par):
                    dve.wait_ge(u_hi_ready, h + 1)
                    dve.tensor_tensor(u_parts[par][1][:].rearrange("p k b -> p (k b)"), p_u[par][:],
                                      u_parts[par][0][:].rearrange("p k b -> p (k b)"), ALU.subtract
                                      ).then_inc(u_ready, 1)

                def finish(h, par, x_slot, n):
                    dve.wait_ge(y_done, h + 3)
                    dve.tensor_tensor(masked[:, par, :], p_y[par][:], mask[:], ALU.mult).then_inc(masked_ready, 1)
                    dve.wait_ge(masked_ready, h + 3)
                    dve.wait_ge(stored[par], 16 * n)
                    x3 = x_raw[:, x_slot, :].rearrange("p (k c) -> p k c", c=P)[:, :, ::-1]
                    dve.tensor_tensor(out_sb[:, par, :].rearrange("p (k c) -> p k c", c=P),
                                      masked[:, par, :].rearrange("p (k c) -> p k c", c=P), x3, ALU.add
                                      ).then_inc(out_ready, 1)

                dve.sem_inc(u_ready, 2)
                dve.sem_inc(masked_ready, 2)
                dve.sem_inc(out_ready, 4)
                dve.wait_ge(iota_ready, 1)
                dve.tensor_scalar(mask[:], iota_l[:], keep["length"][:, 0:1], None, ALU.is_lt
                                  ).then_inc(mask_ready, 1)
                dve.wait_ge(mask_ready, 1)
                u_lo(0, 0)
                with dve.Fori(0, STEPS // 4 - 1) as i:
                    for n in range(4):
                        u_lo(4 * i + n + 1, 1 - n % 2)
                        finish(4 * i + n, n % 2, n, 2 * i + n // 2 + 1)
                for n in range(4):
                    h = STEPS - 4 + n
                    if n < 3:
                        u_lo(h + 1, 1 - n % 2)
                    finish(h, n % 2, n, STEPS // 2 - 2 + n // 2 + 1)

            @block.tensor
            def _(pe):
                def turn(h, par, x_slot, n):
                    pe.wait_ge(x_loaded[x_slot], 16 * n)
                    pe.wait_ge(u_ready, h + 1)
                    for k in range(KB):
                        last = pe.transpose(p_u[par][:, k * P:(k + 1) * P], x_raw[:, x_slot, k * P:(k + 1) * P],
                                            keep["ident"][:])
                    last.then_inc(turned, 1)

                def convolve(h, par):
                    pe.wait_ge(u_ready, h + 3)
                    pe.wait_ge(t_ready, h + 3)
                    pe.wait_ge(masked_ready, h + 1)
                    u_hi, u_lo = u_parts[par]
                    t_hi, t_lo = t_parts[par]
                    for k in range(KB):
                        for w, t in ((u_hi, t_hi), (u_hi, t_lo), (u_lo, t_hi)):
                            for bank in range(k * P // HALF, D // HALF):
                                lo, hi = max(k * P, bank * HALF), (bank + 1) * HALF
                                first = k == 0 and w is u_hi and t is t_hi
                                done = (k + 1) * P == hi if k >= KB // 2 else (bank == 0 and k == KB // 2 - 1)
                                last = pe.matmul(p_y[par][:, lo:hi], w[:, k, :], t[:, lo - k * P:hi - k * P],
                                                 start=first, stop=done and w is u_lo)
                    last.then_inc(y_done, 1)

                pe.sem_inc(y_done, 2)
                turn(0, 0, 0, 1)
                with pe.Fori(0, STEPS // 4 - 1) as i:
                    for n in range(4):
                        turn(4 * i + n + 1, 1 - n % 2, (n + 1) % 4, i + 1 + (n + 1) // 4)
                        convolve(4 * i + n, n % 2)
                for n in range(4):
                    h = STEPS - 4 + n
                    if n < 3:
                        turn(h + 1, 1 - n % 2, n + 1, STEPS // 4)
                    convolve(h, n % 2)


def bass_cond_resid(nc, io, phases=5):
    ctx = ExitStack()
    with ctx:
        def sb(name, shape, dt=F32):
            return ctx.enter_context(nc.sbuf_tensor(name, shape, dt))

        keep = {
            "ident": sb("ident", [P, P]),
            "anti": sb("anti", [P, P]),
            "iota8": sb("iota8", [P, 8]),
            "own2": sb("own2", [P, TB, STEPS], BF16),
            "gate_bias": sb("gate_bias", [P, STEPS, 8], BF16),
            "b1": sb("b1", [P, KB]),
            "length": sb("length", [P, 1]),
            "zero": sb("zero", [P, 1]),
            "adapter": sb("adapter", [1, BATCHES], I32),
            "tbl": sb("tbl", [1, T_WIDTH], I32),
            "co": sb("co", [P, 4, STEPS]),
            "lq": sb("lq", [P, 2, QN]),
            "off": sb("off", [P, 3]),
            "dskip": sb("dskip", [1, STEPS]),
        }
        across = {
            "a_stored": ctx.enter_context(nc.semaphore("a_stored")),
            "m_stored": [ctx.enter_context(nc.semaphore(f"m_stored{i}")) for i in range(2)],
            "x_loaded": [ctx.enter_context(nc.semaphore(f"x_loaded{i}")) for i in range(XC)],
            "w2_loaded": [ctx.enter_context(nc.semaphore(f"first_w2_loaded{k}")) for k in range(KB)],
            "w2_raw": nc.alloc_sbuf_tensor_at("first_w2_raw", [P, KB, D], F32, offset=nc.sbuf_base),
        }
        with nc.sbuf_tensor("x0_lo", [P, KB, TOK], F32R) as x0_lo:
            across["x0_lo"] = x0_lo
            across["x0_raw"] = raw_under(nc, "x0_raw", [P, KB, TOK])
            products_phase(nc, keep, across, io)
            if phases > 2:
                layers01_phase(nc, keep, across, io)
        if phases > 3:
            layer2_phase(nc, keep, across, io)
        if phases > 4:
            layer3_phase(nc, keep, io)


def kernel(**inputs):
    import numpy as np
    import concourse.bacc as bacc
    from concourse.bass_utils import run_bass_kernel_spmd

    a = {name: np.asarray(value) for name, value in inputs.items()}
    arrays = {
        "xt": a["x"].reshape(TILES, TOK, KB, P).transpose(0, 3, 2, 1),
        "lang": a["itok_B_0_7"].reshape(1, BATCHES),
        "adapter": a["itok_B_0_23"].reshape(1, BATCHES),
        "expert": a["itok_B_3_7"].reshape(BATCHES, 1),
        "length": a["itok_B_78_3631"].reshape(BATCHES, 1),
        "s0": np.concatenate([
            a["L0_cond_W"].reshape(KB, P, KB, P).transpose(2, 1, 0, 3),
            a["L0_cond_B"].transpose(1, 0, 2).reshape(1, KB, P, ER).transpose(0, 2, 1, 3)]),
        "fixed": np.concatenate([
            a["L0_cond_Wr"].reshape(EXPERTS0, KB, P).transpose(2, 1, 0),
            a["L0_cond_A"].reshape(ER, KB, P).transpose(2, 1, 0)], axis=2),
        "w1t": a["L1_cond_W"].T.reshape(KB, P, D),
        "b1": a["L1_cond_b"].reshape(KB, P).T,
        "a1": a["L1_cond_lora_As"].transpose(1, 0, 2).reshape(KB, P, ADAPTERS * RANK),
        "b1r": a["L1_cond_lora_Bs"],
        "w2t": a["L2_cond_weight"].transpose(0, 2, 1).reshape(EXPERTS2, KB, P, KB, P)[..., ::-1]
        .reshape(EXPERTS2, KB, P, D),
        "log_dt": a["L3_cond_log_dt"].reshape(1, STEPS),
        "c": a["L3_cond_C"].transpose(2, 1, 0),
        "log_a": a["L3_cond_log_A_real"].T,
        "a_imag": a["L3_cond_A_imag"].T,
        "d": a["L3_cond_D"].reshape(1, STEPS),
    }
    arrays = {name: np.ascontiguousarray(value) for name, value in arrays.items()}
    nc = bacc.Bacc("TRN2", target_bir_lowering=False, num_devices=1)
    io = {name: nc.dram_tensor(name + "_dram", value.shape, mybir.dt.from_np(value.dtype), kind="ExternalInput").ap()
          for name, value in arrays.items()}
    io["out"] = nc.dram_tensor("out_dram", (BATCHES, STEPS, D), F32, kind="ExternalOutput").ap()
    for name, shape in (("m01", (KB + 1, P, D)), ("pa", (ADAPTERS, P, AW)), ("x2", (BATCHES, P, KB, STEPS)),
                        ("x3", (PLACES, STEPS, D)), ("kpad", (STEPS, KROW))):
        io[name] = nc.dram_tensor(name + "_dram", shape, F32, kind="Internal").ap()
    k = io["kpad"]
    io["toeplitz"] = bass.AP(tensor=k.tensor, offset=0, ap=[[KROW, STEPS], [1, P], [1, D]])
    bass_cond_resid(nc, io)
    r = run_bass_kernel_spmd(nc, [{name + "_dram": value for name, value in arrays.items()}], core_ids=[0])
    return r.results[0]["out_dram"]
```
